# Optimizing a Trainium2 kernel written in Bass

```python
import numpy as np
import jax
import jax.numpy as jnp

def _softmax(x, axis=-1):
    return jax.nn.softmax(x, axis=axis)

def _gelu(x):
    return jax.nn.gelu(x, approximate=True)

def _silu(x):
    return jax.nn.silu(x)

def _sigmoid(x):
    return jax.nn.sigmoid(x)

def _layernorm(x, axis=-1, eps=1e-05):
    m = jnp.mean(x, axis=axis, keepdims=True)
    v = jnp.var(x, axis=axis, keepdims=True)
    return (x - m) / jnp.sqrt(v + eps)

def _scatter_add(tgt, idx, src, axis=0):
    return tgt.at[idx].add(src)

def _segment_sum(src, seg, n):
    return jax.ops.segment_sum(src, seg, n)
kernel_name = 'mk_sandwich_d1_jaxref_r2_1db5d2'

def setup_inputs(seed: int=0):
    np.random.seed(seed)
    _w = jnp.asarray

    def _L0_attn_setup():
        import math
        import jax, jax.numpy as jnp
        import numpy as np
        HID = 1024
        H = 16
        HKV = 8
        D = HID // H
        F = D
        SEQ = 1024
        BATCH = 2
        THETA = 10000.0

        def _rotate_half(x):
            x1, x2 = (x[..., :x.shape[-1] // 2], x[..., x.shape[-1] // 2:])
            return jnp.concatenate((-x2, x1), axis=-1)

        def _softmax_kernel(x, R):
            n = jnp.sqrt(jnp.sum(x * x, axis=-1, keepdims=True))
            x = x / jnp.maximum(n, 1e-06)
            p = jnp.einsum('...d,ed->...e', x, R)
            feats = jnp.concatenate([jnp.sin(p), jnp.cos(p)], axis=-1)
            return feats / math.sqrt(F)
        key = jax.random.key(seed)
        ks = jax.random.split(key, 10)
        s = lambda k, shape, scale=0.02: jax.random.normal(k, shape, dtype=jnp.float32) * scale
        return {'hidden_states': jax.random.normal(ks[0], (BATCH, SEQ, HID), dtype=jnp.float32), 'Wq': s(ks[1], (HID, HID)), 'bq': s(ks[2], (HID,)), 'Wk': s(ks[3], (HKV * D, HID)), 'bk': s(ks[4], (HKV * D,)), 'Wv': s(ks[5], (HKV * D, HID)), 'bv': s(ks[6], (HKV * D,)), 'Wo': s(ks[7], (HID, HID)), 'bo': s(ks[8], (HID,)), 'rand_matrix': jax.random.normal(ks[9], (F // 2, D), dtype=jnp.float32)}
    _L0_attn_in = _L0_attn_setup()

    def _L0_ffn_setup():
        import jax, jax.numpy as jnp
        import numpy as np
        B, L, D = (4, 2048, 1024)
        DF = 4 * D
        CAPACITY_RATIO = 0.5
        key = jax.random.key(seed)
        ks = jax.random.split(key, 4)
        s = 0.02
        return {'x': jax.random.normal(ks[0], (B, L, D), dtype=jnp.float32), 'w_r': jax.random.normal(ks[1], (D,), dtype=jnp.float32) * s, 'b_r': jnp.zeros((), dtype=jnp.float32), 'w1': jax.random.normal(ks[2], (D, DF), dtype=jnp.float32) * s, 'b1': jnp.zeros((DF,), dtype=jnp.float32), 'w2': jax.random.normal(ks[3], (DF, D), dtype=jnp.float32) * s, 'b2': jnp.zeros((D,), dtype=jnp.float32)}
    _L0_ffn_in = _L0_ffn_setup()
    _d = {'L0_attn_hidden_states': _L0_attn_in['hidden_states'], 'L0_attn_Wq': _L0_attn_in['Wq'], 'L0_attn_bq': _L0_attn_in['bq'], 'L0_attn_Wk': _L0_attn_in['Wk'], 'L0_attn_bk': _L0_attn_in['bk'], 'L0_attn_Wv': _L0_attn_in['Wv'], 'L0_attn_bv': _L0_attn_in['bv'], 'L0_attn_Wo': _L0_attn_in['Wo'], 'L0_attn_bo': _L0_attn_in['bo'], 'L0_attn_rand_matrix': _L0_attn_in['rand_matrix'], 'L0_ffn_w_r': _L0_ffn_in['w_r'], 'L0_ffn_b_r': _L0_ffn_in['b_r'], 'L0_ffn_w1': _L0_ffn_in['w1'], 'L0_ffn_b1': _L0_ffn_in['b1'], 'L0_ffn_w2': _L0_ffn_in['w2'], 'L0_ffn_b2': _L0_ffn_in['b2']}
    _x0 = _d['L0_attn_hidden_states']
    _d['L0_attn_hidden_states'] = jax.random.normal(jax.random.fold_in(jax.random.key(seed), 1), (1, 4096, 1024), dtype=_x0.dtype)
    del _x0
    return _d

def reference(L0_attn_hidden_states, L0_attn_Wq, L0_attn_bq, L0_attn_Wk, L0_attn_bk, L0_attn_Wv, L0_attn_bv, L0_attn_Wo, L0_attn_bo, L0_attn_rand_matrix, L0_ffn_w_r, L0_ffn_b_r, L0_ffn_w1, L0_ffn_b1, L0_ffn_w2, L0_ffn_b2):

    def _L0_attn_ref(hidden_states, Wq, bq, Wk, bk, Wv, bv, Wo, bo, rand_matrix):
        import math
        import jax, jax.numpy as jnp
        import numpy as np
        HID = 1024
        H = 16
        HKV = 8
        D = HID // H
        F = D
        SEQ = 1024
        BATCH = 2
        THETA = 10000.0

        def _rotate_half(x):
            x1, x2 = (x[..., :x.shape[-1] // 2], x[..., x.shape[-1] // 2:])
            return jnp.concatenate((-x2, x1), axis=-1)

        def _softmax_kernel(x, R):
            n = jnp.sqrt(jnp.sum(x * x, axis=-1, keepdims=True))
            x = x / jnp.maximum(n, 1e-06)
            p = jnp.einsum('...d,ed->...e', x, R)
            feats = jnp.concatenate([jnp.sin(p), jnp.cos(p)], axis=-1)
            return feats / math.sqrt(F)
        b, s, _ = hidden_states.shape
        q = (hidden_states @ Wq.T + bq).reshape(b, s, H, D).transpose(0, 2, 1, 3)
        k = (hidden_states @ Wk.T + bk).reshape(b, s, HKV, D).transpose(0, 2, 1, 3)
        v = (hidden_states @ Wv.T + bv).reshape(b, s, HKV, D).transpose(0, 2, 1, 3)
        inv_freq = 1.0 / THETA ** (jnp.arange(0, D, 2, dtype=jnp.float32) / D)
        freqs = jnp.arange(s, dtype=jnp.float32)[:, None] * inv_freq[None, :]
        emb = jnp.concatenate((freqs, freqs), axis=-1)
        cos = jnp.cos(emb)[None, None, :, :]
        sin = jnp.sin(emb)[None, None, :, :]
        q = q * cos + _rotate_half(q) * sin
        k = k * cos + _rotate_half(k) * sin
        rep = H // HKV
        k = jnp.repeat(k, rep, axis=1)
        v = jnp.repeat(v, rep, axis=1)
        qp = _softmax_kernel(q, rand_matrix)
        kp = _softmax_kernel(k, rand_matrix)
        kv = jnp.einsum('bhsf,bhsd->bsfd', kp, v)
        out = jnp.einsum('bhsf,bsfd->bhsd', qp, kv)
        out = out.reshape(b, s, HID)
        return out @ Wo.T + bo

    def _L0_ffn_ref(x, w_r, b_r, w1, b1, w2, b2):
        import jax, jax.numpy as jnp
        import numpy as np
        B, L, D = (4, 2048, 1024)
        DF = 4 * D
        CAPACITY_RATIO = 0.5
        b, l, d = x.shape
        k = int(l * CAPACITY_RATIO)
        scores = jnp.einsum('bld,d->bl', x, w_r) + b_r
        _, idx = jax.lax.top_k(scores, k)
        x_sel = jnp.take_along_axis(x, idx[:, :, None], axis=1)
        h = jax.nn.gelu(jnp.einsum('bkd,df->bkf', x_sel, w1) + b1)
        out_sel = jnp.einsum('bkf,fd->bkd', h, w2) + b2
        batch_ix = jnp.arange(b)[:, None]
        out = jnp.zeros_like(x).at[batch_ix, idx].set(out_sel)
        return out
    x = L0_attn_hidden_states
    x = x + _layernorm(_L0_attn_ref(_layernorm(x, axis=-1), L0_attn_Wq, L0_attn_bq, L0_attn_Wk, L0_attn_bk, L0_attn_Wv, L0_attn_bv, L0_attn_Wo, L0_attn_bo, L0_attn_rand_matrix), axis=-1)
    x = x + _layernorm(_L0_ffn_ref(_layernorm(x, axis=-1), L0_ffn_w_r, L0_ffn_b_r, L0_ffn_w1, L0_ffn_b1, L0_ffn_w2, L0_ffn_b2), axis=-1)
    return x

_drawn_inputs = setup_inputs


def setup_inputs(seed=0):
    import zlib

    import numpy as np

    out = dict(_drawn_inputs(seed))
    spreads = {'L0_ffn_b1': (0.0, 0.1), 'L0_ffn_b2': (0.0, 0.1)}
    factors = {}
    for name, (base, spread) in spreads.items():
        noise = np.random.default_rng([zlib.crc32(name.encode()), seed]).standard_normal(out[name].shape)
        drawn = base * np.exp(spread * noise) if base else spread * noise
        out[name] = jnp.asarray(drawn.astype(out[name].dtype))
    for name, factor in factors.items():
        out[name] = (out[name] * factor).astype(out[name].dtype)
    return out
```

```python
from contextlib import ExitStack

import concourse.bass as bass
from concourse import mybir

P = 128
F32 = mybir.dt.float32
F32R = mybir.dt.float32r
I32 = mybir.dt.int32
U32 = mybir.dt.uint32
ALU = mybir.AluOpType
ACT = mybir.ActivationFunctionType
AX_X = mybir.AxisListType.X

HEADS, KV_HEADS, HEAD = 16, 8, 64
LN_EPS = 1e-5
TOK_BLOCK = 512
TILES = TOK_BLOCK // P


START = 2


def alone(eng, sem):
    eng.sem_inc(sem, 1)


def split_passes(hi_a, lo_a, hi_b, lo_b):
    return ((hi_a, hi_b), (hi_a, lo_b), (lo_a, hi_b))


def project_phase(nc, x, w_qkv_t, b_qk, identity, same_head, qk_scratch, v_scratch):
    tokens, width = x.shape
    KT = width // P
    cols = w_qkv_t.shape[1]
    blocks = tokens // TOK_BLOCK
    qk_tiles = qk_scratch.shape[1]
    outs_per_block = qk_tiles + TILES
    QK_PER_CHUNK = qk_tiles // TILES
    CH = QK_PER_CHUNK + 1
    MM_BANKS = CH
    STAGES = QK_PER_CHUNK
    pieces = cols // TOK_BLOCK
    W_PER_TILE = KT // TILES
    assert pieces == STAGES + 1

    with ExitStack() as ctx:
        sb = lambda n, s, d: ctx.enter_context(nc.sbuf_tensor(n, s, d))
        sem = lambda n: ctx.enter_context(nc.semaphore(n))
        w_hi = sb("w_hi", [P, KT, cols], F32R)
        w_lo = sb("w_lo", [P, KT, cols], F32R)
        h_hi = [sb(f"h_hi{b}", [P, KT, TOK_BLOCK], F32R) for b in range(2)]
        h_lo = [sb(f"h_lo{b}", [P, KT, TOK_BLOCK], F32R) for b in range(2)]
        xt = sb("xt", [P, width], F32)
        stage = [sb(f"stage{b}", [P, TOK_BLOCK], F32) for b in range(STAGES)]
        squares = [sb(f"squares{b}", [P, TOK_BLOCK], F32) for b in range(2)]
        piece_in = stage + squares[:1]
        ident = sb("ident", [P, P], F32)
        ones = sb("ones", [P, P], F32)
        bias = sb("bias", [P, qk_tiles], F32)
        stats = sb("stats", [P, 2, 6], F32)
        moments = [sb(f"moments{b}", [P, 2], F32) for b in range(2)]
        var_eps = sb("var_eps", [P, 1], F32)
        rstd = [sb(f"rstd{b}", [P, 1], F32) for b in range(2)]
        neg_half = sb("neg_half", [P, 1], F32)
        mm = [ctx.enter_context(nc.psum_tensor(f"mm{b}", [P, TOK_BLOCK], F32)) for b in range(MM_BANKS)]
        turn = [ctx.enter_context(nc.psum_tensor(f"turn{b}", [P, KT // 2, P], F32)) for b in range(2)]
        norm_ps = ctx.enter_context(nc.psum_tensor("norm_ps", [P, TOK_BLOCK], F32))

        consts_in = sem("p_consts_in")
        parted = {e: sem(f"p_parted_{e}") for e in ("pool", "dve")}
        w_in = [sem(f"p_w_in{b}") for b in range(pieces)]
        w_hi_done = sem("p_w_hi_done")
        w_split = sem("p_w_split")
        x_in = sem("p_x_in")
        stat_step = sem("p_stat_step")
        rstd_step = sem("p_rstd_step")
        normed = sem("p_normed")
        turned = sem("p_turned")
        hi_done = sem("p_hi_done")
        lo_done = sem("p_lo_done")
        mm_done = sem("p_mm_done")
        evac = sem("p_evac")
        norm_done = sem("p_norm_done")
        root_done = sem("p_root_done")
        recip_done = sem("p_recip_done")
        scaled = sem("p_scaled")
        stored = [sem(f"p_stored{b}") for b in range(STAGES)]

        block = ctx.enter_context(nc.Block())

        def per_block(eng, chunk):
            with eng.Fori(0, blocks // 2 - 1) as i:
                for b in range(2):
                    for t in range(TILES):
                        chunk(2 * i + b, b, t, True, False)
            for b in range(2):
                for t in range(TILES):
                    chunk(blocks - 2 + b, b, t, b == 0, True)

        def piece(k, q):
            return (slice(None), bass.ds(k, 1), slice(q * TOK_BLOCK, (q + 1) * TOK_BLOCK))

        @block.sync
        def _(sp):
            for s in stored:
                sp.sem_inc(s, START)
            sp.dma_start(ident[:], identity).then_inc(consts_in, 16)
            sp.dma_start(xt[:], x[0:P, :]).then_inc(x_in, 16)
            sp.dma_start(ones[:], same_head).then_inc(consts_in, 16)
            sp.dma_start(bias[:], b_qk).then_inc(consts_in, 16)

            def load_w(k, q):
                sp.dma_start(piece_in[q][:], w_qkv_t[bass.ts(k, P), q * TOK_BLOCK:(q + 1) * TOK_BLOCK]).then_inc(w_in[q], 16)

            def load_x(n):
                sp.wait_ge(turned, n)
                sp.dma_start(xt[:], x[bass.ts(n, P), :]).then_inc(x_in, 16)

            for q in range(pieces):
                load_w(0, q)
            for t in range(TILES):
                with sp.Fori(max(1, t * W_PER_TILE), (t + 1) * W_PER_TILE) as k:
                    for q in range(pieces):
                        sp.wait_ge(w_split, pieces * (k - 1) + q + 1)
                        load_w(k, q)
                load_x(t + 1)

            def chunk(blk, par, t, more, peeled):
                for jj in range(CH):
                    out = blk * outs_per_block + t * CH + jj
                    if jj < QK_PER_CHUNK:
                        m = t * QK_PER_CHUNK + jj
                        sp.wait_ge(scaled, START + blk * qk_tiles + m + 1)
                        sp.dma_start(qk_scratch[blk, m], stage[jj][:]).then_inc(stored[jj], 16)
                        if jj == 0 and more and not (peeled and t == TILES - 1):
                            load_x((blk + 1) * TILES + t + 1)
                    else:
                        sp.wait_ge(evac, START + out + 1)
                        sp.dma_start(v_scratch[bass.ts(blk * TILES + t, P), :], stage[0][:]).then_inc(stored[0], 16)
            per_block(sp, chunk)
            for b in range(STAGES):
                sp.wait_ge(stored[b], START + 16 * blocks * TILES * (2 if b == 0 else 1))

        @block.gpsimd
        def _(pool):
            nc.gpsimd.memset(neg_half[:], -0.5).then_inc(rstd_step, 1)

            def rstd_of(n, b):
                pool.wait_ge(stat_step, 3 * n + 3)
                pool.wait_ge(rstd_step, 2 * n + 1)
                alone(pool, parted["pool"])
                nc.gpsimd.tensor_scalar(var_eps[:], moments[b][:, 1:2], LN_EPS, None, ALU.add).then_inc(rstd_step, 1)
                pool.wait_ge(rstd_step, 2 * n + 2)
                nc.gpsimd.tensor_tensor(rstd[b][:], var_eps[:], neg_half[:], ALU.pow).then_inc(rstd_step, 1)

            for t in range(TILES):
                rstd_of(t, t % 2)

            def chunk(blk, par, t, more, peeled):
                if more:
                    rstd_of((blk + 1) * TILES + t, t % 2)
            per_block(pool, chunk)

        @block.vector
        def _(dve):
            dve.sem_inc(scaled, START)
            def split_weights(k, q):
                dve.wait_ge(w_hi_done, pieces * k + q + 1)
                nc.vector.tensor_tensor(w_lo[piece(k, q)].rearrange("p a n -> p (a n)"), piece_in[q][:],
                                        w_hi[piece(k, q)].rearrange("p a n -> p (a n)").bitcast(F32),
                                        ALU.subtract).then_inc(w_split, 1)

            def norm(n, b):
                dve.wait_ge(x_in, 16 * n + 16)
                dve.wait_ge(stat_step, 3 * n)
                for c in range(2):
                    nc.vector.bn_stats(stats[:, c, :], xt[:, c * 512:(c + 1) * 512]).then_inc(stat_step, 1)
                dve.wait_ge(stat_step, 3 * n + 2)
                alone(dve, parted["dve"])
                nc.vector.bn_aggr(moments[b][:], stats[:]).then_inc(stat_step, 1)
                dve.wait_ge(rstd_step, 2 * n + 3)
                dve.wait_ge(stat_step, 3 * n + 3)
                nc.vector.tensor_scalar(xt[:], xt[:], moments[b][:, 0:1], rstd[b][:], ALU.subtract,
                                        ALU.mult).then_inc(normed, 1)

            def low(n, par, t):
                dve.wait_ge(hi_done, n + 1)
                for c in range(2):
                    at = (slice(None), slice(c * KT // 2, (c + 1) * KT // 2), slice(t * P, (t + 1) * P))
                    last = nc.vector.tensor_tensor(h_lo[par][at], turn[c][:], h_hi[par][at].bitcast(F32), ALU.subtract)
                last.then_inc(lo_done, 1)

            for t in range(TILES):
                norm(t, t % 2)
                with dve.Fori(t * W_PER_TILE, (t + 1) * W_PER_TILE) as k:
                    for q in range(pieces):
                        split_weights(k, q)
                low(t, 0, t)

            def chunk(blk, par, t, more, peeled):
                n = (blk + 1) * TILES + t
                if more:
                    norm(n, t % 2)
                for jj in range(QK_PER_CHUNK):
                    m = t * QK_PER_CHUNK + jj
                    sq = squares[m % 2]
                    dve.wait_ge(root_done, START + blk * qk_tiles + m + 1)
                    nc.vector.reciprocal(sq[:], sq[:]).then_inc(recip_done, 1)
                    dve.wait_ge(recip_done, blk * qk_tiles + m + 1)
                    nc.vector.scalar_tensor_tensor(out=stage[jj][:], in0=sq[:], scalar=1e6, in1=stage[jj][:],
                                                   op0=ALU.min, op1=ALU.mult).then_inc(scaled, 1)
                    if more and jj == 0:
                        low(n, 1 - par, t)
            per_block(dve, chunk)

        @block.scalar
        def _(act):
            act.sem_inc(evac, START)
            act.sem_inc(root_done, START)
            act.wait_ge(consts_in, 48)

            def high(n, par, t):
                act.wait_ge(turned, n + 1)
                for c in range(2):
                    at = (slice(None), slice(c * KT // 2, (c + 1) * KT // 2), slice(t * P, (t + 1) * P))
                    last = nc.scalar.activation(h_hi[par][at], turn[c][:], ACT.Copy)
                last.then_inc(hi_done, 1)

            for t in range(TILES):
                with act.Fori(t * W_PER_TILE, (t + 1) * W_PER_TILE) as k:
                    for q in range(pieces):
                        act.wait_ge(w_in[q], 16 * k + 16)
                        nc.scalar.activation(w_hi[piece(k, q)].rearrange("p a n -> p (a n)"), piece_in[q][:],
                                             ACT.Copy).then_inc(w_hi_done, 1)
                high(t, 0, t)

            def chunk(blk, par, t, more, peeled):
                for jj in range(CH):
                    out = blk * outs_per_block + t * CH + jj
                    b = jj % STAGES
                    act.wait_ge(mm_done, out + 1)
                    earlier = 2 * (blk * TILES + t) + jj // STAGES if b == 0 else blk * TILES + t
                    act.wait_ge(stored[b], START + 16 * earlier)
                    if jj < QK_PER_CHUNK:
                        m = t * QK_PER_CHUNK + jj
                        nc.scalar.activation(stage[b][:], mm[jj][:], ACT.Identity, bias=bias[:, m:m + 1])
                        act.wait_ge(scaled, START + blk * qk_tiles + m - 1)
                        nc.scalar.activation(squares[m % 2][:], mm[jj][:], ACT.Square, bias=bias[:, m:m + 1]).then_inc(evac, 1)
                        if jj == 1 and more:
                            high((blk + 1) * TILES + t, 1 - par, t)
                        act.wait_ge(norm_done, blk * qk_tiles + m + 1)
                        nc.scalar.activation(squares[m % 2][:], norm_ps[:], ACT.Sqrt).then_inc(root_done, 1)
                    else:
                        nc.scalar.activation(stage[b][:], mm[jj][:], ACT.Copy).then_inc(evac, 1)
            per_block(act, chunk)

        @block.tensor
        def _(pe):
            pe.wait_ge(consts_in, 48)

            def transposes(n):
                pe.wait_ge(normed, n + 1)
                pe.wait_ge(lo_done, n)
                for k in range(KT):
                    last = nc.tensor.transpose(turn[k * 2 // KT][:, k % (KT // 2), :], xt[:, k * P:(k + 1) * P], ident[:])
                last.then_inc(turned, 1)

            for t in range(TILES):
                transposes(t)
            pe.wait_ge(w_split, pieces * KT)

            def norms(blk, out, m):
                pe.wait_ge(evac, START + out + 1)
                pe.wait_ge(root_done, START + blk * qk_tiles + m)
                nc.tensor.matmul(norm_ps[:], ones[:], squares[m % 2][:], start=True, stop=True).then_inc(norm_done, 1)

            def chunk(blk, par, t, more, peeled):
                if t == 0:
                    pe.wait_ge(lo_done, (blk + 1) * TILES)
                for jj in range(CH):
                    out = blk * outs_per_block + t * CH + jj
                    bank = mm[jj]
                    if t or jj == MM_BANKS - 1:
                        pe.wait_ge(evac, START + out - MM_BANKS + 1)
                    hh, hl = h_hi[par], h_lo[par]
                    for k in range(KT):
                        if jj < QK_PER_CHUNK:
                            c = slice((t * QK_PER_CHUNK + jj) * P, (t * QK_PER_CHUNK + jj + 1) * P)
                            terms = split_passes(w_hi[:, k, c], w_lo[:, k, c], hh[:, k, :], hl[:, k, :])
                        else:
                            c = slice(t * P, (t + 1) * P)
                            terms = split_passes(hh[:, k, c], hl[:, k, c], w_hi[:, k, qk_tiles * P:], w_lo[:, k, qk_tiles * P:])
                        for s, (a, b) in enumerate(terms):
                            last = nc.tensor.matmul(bank[:], a, b, start=(k == 0 and s == 0), stop=(k == KT - 1 and s == 2))
                    last.then_inc(mm_done, 1)
                    if jj:
                        norms(blk, out - 1, t * QK_PER_CHUNK + jj - 1)
                    if jj == 1 and more:
                        transposes((blk + 1) * TILES + t)
                if more and t == TILES - 1:
                    pe.wait_ge(evac, START + (blk + 1) * outs_per_block - 1)
            per_block(pe, chunk)


ROUND = 1.5 * 2.0 ** 23
TWO_PI = 6.2831850
GROUP = P // KV_HEADS
ROTARY_SHIFT = HEAD // 2


def mix_phase(nc, x, qk_scratch, v_scratch, cos_t, sin_t, features, phase, v_bias, own_token, w_o_t, o_bias,
              router, router_bias, out, score_out):
    tokens, width = x.shape
    blocks = tokens // TOK_BLOCK
    KT = width // P
    q_tiles = HEADS // 2
    rot_tiles = q_tiles + KV_HEADS // 2
    UNITS = KV_HEADS + q_tiles
    UPT = UNITS // TILES
    SUPER = 4 * GROUP
    SUPERS = TOK_BLOCK // SUPER
    SPT = SUPERS // TILES
    QK_RING = 3
    GROUPS = TOK_BLOCK // GROUP
    V_PER_TURN = 8
    HALVES = width // 512
    feature_scale = 2.0 / HEAD

    def rotated_of(u):
        return u // 2 if u < KV_HEADS else u - KV_HEADS // 2

    with ExitStack() as ctx:
        sb = lambda n, s, d=F32: ctx.enter_context(nc.sbuf_tensor(n, s, d))
        ps = lambda n, s: ctx.enter_context(nc.psum_tensor(n, s, F32))
        sem = lambda n: ctx.enter_context(nc.semaphore("m_" + n))
        wo_hi = sb("wo_hi", [P, KT, width], F32R)
        wo_lo = sb("wo_lo", [P, KT, width], F32R)
        qf = sb("qf", [P, q_tiles, TOK_BLOCK])
        kf = sb("kf", [P, TOK_BLOCK, KV_HEADS])
        ctx_hi = [sb(f"ctx_hi{t}", [P, P, GROUP // 2], F32R) for t in range(TILES)]
        ctx_lo = [sb(f"ctx_lo{t}", [P, P, GROUP // 2], F32R) for t in range(TILES)]
        att = [sb(f"att{b}", [P, 2, GROUP // 2, 4, HEADS]) for b in range(2)]
        qk_in = [sb(f"qk_in{b}", [P, TOK_BLOCK]) for b in range(QK_RING)]
        q_cos = [sb(f"q_cos{b}", [P, TOK_BLOCK]) for b in range(2)]
        q_sin = [sb(f"q_sin{b}", [P, TOK_BLOCK]) for b in range(2)]
        turns = [sb(f"turns{b}", [P, TOK_BLOCK]) for b in range(2)]
        whole = sb("whole", [P, TOK_BLOCK])
        cs = sb("cs", [P, 2, TOK_BLOCK])
        vg = sb("vg", [P, GROUPS, HEAD])
        vb = sb("vb", [P, HEAD])
        xr = [sb(f"xr{b}", [P, width]) for b in range(2)]
        y = [sb(f"y{b}", [P, width]) for b in range(2)]
        bo = sb("bo", [P, width])
        wr = sb("wr", [P, width])
        feat_w = sb("feat_w", [P, 6, P])
        phases = sb("phases", [P, 1])
        own = sb("own", [P, GROUP])
        br = sb("br", [P, 1])
        score = sb("score", [P, TILES])
        scores = sb("scores", [P, blocks * TILES])
        stats = sb("m_stats", [P, 2, 6])
        moments = [sb(f"m_moments{b}", [P, 2]) for b in range(2)]
        var_eps = sb("m_var_eps", [P, 1])
        rstd = [sb(f"m_rstd{b}", [P, 1]) for b in range(2)]
        neg_half = sb("m_neg_half", [P, 1])
        feat_ps = ps("feat_ps", [P, TOK_BLOCK])
        att_ps = [[ps(f"att_ps{b}{r}", [P, 4 * P]) for r in range(2)] for b in range(2)]
        ctx_ps = ps("ctx_ps", [P, 4 * P])
        y_ps = [ps(f"y_ps{h}", [P, 512]) for h in range(HALVES)]

        consts_in = sem("consts_in")
        parted = {e: sem(f"parted_{e}") for e in ("pool", "dve", "sp")}
        w_in = [sem(f"w_in{b}") for b in range(2)]
        w_hi_done = sem("w_hi_done")
        w_split = sem("w_split")
        cs_in = sem("cs_in")
        qk_loaded = [sem(f"qk_loaded{b}") for b in range(QK_RING)]
        v_in = sem("v_in")
        v_ready = sem("v_ready")
        cos_done = sem("cos_done")
        sin_done = sem("sin_done")
        p_done = sem("p_done")
        turn_done = sem("turn_done")
        whole_done = sem("whole_done")
        frac_done = sem("frac_done")
        feat_done = sem("feat_done")
        att_done = sem("att_done")
        masked = sem("masked")
        ctx_done = sem("ctx_done")
        ctx_hi_done = sem("ctx_hi_done")
        ctx_lo_done = sem("ctx_lo_done")
        y_done = sem("y_done")
        y_evac = sem("y_evac")
        stat_step = sem("stat_step")
        rstd_step = sem("rstd_step")
        y_normed = sem("y_normed")
        x_loaded = [sem(f"x_loaded{b}") for b in range(2)]
        x1_done = sem("x1_done")
        z_done = sem("z_done")
        scored = sem("scored")
        scores_kept = sem("scores_kept")
        x1_stored = [sem(f"x1_stored{b}") for b in range(2)]
        score_final = sem("score_final")
        score_stored = sem("score_stored")

        v_rows = v_scratch.rearrange("t (g d) -> (t g) d", d=HEAD).rearrange("(n p) d -> n p d", p=P)
        x_rows = x.rearrange("(h n g) d -> n h g d", h=HEADS, g=GROUP // 2)
        out_rows = out.rearrange("(h n g) d -> n h g d", h=HEADS, g=GROUP // 2)

        block = ctx.enter_context(nc.Block())

        def last_unit(m):
            return 2 * m + 1 if m < KV_HEADS // 2 else m + KV_HEADS // 2

        def readers_before(m):
            return last_unit(m - 2) + 1 if m >= 2 else last_unit(m - 2 + rot_tiles) + 1 - UNITS

        def rotations_before(t):
            done = rotated_of(UPT * t - 1) + 2 if t else 0
            return range(done, min(rotated_of(UPT * (t + 1) - 1) + 2, rot_tiles))

        def per_block(eng, chunk):
            with eng.Fori(0, blocks - 1) as i:
                chunk(i, True)
            chunk(blocks - 1, False)

        @block.sync
        def _(sp):
            for dst, src in ((feat_w, features), (phases, phase), (vb, v_bias), (own, own_token), (bo, o_bias),
                             (wr, router), (br, router_bias)):
                sp.dma_start(dst[:], src).then_inc(consts_in, 16)

            def load_cs(blk):
                for j, table in enumerate((cos_t, sin_t)):
                    sp.dma_start(cs[:, j, :], table[:, bass.ts(blk, TOK_BLOCK)]).then_inc(cs_in, 16)

            def load_qk(blk, m):
                tile = m + q_tiles if m < KV_HEADS // 2 else m - KV_HEADS // 2
                sp.dma_start(qk_in[m % QK_RING][:], qk_scratch[blk, tile]).then_inc(qk_loaded[m % QK_RING], 16)

            def load_v(blk):
                with sp.Fori(0, GROUPS // V_PER_TURN) as j:
                    for n in range(V_PER_TURN):
                        sp.dma_start(vg[:, bass.ds(V_PER_TURN * j + n, 1), :].rearrange("p a d -> p (a d)"),
                                     v_rows[bass.ds(blk * GROUPS + V_PER_TURN * j + n, 1)].rearrange("a p d -> (a p) d")).then_inc(v_in, 16)

            def load_x(n, b):
                sp.dma_start(xr[b][:], x_rows[n]).then_inc(x_loaded[b], 16)

            def reload_qk(blk, m):
                for s in (cos_done, sin_done):
                    sp.wait_ge(s, rot_tiles * blk + m - QK_RING + 1)
                alone(sp, parted["sp"])
                load_qk(blk, m)

            def store_x1(blk, t):
                sp.wait_ge(x1_done, blk * TILES + t + 1)
                sp.dma_start(out_rows[blk * TILES + t], xr[t % 2][:]).then_inc(x1_stored[t % 2], 16)

            load_cs(0)
            for m in range(QK_RING):
                load_qk(0, m)
            for k in range(2):
                sp.dma_start(xr[k][:], w_o_t[k * P:(k + 1) * P, :]).then_inc(w_in[k], 16)
            with sp.Fori(1, KT // 2) as j:
                for b in range(2):
                    sp.wait_ge(w_split, 2 * j + b - 1)
                    sp.dma_start(xr[b][:], w_o_t[bass.ts(2 * j + b, P), :]).then_inc(w_in[b], 16)
            load_v(0)
            for m in range(QK_RING, rot_tiles):
                reload_qk(0, m)
            for b in range(2):
                sp.wait_ge(w_split, KT - 1 + b)
                load_x(b, b)

            def chunk(blk, more):
                if more:
                    for s in (cos_done, sin_done):
                        sp.wait_ge(s, rot_tiles * (blk + 1))
                    alone(sp, parted["sp"])
                    load_cs(blk + 1)
                    for m in range(QK_RING):
                        load_qk(blk + 1, m)
                    sp.wait_ge(ctx_done, SUPERS * (blk + 1))
                    alone(sp, parted["sp"])
                    load_v(blk + 1)
                for t in range(TILES):
                    if more:
                        for m in range(QK_RING + 3 * t, min(QK_RING + 3 * t + 3, rot_tiles)):
                            reload_qk(blk + 1, m)
                    store_x1(blk, t)
                    if more or t < TILES - 2:
                        sp.wait_ge(x1_stored[t % 2], 16 * (blk * 2 + t // 2 + 1))
                        sp.wait_ge(z_done, blk * TILES + t + 1)
                        load_x(blk * TILES + t + 2, t % 2)
            per_block(sp, chunk)
            sp.wait_ge(score_final, 1)
            sp.dma_start(score_out, scores[:]).then_inc(score_stored, 16)
            for b in range(2):
                sp.wait_ge(x1_stored[b], 16 * blocks * TILES // 2)
            sp.wait_ge(score_stored, 16)

        @block.gpsimd
        def _(pool):
            nc.gpsimd.memset(neg_half[:], -0.5).then_inc(rstd_step, 1)
            pool.wait_ge(consts_in, 16 * 7)

            def rstd_of(e, b):
                pool.wait_ge(stat_step, START + 3 * e + 3)
                pool.wait_ge(rstd_step, 2 * e + 1)
                alone(pool, parted["pool"])
                nc.gpsimd.tensor_scalar(var_eps[:], moments[b][:, 1:2], LN_EPS, None, ALU.add).then_inc(rstd_step, 1)
                pool.wait_ge(rstd_step, 2 * e + 2)
                nc.gpsimd.tensor_tensor(rstd[b][:], var_eps[:], neg_half[:], ALU.pow).then_inc(rstd_step, 1)

            def rotate(blk, m):
                pool.wait_ge(qk_loaded[m % QK_RING], 16 * (blk * (rot_tiles // QK_RING) + m // QK_RING + 1))
                if m == 0:
                    pool.wait_ge(cs_in, 32 * (blk + 1))
                if m >= 2 or not (isinstance(blk, int) and blk == 0):
                    pool.wait_ge(p_done, UNITS * blk + readers_before(m))
                nc.gpsimd.tensor_tensor(q_sin[m % 2][:], qk_in[m % QK_RING][:], cs[:, 1, :], ALU.mult).then_inc(sin_done, 1)

            def add_v_bias(blk):
                pool.wait_ge(v_in, 16 * GROUPS * (blk + 1))
                nc.gpsimd.tensor_tensor(vg[:], vg[:], vb[:].unsqueeze(1).to_broadcast([P, GROUPS, HEAD]),
                                        ALU.add).then_inc(v_ready, 1)

            def residual(n, pairs, b):
                pool.wait_ge(y_normed, n + 1)
                pool.wait_ge(x_loaded[b], 16 * (pairs + 1))
                nc.gpsimd.tensor_tensor(xr[b][:], xr[b][:], y[b][:], ALU.add).then_inc(x1_done, 1)

            for m in range(rot_tiles):
                rotate(0, m)
            add_v_bias(0)

            def chunk(blk, more):
                for t in range(TILES):
                    n = blk * TILES + t
                    if more:
                        for m in rotations_before(t):
                            rotate(blk + 1, m)
                    rstd_of(2 * n, 0)
                    residual(n, blk * 2 + t // 2, t % 2)
                    rstd_of(2 * n + 1, 1)
                if more:
                    add_v_bias(blk + 1)
            per_block(pool, chunk)

        @block.vector
        def _(dve):
            dve.sem_inc(ctx_lo_done, START)
            dve.sem_inc(stat_step, START)
            with dve.Fori(0, KT // 2) as j:
                for b in range(2):
                    dve.wait_ge(w_hi_done, 2 * j + b + 1)
                    k = 2 * j + b
                    nc.vector.tensor_tensor(wo_lo[:, bass.ds(k, 1), :].rearrange("p a n -> p (a n)"), xr[b][:],
                                            wo_hi[:, bass.ds(k, 1), :].rearrange("p a n -> p (a n)").bitcast(F32),
                                            ALU.subtract).then_inc(w_split, 1)
            dve.wait_ge(consts_in, 16 * 7)

            def rotate(blk, m):
                dve.wait_ge(qk_loaded[m % QK_RING], 16 * (blk * (rot_tiles // QK_RING) + m // QK_RING + 1))
                if m == 0:
                    dve.wait_ge(cs_in, 32 * (blk + 1))
                if m >= 2 or not (isinstance(blk, int) and blk == 0):
                    dve.wait_ge(p_done, UNITS * blk + readers_before(m))
                nc.vector.tensor_tensor(q_cos[m % 2][:], qk_in[m % QK_RING][:], cs[:, 0, :], ALU.mult).then_inc(cos_done, 1)

            def fraction(blk, u):
                e = UNITS * blk + u
                dve.wait_ge(turn_done, e + 1)
                dve.wait_ge(frac_done, e)
                nc.vector.tensor_scalar(whole[:], turns[u % 2][:], ROUND, ROUND, ALU.add, ALU.subtract).then_inc(whole_done, 1)
                dve.wait_ge(whole_done, e + 1)
                nc.vector.tensor_tensor(turns[u % 2][:], turns[u % 2][:], whole[:], ALU.subtract).then_inc(frac_done, 1)

            def units(blk, t, half):
                per = UPT // 2
                for u in range(UPT * t + per * half, UPT * t + per * (half + 1)):
                    if u == 0:
                        rotate(blk, 0)
                        rotate(blk, 1)
                    elif rotated_of(u) != rotated_of(u - 1) and rotated_of(u) + 1 < rot_tiles:
                        rotate(blk, rotated_of(u) + 1)
                    fraction(blk, u)

            def moments_of(e, src, b):
                dve.wait_ge(stat_step, START + 3 * e)
                for c in range(HALVES):
                    nc.vector.bn_stats(stats[:, c, :], src[:, c * 512:(c + 1) * 512]).then_inc(stat_step, 1)
                dve.wait_ge(stat_step, START + 3 * e + 2)
                alone(dve, parted["dve"])
                nc.vector.bn_aggr(moments[b][:], stats[:]).then_inc(stat_step, 1)

            def normalise(e, dst, src, b, done):
                dve.wait_ge(rstd_step, 2 * e + 3)
                dve.wait_ge(stat_step, START + 3 * e + 3)
                nc.vector.tensor_scalar(dst[:], src[:], moments[b][:, 0:1], rstd[b][:], ALU.subtract, ALU.mult).then_inc(done, 1)

            for t in range(TILES):
                for half in range(2):
                    units(0, t, half)

            def mask(blk, s):
                e = SUPERS * blk + s
                dve.wait_ge(att_done, e + 1)
                if s >= 2:
                    dve.wait_ge(ctx_done, e - 1)
                for r in range(2):
                    src = att_ps[s % 2][r][:].rearrange("p (gh t a) -> p gh t a", t=GROUP // 2, a=2)
                    dst = att[s % 2][:, :, :, :, r::2].rearrange("p a t g h -> p (g h) t a")
                    keep = own[:].rearrange("p (t a) -> p t a", a=2).unsqueeze(1).to_broadcast([P, 4 * q_tiles, GROUP // 2, 2])
                    last = nc.vector.tensor_tensor(dst, src, keep, ALU.mult)
                last.then_inc(masked, 1)

            def low(blk, s):
                e = SUPERS * blk + s
                dve.wait_ge(ctx_hi_done, e + 1)
                at = (slice(None), slice(None), slice(4 * (s % SPT), 4 * (s % SPT) + 4))
                nc.vector.scalar_tensor_tensor(out=ctx_lo[s // SPT][at], in0=ctx_ps[:].rearrange("p (g c) -> p c g", g=4),
                                               scalar=feature_scale, in1=ctx_hi[s // SPT][at].bitcast(F32),
                                               op0=ALU.mult, op1=ALU.subtract).then_inc(ctx_lo_done, 1)

            def chunk(blk, more):
                mask(blk, 0)
                for s in range(SUPERS):
                    if s + 1 < SUPERS:
                        mask(blk, s + 1)
                    low(blk, s)
                for t in range(TILES):
                    n = blk * TILES + t
                    for h in range(HALVES):
                        if more:
                            units(blk + 1, t, h)
                        dve.wait_ge(y_done, HALVES * n + h + 1)
                        c = slice(h * 512, (h + 1) * 512)
                        nc.vector.tensor_tensor(y[t % 2][:, c], y_ps[h][:], bo[:, c], ALU.add).then_inc(y_evac, 1)
                    dve.wait_ge(y_evac, HALVES * (n + 1))
                    moments_of(2 * n, y[t % 2], 0)
                    normalise(2 * n, y[t % 2], y[t % 2], 0, y_normed)
                    dve.wait_ge(x1_done, n + 1)
                    moments_of(2 * n + 1, xr[t % 2], 1)
                    normalise(2 * n + 1, y[t % 2], xr[t % 2], 1, z_done)
                    dve.wait_ge(z_done, n + 1)
                    nc.vector.tensor_tensor_reduce(y[t % 2][:], y[t % 2][:], wr[:], 1.0, 0.0, ALU.mult, ALU.add,
                                                   score[:, t:t + 1]).then_inc(scored, 1)
                dve.wait_ge(scored, TILES * (blk + 1))
                nc.vector.tensor_copy(scores[:, bass.ds(blk * TILES, TILES)], score[:]).then_inc(scores_kept, 1)
            per_block(dve, chunk)
            dve.wait_ge(scores_kept, blocks)
            nc.vector.tensor_scalar(scores[:], scores[:], br[:], None, ALU.add).then_inc(score_final, 1)

        @block.scalar
        def _(act):
            with act.Fori(0, KT // 2) as j:
                for b in range(2):
                    act.wait_ge(w_in[b], 16 * j + 16)
                    nc.scalar.activation(wo_hi[:, bass.ds(2 * j + b, 1), :].rearrange("p a n -> p (a n)"), xr[b][:],
                                         ACT.Copy).then_inc(w_hi_done, 1)
            act.wait_ge(consts_in, 16 * 7)

            def sine(blk, u):
                act.wait_ge(frac_done, UNITS * blk + u + 1)
                dst = kf[:, :, u] if u < KV_HEADS else qf[:, u - KV_HEADS, :]
                nc.scalar.activation(dst, turns[u % 2][:], ACT.Sin, scale=TWO_PI).then_inc(feat_done, 1)

            def units(blk, t):
                for u in range(UPT * t, UPT * (t + 1)):
                    act.wait_ge(p_done, UNITS * blk + u + 1)
                    if u >= 2:
                        act.wait_ge(feat_done, UNITS * blk + u - 1)
                    nc.scalar.activation(turns[u % 2][:], feat_ps[:], ACT.Identity, bias=phases[:],
                                         scale=0.15915494309189535).then_inc(turn_done, 1)
                    if u:
                        sine(blk, u - 1)
                if t == TILES - 1:
                    sine(blk, UNITS - 1)
            for t in range(TILES):
                units(0, t)

            def chunk(blk, more):
                for s in range(SUPERS):
                    e = SUPERS * blk + s
                    act.wait_ge(ctx_done, e + 1)
                    nc.scalar.activation(ctx_hi[s // SPT][:, :, 4 * (s % SPT):4 * (s % SPT) + 4],
                                         ctx_ps[:].rearrange("p (g c) -> p c g", g=4), ACT.Copy,
                                         scale=feature_scale).then_inc(ctx_hi_done, 1)
                if more:
                    for t in range(TILES):
                        units(blk + 1, t)
            per_block(act, chunk)

        @block.tensor
        def _(pe):
            pe.wait_ge(consts_in, 16 * 7)

            def unit(blk, u):
                m = rotated_of(u)
                for s in (cos_done, sin_done):
                    pe.wait_ge(s, rot_tiles * blk + m + 1)
                pe.wait_ge(turn_done, UNITS * blk + u)
                kind = 1 + u % 2 if u < KV_HEADS else 0
                nc.tensor.matmul(feat_ps[:], feat_w[:, 2 * kind, :], q_cos[m % 2][:], start=True, stop=False)
                nc.tensor.matmul(feat_ps[:], feat_w[:, 2 * kind + 1, :], q_sin[m % 2][:], start=False, stop=True).then_inc(p_done, 1)

            for u in range(UNITS):
                unit(0, u)
            pe.wait_ge(w_split, KT)

            def scores_of(blk, s):
                e = SUPERS * blk + s
                if s >= 2:
                    pe.wait_ge(masked, e - 1)
                for r in range(2):
                    half = slice(r * HEAD, (r + 1) * HEAD)
                    for g in range(4):
                        tok = slice((4 * s + g) * GROUP, (4 * s + g + 1) * GROUP)
                        last = nc.tensor.matmul(att_ps[s % 2][r][:, g * P:(g + 1) * P],
                                                kf[half, tok, :].rearrange("p t g -> p (t g)"), qf[half, :, tok],
                                                start=True, stop=True)
                last.then_inc(att_done, 1)

            def context_of(blk, s):
                e = SUPERS * blk + s
                pe.wait_ge(masked, e + 1)
                pe.wait_ge(ctx_lo_done, START + e)
                for g in range(4):
                    for a in range(2):
                        last = nc.tensor.matmul(ctx_ps[a * HEAD:(a + 1) * HEAD, g * P:(g + 1) * P], vg[:, 4 * s + g, :],
                                                att[s % 2][:, a, :, g, :], start=True, stop=True)
                last.then_inc(ctx_done, 1)

            def chunk(blk, more):
                pe.wait_ge(feat_done, UNITS * (blk + 1))
                pe.wait_ge(v_ready, blk + 1)
                scores_of(blk, 0)
                for s in range(SUPERS):
                    if s + 1 < SUPERS:
                        scores_of(blk, s + 1)
                    context_of(blk, s)
                for t in range(TILES):
                    pe.wait_ge(ctx_lo_done, START + SUPERS * blk + SPT * (t + 1))
                    for h in range(HALVES):
                        if t:
                            pe.wait_ge(y_evac, HALVES * (blk * TILES + t - 1) + h + 1)
                        cols = slice(h * 512, (h + 1) * 512)
                        for k in range(KT):
                            rows = slice(k * HEADS, (k + 1) * HEADS)
                            a_hi = ctx_hi[t][:, rows, :].rearrange("p h g -> p (h g)")
                            a_lo = ctx_lo[t][:, rows, :].rearrange("p h g -> p (h g)")
                            for s, (a, b) in enumerate(split_passes(a_hi, a_lo, wo_hi[:, k, cols], wo_lo[:, k, cols])):
                                last = nc.tensor.matmul(y_ps[h][:], a, b, start=(k == 0 and s == 0), stop=(k == KT - 1 and s == 2))
                            if more and k % (KT // 2) == KT // 2 - 1:
                                unit(blk + 1, UPT * t + UPT // 2 * h + k // (KT // 2))
                        last.then_inc(y_done, 1)
            per_block(pe, chunk)


def route_phase(nc, score_in, order_masks, token_ids, lane_ids, count_up, chosen, keep):
    lanes, per_lane = score_in.shape
    tokens = lanes * per_lane
    slots_a = keep // P
    SIGN, EXPONENT, EXPONENT_LOW = -2 ** 31, 0x7F800000, 0x00800000

    with ExitStack() as ctx:
        sb = lambda n, s, d=F32: ctx.enter_context(nc.sbuf_tensor("r_" + n, s, d))
        ps = lambda n, s: ctx.enter_context(nc.psum_tensor("r_" + n, s, F32))
        sem = lambda n: ctx.enter_context(nc.semaphore("r_" + n))
        every = sb("every", [P, tokens])
        above = sb("above", [P, tokens])
        own = sb("own", [P, per_lane])
        masks = sb("masks", [P, 4, P])
        ids = sb("ids", [P, per_lane])
        lane_f = sb("lane_f", [P, 2])
        up = sb("up", [P, P])
        lane = sb("lane", [P, 2], I32)
        prefix = sb("prefix", [P, 1], I32)
        cand = sb("cand", [P, 1], I32)
        flip = sb("flip", [P, 1], I32)
        bits = sb("bits", [P, 1], I32)
        count = sb("count", [P, 1])
        passing = sb("passing", [P, 1])
        best = sb("best", [P, 1])
        best_i = sb("best_i", [P, 1], I32)
        ones = sb("ones", [P, per_lane])
        over = sb("over", [P, per_lane])
        tie = sb("tie", [P, per_lane])
        incl = sb("incl", [P, per_lane])
        excl = sb("excl", [P, per_lane])
        total = sb("total", [P, per_lane])
        n_over = sb("n_over", [P, 1])
        need = sb("need", [P, 1])
        sel = sb("sel", [P, per_lane])
        slot_i = sb("slot_i", [P, per_lane], I32)
        part_i = sb("part_i", [P, 2, per_lane], I32)
        part = sb("part", [P, 2, per_lane])
        picked = sb("picked", [P, per_lane])
        hot_b = sb("hot_b", [P, per_lane, P])
        hot_a = sb("hot_a", [P, per_lane, slots_a])
        rank_ps = ps("rank_ps", [P, per_lane])
        over_ps = ps("over_ps", [P, 1])
        chosen_ps = ps("chosen_ps", [P, slots_a])

        loaded = sem("loaded")
        step = sem("step")
        passed = sem("passed")
        reduced = sem("reduced")
        rank_ready = sem("rank_ready")
        ranked = sem("ranked")
        over_ready = sem("over_ready")
        over_summed = sem("over_summed")
        hot_ready = sem("hot_ready")
        listed = sem("listed")
        shifts = (25, 18, 11, 4, 0)

        block = ctx.enter_context(nc.Block())

        @block.sync
        def _(sp):
            flat = score_in.rearrange("p n -> (p n)").rearrange("(a n) -> a n", a=1)
            sp.dma_start(every[:], flat.to_broadcast([P, tokens])).then_inc(loaded, 16)
            for dst, src in ((own, score_in), (masks, order_masks), (ids, token_ids), (lane_f, lane_ids), (up, count_up)):
                sp.dma_start(dst[:], src).then_inc(loaded, 16)

        @block.gpsimd
        def _(pool):
            for r in range(len(shifts)):
                pool.wait_ge(passed, r + 1)
                nc.gpsimd.partition_all_reduce(best[:], passing[:], P, bass.bass_isa.ReduceOp.max).then_inc(reduced, 1)

        @block.vector
        def _(dve):
            done = [0]

            def link(instruction):
                done[0] += 1
                instruction.then_inc(step, 1)
                dve.wait_ge(step, done[0])

            def threshold_bits(src):
                link(nc.vector.tensor_scalar(flip[:], src[:], 31, -1, ALU.arith_shift_right, ALU.bitwise_xor))
                link(nc.vector.tensor_scalar(flip[:], flip[:], SIGN, None, ALU.bitwise_or))
                link(nc.vector.tensor_tensor(bits[:], src[:], flip[:], ALU.bitwise_xor))
                link(nc.vector.tensor_scalar(flip[:], bits[:], EXPONENT, None, ALU.bitwise_and))
                link(nc.vector.tensor_scalar(flip[:], flip[:], float(EXPONENT), -1.0, ALU.is_equal, ALU.mult))
                link(nc.vector.tensor_scalar(best_i[:], flip[:], EXPONENT_LOW, -1, ALU.bitwise_and, ALU.bitwise_xor))
                link(nc.vector.tensor_tensor(bits[:], bits[:], best_i[:], ALU.bitwise_and))
                link(nc.vector.tensor_scalar(flip[:], flip[:], EXPONENT_LOW - 1, None, ALU.bitwise_and))
                link(nc.vector.tensor_tensor(bits[:], bits[:], flip[:], ALU.bitwise_or))

            dve.wait_ge(loaded, 16 * 6)
            link(nc.vector.tensor_copy(lane[:], lane_f[:]))
            link(nc.vector.memset(prefix[:], 0))
            link(nc.vector.memset(ones[:], 1.0))
            for r, shift in enumerate(shifts):
                narrow = 1 if shift == 0 else 0
                link(nc.vector.tensor_scalar(cand[:], lane[:, narrow:narrow + 1], shift, None, ALU.logical_shift_left))
                link(nc.vector.tensor_tensor(cand[:], cand[:], prefix[:], ALU.bitwise_or))
                threshold_bits(cand)
                link(nc.vector.tensor_scalar(above[:], every[:], bits[:].bitcast(F32), 0.0, ALU.is_ge, ALU.add,
                                             accum_out=count[:]))
                nc.vector.tensor_scalar(passing[:], count[:], float(keep), lane_f[:, narrow:narrow + 1], ALU.is_ge,
                                        ALU.mult).then_inc(passed, 1)
                dve.wait_ge(reduced, r + 1)
                link(nc.vector.tensor_copy(best_i[:], best[:]))
                link(nc.vector.tensor_scalar(best_i[:], best_i[:], shift, None, ALU.logical_shift_left))
                link(nc.vector.tensor_tensor(prefix[:], prefix[:], best_i[:], ALU.bitwise_or))
            threshold_bits(prefix)
            limit = bits[:].bitcast(F32)
            link(nc.vector.tensor_scalar(over[:], own[:], limit, 0.0, ALU.is_gt, ALU.add, accum_out=n_over[:]))
            nc.vector.tensor_scalar(tie[:], own[:], limit, None, ALU.is_equal).then_inc(over_ready, 1)

            def rank_operands(flags):
                link(nc.vector.tensor_tensor_scan(incl[:], ones[:], flags[:], 0.0, ALU.mult, ALU.add))
                link(nc.vector.tensor_tensor(excl[:], incl[:], flags[:], ALU.subtract))
                nc.vector.tensor_scalar(total[:], flags[:], 0.0, incl[:, per_lane - 1:per_lane], ALU.mult,
                                        ALU.add).then_inc(rank_ready, 1)

            dve.wait_ge(over_ready, 1)
            rank_operands(tie)
            dve.wait_ge(over_summed, 1)
            link(nc.vector.tensor_scalar(need[:], over_ps[:], -1.0, float(keep), ALU.mult, ALU.add))
            dve.wait_ge(ranked, 1)
            link(nc.vector.tensor_scalar(sel[:], rank_ps[:], need[:], None, ALU.is_lt))
            link(nc.vector.tensor_tensor(sel[:], sel[:], tie[:], ALU.mult))
            link(nc.vector.tensor_tensor(sel[:], sel[:], over[:], ALU.add))
            rank_operands(sel)
            dve.wait_ge(ranked, 2)
            link(nc.vector.tensor_copy(slot_i[:], rank_ps[:]))
            link(nc.vector.tensor_scalar(part_i[:, 0, :], slot_i[:], P - 1, None, ALU.bitwise_and))
            link(nc.vector.tensor_scalar(part_i[:, 1, :], slot_i[:], P.bit_length() - 1, None, ALU.arith_shift_right))
            link(nc.vector.tensor_copy(part[:], part_i[:]))
            link(nc.vector.tensor_tensor(picked[:], sel[:], ids[:], ALU.mult))
            link(nc.vector.tensor_tensor(hot_b[:], up[:].unsqueeze(1).to_broadcast([P, per_lane, P]),
                                         part[:, 0, :].unsqueeze(2).to_broadcast([P, per_lane, P]), ALU.is_equal))
            link(nc.vector.tensor_tensor(hot_a[:], up[:, 0:slots_a].unsqueeze(1).to_broadcast([P, per_lane, slots_a]),
                                         part[:, 1, :].unsqueeze(2).to_broadcast([P, per_lane, slots_a]), ALU.is_equal))
            nc.vector.tensor_tensor(hot_a[:], hot_a[:], picked[:].unsqueeze(2).to_broadcast([P, per_lane, slots_a]),
                                    ALU.mult).then_inc(hot_ready, 1)
            dve.wait_ge(listed, 1)
            nc.vector.tensor_copy(chosen[:], chosen_ps[:])

        @block.tensor
        def _(pe):
            pe.wait_ge(over_ready, 1)
            nc.tensor.matmul(over_ps[:], masks[:, 3, :], n_over[:], start=True, stop=True).then_inc(over_summed, 1)
            for n in range(2):
                pe.wait_ge(rank_ready, n + 1)
                nc.tensor.matmul(rank_ps[:], masks[:, 0, :], total[:], start=True, stop=False)
                nc.tensor.matmul(rank_ps[:], masks[:, 1, :], excl[:], start=False, stop=False)
                nc.tensor.matmul(rank_ps[:], masks[:, 2, :], (tie, sel)[n][:], start=False, stop=True).then_inc(ranked, 1)
            pe.wait_ge(hot_ready, 1)
            for n in range(per_lane):
                last = nc.tensor.matmul(chosen_ps[:], hot_b[:, n, :], hot_a[:, n, :], start=(n == 0), stop=(n == per_lane - 1))
            last.then_inc(listed, 1)


def ffn_phase(nc, x1, w1, b1, w2, b2_rows, identity, chosen, out, keep):
    width, hidden = w1.shape
    KT = width // P
    PASSES = 2
    TT = keep // PASSES // P
    CHUNK = 2 * P
    FT = CHUNK // P
    chunks = hidden // CHUNK
    TB = TT * P // TOK_BLOCK
    steps = chunks * TB
    HALVES = width // 512
    OPS = TILES * HALVES
    O_BANKS = 4
    assert TB == 2

    with ExitStack() as ctx:
        sb = lambda n, s, d=F32: ctx.enter_context(nc.sbuf_tensor("f_" + n, s, d))
        ps = lambda n, s: ctx.enter_context(nc.psum_tensor("f_" + n, s, F32))
        sem = lambda n: ctx.enter_context(nc.semaphore("f_" + n))
        xt_hi = sb("xt_hi", [P, KT, TT * P], F32R)
        xt_lo = sb("xt_lo", [P, KT, TT * P], F32R)
        acc = sb("acc", [P, TT, width])
        w1_raw = sb("w1_raw", [P, KT, CHUNK])
        w2_raw = sb("w2_raw", [P, FT, width])
        w1_hi = [sb(f"w1_hi{b}", [P, KT, CHUNK], F32R) for b in range(2)]
        w1_lo = [sb(f"w1_lo{b}", [P, KT, CHUNK], F32R) for b in range(2)]
        w2_hi = [sb(f"w2_hi{b}", [P, FT, width], F32R) for b in range(2)]
        w2_lo = [sb(f"w2_lo{b}", [P, FT, width], F32R) for b in range(2)]
        h_hi = [sb(f"h_hi{b}", [P, FT, TOK_BLOCK], F32R) for b in range(2)]
        h_lo = [sb(f"h_lo{b}", [P, FT, TOK_BLOCK], F32R) for b in range(2)]
        act_out = [sb(f"act_out{f}", [P, TOK_BLOCK]) for f in range(FT)]
        rows = [sb(f"rows{b}", [P, width]) for b in range(2)]
        ident = sb("ident", [P, P])
        bias = sb("bias", [P, hidden // P])
        stats = sb("stats", [P, 2, 6])
        moments = [sb(f"moments{b}", [P, 2]) for b in range(2)]
        var_eps = sb("var_eps", [P, 1])
        rstd = [sb(f"rstd{b}", [P, 1]) for b in range(2)]
        neg_half = sb("neg_half", [P, 1])
        h_ps = [[ps(f"h_ps{b}{f}", [P, TOK_BLOCK]) for f in range(FT)] for b in range(2)]
        o_ps = [ps(f"o_ps{b}", [P, 512]) for b in range(O_BANKS)]
        turn = [t[:].rearrange("p (k n) -> p k n", n=P) for t in h_ps[0]]

        consts_in = sem("consts_in")
        parted = {e: sem(f"parted_{e}") for e in ("pool", "dve", "act")}
        gathered = [sem(f"gathered{u}") for u in range(TT)]
        stat_step = sem("stat_step")
        rstd_step = sem("rstd_step")
        normed = sem("normed")
        turned = sem("turned")
        x_hi = sem("x_hi")
        x_lo = sem("x_lo")
        acc_set = sem("acc_set")
        w1_in, w2_in = sem("w1_in"), sem("w2_in")
        w1_h, w2_h = sem("w1_h"), sem("w2_h")
        w1_l, w2_l = sem("w1_l"), sem("w2_l")
        h_mm = sem("h_mm")
        gelu_done = sem("gelu_done")
        h_h, h_l = sem("h_h"), sem("h_l")
        o_mm = sem("o_mm")
        added = sem("added")
        y_normed = sem("y_normed")
        regathered = [sem(f"regathered{b}") for b in range(2)]
        summed = sem("summed")
        scattered = [sem(f"scattered{b}") for b in range(2)]

        w1_v = w1.rearrange("(k p) (c f) -> c p k f", p=P, f=CHUNK)
        w2_v = w2.rearrange("(c j p) d -> c p j d", p=P, j=FT)

        block = ctx.enter_context(nc.Block())

        def per_pass(eng, prologue, step, epilogue):
            with eng.Fori(0, PASSES) as hf:
                prologue(hf)
                with eng.Fori(0, chunks // 2 - 1) as i:
                    for q in range(2 * TB):
                        step(hf, 2 * i + q // TB, 2 * TB * i + q, q // TB, q, True)
                for q in range(2 * TB):
                    step(hf, chunks - 2 + q // TB, steps - 2 * TB + q, q // TB, q, q < TB)
                epilogue(hf)

        @block.sync
        def _(sp):
            sp.dma_start(ident[:], identity).then_inc(consts_in, 16)
            sp.dma_start(bias[:], b1).then_inc(consts_in, 16)

            def load_w1(hf, c):
                sp.wait_ge(w1_l, START + chunks * hf + c)
                sp.dma_start(w1_raw[:].unsqueeze(1), w1_v[bass.ds(c, 1)].rearrange("c p k f -> p c k f")).then_inc(w1_in, 16)

            def load_w2(hf, c):
                sp.wait_ge(w2_l, START + chunks * hf + c)
                sp.dma_start(w2_raw[:].unsqueeze(1), w2_v[bass.ds(c, 1)].rearrange("c p j d -> p c j d")).then_inc(w2_in, 16)

            def prologue(hf):
                load_w1(hf, 0)
                load_w2(hf, 0)
                for u in range(TT):
                    sp.wait_ge(turned, TT * hf + u + 1)
                    sp.dma_start(acc[:, u, :], b2_rows).then_inc(acc_set, 16)

            def step(hf, c, s, cp, q, more):
                if more:
                    (load_w1 if q % TB == 0 else load_w2)(hf, c + 1)
            per_pass(sp, prologue, step, lambda hf: None)

        @block.gpsimd
        def _(pool):
            nc.gpsimd.memset(neg_half[:], -0.5).then_inc(rstd_step, 1)

            def rstd_of(e):
                pool.wait_ge(stat_step, START + 3 * e + 3)
                pool.wait_ge(rstd_step, 2 * e + 1)
                nc.gpsimd.tensor_scalar(var_eps[:], moments[e % 2][:, 1:2], LN_EPS, None, ALU.add).then_inc(rstd_step, 1)
                pool.wait_ge(rstd_step, 2 * e + 2)
                nc.gpsimd.tensor_tensor(rstd[e % 2][:], var_eps[:], neg_half[:], ALU.pow).then_inc(rstd_step, 1)

            def gather(dst, tile, done):
                pool.indirect_dma_start(out=dst, out_offset=None, in_=x1,
                                        in_offset=bass.IndirectOffsetOnAxis(ap=chosen[:, tile:tile + 1], axis=0)).then_inc(done, 16)

            for hf in range(PASSES):
                for u in range(TT):
                    if hf:
                        pool.wait_ge(summed, hf * TT - TT + u + 1)
                    gather(acc[:, u, :], hf * TT + u, gathered[u])
                for u in range(TT):
                    rstd_of(hf * 2 * TT + u)
                for b in range(2):
                    if hf:
                        pool.wait_ge(scattered[b], 16 * (hf * TT // 2))
                    gather(rows[b][:], hf * TT + b, regathered[b])
                for u in range(TT):
                    b = u % 2
                    rstd_of(hf * 2 * TT + TT + u)
                    pool.wait_ge(y_normed, hf * TT + u + 1)
                    pool.wait_ge(regathered[b], 16 * (hf * TT // 2 + u // 2 + 1))
                    nc.gpsimd.tensor_tensor(rows[b][:], rows[b][:], acc[:, u, :], ALU.add).then_inc(summed, 1)
                    pool.wait_ge(summed, hf * TT + u + 1)
                    pool.indirect_dma_start(out=out, out_offset=bass.IndirectOffsetOnAxis(
                        ap=chosen[:, hf * TT + u:hf * TT + u + 1], axis=0), in_=rows[b][:], in_offset=None).then_inc(scattered[b], 16)
                    if u + 2 < TT:
                        pool.wait_ge(scattered[b], 16 * (hf * TT // 2 + u // 2 + 1))
                        gather(rows[b][:], hf * TT + u + 2, regathered[b])
            for b in range(2):
                pool.wait_ge(scattered[b], 16 * PASSES * TT // 2)

        @block.vector
        def _(dve):
            dve.sem_inc(added, START)
            dve.sem_inc(h_l, START)
            dve.sem_inc(stat_step, START)
            dve.sem_inc(w1_l, START)
            dve.sem_inc(w2_l, START)
            dve.sem_inc(x_lo, START)
            def moments_of(e, b, u):
                dve.wait_ge(stat_step, START + 3 * e)
                for c in range(HALVES):
                    nc.vector.bn_stats(stats[:, c, :], acc[:, u, c * 512:(c + 1) * 512]).then_inc(stat_step, 1)
                dve.wait_ge(stat_step, START + 3 * e + 2)
                alone(dve, parted["dve"])
                nc.vector.bn_aggr(moments[b][:], stats[:]).then_inc(stat_step, 1)

            def normalise(e, b, u, done):
                dve.wait_ge(rstd_step, 2 * e + 3)
                dve.wait_ge(stat_step, START + 3 * e + 3)
                nc.vector.tensor_scalar(acc[:, u, :], acc[:, u, :], moments[b][:, 0:1], rstd[b][:], ALU.subtract,
                                        ALU.mult).then_inc(done, 1)

            def low_w(raw, hi, lo, high, done, n, cp):
                dve.wait_ge(high, n)
                nc.vector.tensor_tensor(lo[cp][:], raw[:], hi[cp][:].bitcast(F32), ALU.subtract).then_inc(done, 1)

            def low_h(hf, s, q):
                for f in range(FT):
                    dve.wait_ge(h_h, FT * (steps * hf + s) + f + 1)
                    nc.vector.tensor_tensor(h_lo[q % 2][:, f, :], act_out[f][:], h_hi[q % 2][:, f, :].bitcast(F32),
                                            ALU.subtract).then_inc(h_l, 1)

            def low_x(hf, u):
                dve.wait_ge(x_hi, TT * hf + u + 1)
                for c in range(2):
                    at = (slice(None), slice(c * KT // 2, (c + 1) * KT // 2), slice(u * P, (u + 1) * P))
                    last = nc.vector.tensor_tensor(xt_lo[at], turn[c], xt_hi[at].bitcast(F32), ALU.subtract)
                last.then_inc(x_lo, 1)

            def prologue(hf):
                low_w(w1_raw, w1_hi, w1_lo, w1_h, w1_l, chunks * hf + 1, 0)
                low_w(w2_raw, w2_hi, w2_lo, w2_h, w2_l, chunks * hf + 1, 0)
                for u in range(TT + 1):
                    if u < TT:
                        e = 2 * TT * hf + u
                        dve.wait_ge(gathered[u], 16 * hf + 16)
                        moments_of(e, u % 2, u)
                        normalise(e, u % 2, u, normed)
                    if u:
                        low_x(hf, u - 1)
                low_h(hf, 0, 0)
                dve.wait_ge(acc_set, 16 * TT * (hf + 1))
                alone(dve, parted["dve"])

            def step(hf, c, s, cp, q, more):
                if more:
                    if q % TB == 0:
                        low_w(w1_raw, w1_hi, w1_lo, w1_h, w1_l, chunks * hf + c + 2, 1 - cp)
                    else:
                        low_w(w2_raw, w2_hi, w2_lo, w2_h, w2_l, chunks * hf + c + 2, 1 - cp)
                if more or q < 2 * TB - 1:
                    low_h(hf, s + 1, q + 1)
                n = OPS * (steps * hf + s)
                dve.wait_ge(added, START + n)
                for j in range(OPS):
                    dve.wait_ge(o_mm, START + n + j + 1)
                    at = (slice(None), q % TB * TILES + j // HALVES, slice(j % HALVES * 512, (j % HALVES + 1) * 512))
                    nc.vector.tensor_tensor(acc[at], o_ps[j % O_BANKS][:], acc[at], ALU.add).then_inc(added, 1)

            def epilogue(hf):
                dve.wait_ge(added, START + OPS * steps * (hf + 1))
                for u in range(TT):
                    e = 2 * TT * hf + TT + u
                    moments_of(e, u % 2, u)
                    normalise(e, u % 2, u, y_normed)
            per_pass(dve, prologue, step, epilogue)

        @block.scalar
        def _(act):
            act.wait_ge(consts_in, 32)

            def high_w(raw, hi, loaded, done, n, cp):
                act.wait_ge(loaded, 16 * n)
                nc.scalar.activation(hi[cp][:], raw[:], ACT.Copy).then_inc(done, 1)

            def gelu(hf, s, c, q, first=False):
                n = steps * hf + s
                for f in range(FT):
                    act.wait_ge(h_mm, FT * n + f + 1)
                    act.wait_ge(h_l, START + (FT * n if first else FT * (n - 1) + f + 1))
                    alone(act, parted["act"])
                    nc.scalar.activation(act_out[f][:], h_ps[q % 2][f][:], ACT.Gelu_apprx_tanh,
                                         bias=bias[:, bass.ds(c * FT + f, 1)]).then_inc(gelu_done, 1)
                    act.wait_ge(gelu_done, FT * n + f + 1)
                    nc.scalar.activation(h_hi[q % 2][:, f, :], act_out[f][:], ACT.Copy).then_inc(h_h, 1)

            def prologue(hf):
                act.wait_ge(o_mm, START + OPS * steps * hf)
                high_w(w1_raw, w1_hi, w1_in, w1_h, chunks * hf + 1, 0)
                high_w(w2_raw, w2_hi, w2_in, w2_h, chunks * hf + 1, 0)
                for u in range(TT):
                    act.wait_ge(turned, TT * hf + u + 1)
                    for k in range(2):
                        at = (slice(None), slice(k * KT // 2, (k + 1) * KT // 2), slice(u * P, (u + 1) * P))
                        last = nc.scalar.activation(xt_hi[at], turn[k], ACT.Copy)
                    last.then_inc(x_hi, 1)
                gelu(hf, 0, 0, 0, True)

            def step(hf, c, s, cp, q, more):
                n = OPS * (steps * hf + s)
                if more:
                    if q % TB == 0:
                        high_w(w1_raw, w1_hi, w1_in, w1_h, chunks * hf + c + 2, 1 - cp)
                    else:
                        act.wait_ge(o_mm, START + n - OPS)
                        high_w(w2_raw, w2_hi, w2_in, w2_h, chunks * hf + c + 2, 1 - cp)
                if more or q < 2 * TB - 1:
                    act.wait_ge(o_mm, START + n)
                    gelu(hf, s + 1, c + (q % TB == TB - 1), q + 1)
            per_pass(act, prologue, step, lambda hf: None)

        @block.tensor
        def _(pe):
            pe.sem_inc(o_mm, START)
            pe.wait_ge(consts_in, 32)

            def first(hf, c, s, cp, q):
                pe.wait_ge(w1_l, START + chunks * hf + c + 1)
                cols = slice(q % TB * TOK_BLOCK, (q % TB + 1) * TOK_BLOCK)
                for f in range(FT):
                    for k in range(KT):
                        fs = slice(f * P, (f + 1) * P)
                        for t, (a, b) in enumerate(split_passes(w1_hi[cp][:, k, fs], w1_lo[cp][:, k, fs],
                                                                xt_hi[:, k, cols], xt_lo[:, k, cols])):
                            last = nc.tensor.matmul(h_ps[q % 2][f][:], a, b, start=(k == 0 and t == 0), stop=(k == KT - 1 and t == 2))
                    last.then_inc(h_mm, 1)

            def second(hf, c, s, cp, q):
                n = steps * hf + s
                pe.wait_ge(h_l, START + FT * (n + 1))
                pe.wait_ge(w2_l, START + chunks * hf + c + 1)
                for j in range(OPS):
                    if q or j >= O_BANKS - 1:
                        pe.wait_ge(added, START + OPS * n + j - O_BANKS + 1)
                    rs, cs = slice(j // HALVES * P, (j // HALVES + 1) * P), slice(j % HALVES * 512, (j % HALVES + 1) * 512)
                    for f in range(FT):
                        for t, (a, b) in enumerate(split_passes(h_hi[q % 2][:, f, rs], h_lo[q % 2][:, f, rs],
                                                                w2_hi[cp][:, f, cs], w2_lo[cp][:, f, cs])):
                            last = nc.tensor.matmul(o_ps[j % O_BANKS][:], a, b, start=(f == 0 and t == 0), stop=(f == FT - 1 and t == 2))
                    last.then_inc(o_mm, 1)
                if q == 2 * TB - 1:
                    pe.wait_ge(added, START + OPS * (n + 1) - 1)

            def prologue(hf):
                for u in range(TT):
                    pe.wait_ge(normed, TT * hf + u + 1)
                    pe.wait_ge(x_lo, START + TT * hf + u)
                    for k in range(KT):
                        last = nc.tensor.transpose(turn[k * 2 // KT][:, k % (KT // 2), :], acc[:, u, k * P:(k + 1) * P], ident[:])
                    last.then_inc(turned, 1)
                pe.wait_ge(x_lo, START + TT * (hf + 1))
                first(hf, 0, 0, 0, 0)

            def step(hf, c, s, cp, q, more):
                if more or q < 2 * TB - 1:
                    nq = (q + 1) % (2 * TB)
                    first(hf, c + (q % TB == TB - 1), s + 1, nq // TB, nq)
                second(hf, c, s, cp, q)
            per_pass(pe, prologue, step, lambda hf: None)


def shape_constants(tokens):
    import numpy as np
    f32 = np.float32
    inv_freq = (f32(1.0) / f32(10000.0) ** (np.arange(0, HEAD, 2, dtype=f32) / f32(HEAD))).astype(f32)
    angles = (np.arange(tokens, dtype=f32)[None, :] * inv_freq[:, None]).astype(f32)
    cos, sin = np.cos(angles), np.sin(angles)
    lane = np.arange(P)
    rows = GROUP // 2
    head, row = lane // rows, lane % rows
    tiles = tokens // P
    earlier = head[:, None] < head[None, :]
    same = head[:, None] == head[None, :]
    return {
        "rope_cos": np.concatenate([cos] * 4),
        "rope_sin": np.concatenate([sin, -sin] * 2),
        "identity": np.eye(P, dtype=f32),
        "same_head": np.kron(np.eye(P // HEAD), np.ones((HEAD, HEAD))).astype(f32),
        "phase": np.tile(np.repeat(np.array([0.0, 0.25], f32), HEAD // 2), P // HEAD)[:, None],
        "own_token": np.kron(np.eye(GROUP), np.ones((KV_HEADS, 1))).astype(f32),
        "order_masks": np.stack([earlier, same, same & (row[:, None] < row[None, :]), np.ones((P, P), bool)], 1).astype(f32),
        "token_ids": (head[:, None] * (tokens // HEADS) + np.arange(tiles)[None, :] * rows + row[:, None]).astype(f32),
        "lane_ids": np.stack([lane, lane % 16], 1).astype(f32),
        "count_up": np.tile(np.arange(P, dtype=f32), (P, 1)),
    }


def feature_weights(R):
    import numpy as np
    e = R.shape[0]
    straight = R.T
    rotated = np.concatenate([straight[ROTARY_SHIFT:], straight[:ROTARY_SHIFT]])
    w = np.zeros((P, 6, P), R.dtype)
    for j in range(2):
        rows = slice(HEAD * j, HEAD * (j + 1))
        for part, m in enumerate((straight, rotated)):
            for c in range(2):
                w[rows, part, HEAD * j + e * c:HEAD * j + e * (c + 1)] = m
                for half in range(2):
                    at = HEAD * half + e * c
                    w[rows, 2 + 2 * j + part, at:at + e] = m
    return w


def build(nc, a, out):
    tokens, width = a["x"].shape
    qk_tiles = (HEADS + KV_HEADS) // 2
    keep = tokens // 2
    qk_scratch = nc.dram_tensor("qk_scratch", (tokens // TOK_BLOCK, qk_tiles, P, TOK_BLOCK), F32, kind="Internal").ap()
    v_scratch = nc.dram_tensor("v_scratch", (tokens, KV_HEADS * HEAD), F32, kind="Internal").ap()
    score_scratch = nc.dram_tensor("score_scratch", (P, tokens // P), F32, kind="Internal").ap()
    project_phase(nc, a["x"], a["w_qkv_t"], a["b_qk"], a["identity"], a["same_head"], qk_scratch, v_scratch)
    mix_phase(nc, a["x"], qk_scratch, v_scratch, a["rope_cos"], a["rope_sin"], a["features"], a["phase"], a["v_bias"],
              a["own_token"], a["w_o_t"], a["o_bias"], a["router"], a["router_bias"], out, score_scratch)
    with nc.sbuf_tensor("chosen", [P, keep // P], I32) as chosen:
        route_phase(nc, score_scratch, a["order_masks"], a["token_ids"], a["lane_ids"], a["count_up"], chosen, keep)
        ffn_phase(nc, out, a["w1"], a["b1"], a["w2"], a["b2_rows"], a["identity"], chosen, out, keep)


def kernel(**inputs):
    import numpy as np
    import concourse.bacc as bacc
    from concourse.bass_utils import run_bass_kernel_spmd

    g = {k: np.asarray(v) for k, v in inputs.items()}
    x = g["L0_attn_hidden_states"]
    arrays = {
        "x": x[0],
        "w_qkv_t": np.concatenate([g["L0_attn_Wq"], g["L0_attn_Wk"], g["L0_attn_Wv"]]).T,
        "b_qk": np.concatenate([g["L0_attn_bq"], g["L0_attn_bk"]]).reshape(-1, P).T,
        "v_bias": np.tile(g["L0_attn_bv"].reshape(KV_HEADS, HEAD), (GROUP, 1)),
        "features": feature_weights(g["L0_attn_rand_matrix"]),
        "w_o_t": g["L0_attn_Wo"].T,
        "o_bias": np.tile(g["L0_attn_bo"], (P, 1)),
        "router": np.tile(g["L0_ffn_w_r"], (P, 1)),
        "router_bias": np.tile(g["L0_ffn_b_r"].reshape(1, 1), (P, 1)),
        "w1": g["L0_ffn_w1"],
        "b1": g["L0_ffn_b1"].reshape(-1, P).T,
        "w2": g["L0_ffn_w2"],
        "b2_rows": np.tile(g["L0_ffn_b2"], (P, 1)),
    }
    arrays.update(shape_constants(x.shape[1]))
    arrays = {k: np.ascontiguousarray(v) for k, v in arrays.items()}

    nc = bacc.Bacc("TRN2", target_bir_lowering=False, num_devices=1)
    tensors = {k: nc.dram_tensor(f"in_{k}", v.shape, mybir.dt.from_np(v.dtype), kind="ExternalInput").ap() for k, v in arrays.items()}
    out = nc.dram_tensor("out_x", x.shape[1:], F32, kind="ExternalOutput").ap()
    build(nc, tensors, out)
    r = run_bass_kernel_spmd(nc, [{f"in_{k}": v for k, v in arrays.items()}], core_ids=[0])
    return r.results[0]["out_x"].reshape(x.shape)
```

```python
from contextlib import ExitStack

import concourse.bass as bass
from concourse import mybir

P = 128
F32 = mybir.dt.float32
F32R = mybir.dt.float32r
I32 = mybir.dt.int32
U32 = mybir.dt.uint32
ALU = mybir.AluOpType
ACT = mybir.ActivationFunctionType
AX_X = mybir.AxisListType.X

HEADS, KV_HEADS, HEAD = 16, 8, 64
LN_EPS = 1e-5
TOK_BLOCK = 512
TILES = TOK_BLOCK // P


START = 2


def alone(eng, sem):
    eng.sem_inc(sem, 1)


def split_passes(hi_a, lo_a, hi_b, lo_b):
    return ((hi_a, hi_b), (hi_a, lo_b), (lo_a, hi_b))


def project_phase(nc, x, w_qkv_t, b_qk, identity, same_head, qk_scratch, v_scratch):
    tokens, width = x.shape
    KT = width // P
    cols = w_qkv_t.shape[1]
    blocks = tokens // TOK_BLOCK
    qk_tiles = qk_scratch.shape[1]
    outs_per_block = qk_tiles + TILES
    QK_PER_CHUNK = qk_tiles // TILES
    CH = QK_PER_CHUNK + 1
    MM_BANKS = CH
    STAGES = QK_PER_CHUNK
    pieces = cols // TOK_BLOCK
    W_PER_TILE = KT // TILES
    assert pieces == STAGES + 1

    with ExitStack() as ctx:
        sb = lambda n, s, d: ctx.enter_context(nc.sbuf_tensor(n, s, d))
        sem = lambda n: ctx.enter_context(nc.semaphore(n))
        w_hi = sb("w_hi", [P, KT, cols], F32R)
        w_lo = sb("w_lo", [P, KT, cols], F32R)
        h_hi = [sb(f"h_hi{b}", [P, KT, TOK_BLOCK], F32R) for b in range(2)]
        h_lo = [sb(f"h_lo{b}", [P, KT, TOK_BLOCK], F32R) for b in range(2)]
        xt = sb("xt", [P, width], F32)
        stage = [sb(f"stage{b}", [P, TOK_BLOCK], F32) for b in range(STAGES)]
        squares = [sb(f"squares{b}", [P, TOK_BLOCK], F32) for b in range(2)]
        piece_in = stage + squares[:1]
        ident = sb("ident", [P, P], F32)
        ones = sb("ones", [P, P], F32)
        bias = sb("bias", [P, qk_tiles], F32)
        stats = sb("stats", [P, 2, 6], F32)
        moments = [sb(f"moments{b}", [P, 2], F32) for b in range(2)]
        var_eps = sb("var_eps", [P, 1], F32)
        rstd = [sb(f"rstd{b}", [P, 1], F32) for b in range(2)]
        neg_half = sb("neg_half", [P, 1], F32)
        mm = [ctx.enter_context(nc.psum_tensor(f"mm{b}", [P, TOK_BLOCK], F32)) for b in range(MM_BANKS)]
        turn = [ctx.enter_context(nc.psum_tensor(f"turn{b}", [P, KT // 2, P], F32)) for b in range(2)]
        norm_ps = ctx.enter_context(nc.psum_tensor("norm_ps", [P, TOK_BLOCK], F32))

        consts_in = sem("p_consts_in")
        parted = {e: sem(f"p_parted_{e}") for e in ("pool", "dve")}
        w_in = [sem(f"p_w_in{b}") for b in range(pieces)]
        w_hi_done = sem("p_w_hi_done")
        w_split = sem("p_w_split")
        x_in = sem("p_x_in")
        stat_step = sem("p_stat_step")
        rstd_step = sem("p_rstd_step")
        normed = sem("p_normed")
        turned = sem("p_turned")
        hi_done = sem("p_hi_done")
        lo_done = sem("p_lo_done")
        mm_done = sem("p_mm_done")
        evac = sem("p_evac")
        norm_done = sem("p_norm_done")
        root_done = sem("p_root_done")
        recip_done = sem("p_recip_done")
        scaled = sem("p_scaled")
        stored = [sem(f"p_stored{b}") for b in range(STAGES)]

        block = ctx.enter_context(nc.Block())

        def per_block(eng, chunk):
            with eng.Fori(0, blocks // 2 - 1) as i:
                for b in range(2):
                    for t in range(TILES):
                        chunk(2 * i + b, b, t, True, False)
            for b in range(2):
                for t in range(TILES):
                    chunk(blocks - 2 + b, b, t, b == 0, True)

        def piece(k, q):
            return (slice(None), bass.ds(k, 1), slice(q * TOK_BLOCK, (q + 1) * TOK_BLOCK))

        @block.sync
        def _(sp):
            for s in stored:
                sp.sem_inc(s, START)
            sp.dma_start(ident[:], identity).then_inc(consts_in, 16)
            sp.dma_start(xt[:], x[0:P, :]).then_inc(x_in, 16)
            sp.dma_start(ones[:], same_head).then_inc(consts_in, 16)
            sp.dma_start(bias[:], b_qk).then_inc(consts_in, 16)

            def load_w(k, q):
                sp.dma_start(piece_in[q][:], w_qkv_t[bass.ts(k, P), q * TOK_BLOCK:(q + 1) * TOK_BLOCK]).then_inc(w_in[q], 16)

            def load_x(n):
                sp.wait_ge(turned, n)
                sp.dma_start(xt[:], x[bass.ts(n, P), :]).then_inc(x_in, 16)

            for q in range(pieces):
                load_w(0, q)
            for t in range(TILES):
                with sp.Fori(max(1, t * W_PER_TILE), (t + 1) * W_PER_TILE) as k:
                    for q in range(pieces):
                        sp.wait_ge(w_split, pieces * (k - 1) + q + 1)
                        load_w(k, q)
                load_x(t + 1)

            def chunk(blk, par, t, more, peeled):
                for jj in range(CH):
                    out = blk * outs_per_block + t * CH + jj
                    if jj < QK_PER_CHUNK:
                        m = t * QK_PER_CHUNK + jj
                        sp.wait_ge(scaled, START + blk * qk_tiles + m + 1)
                        sp.dma_start(qk_scratch[blk, m], stage[jj][:]).then_inc(stored[jj], 16)
                        if jj == 0 and more and not (peeled and t == TILES - 1):
                            load_x((blk + 1) * TILES + t + 1)
                    else:
                        sp.wait_ge(evac, START + out + 1)
                        sp.dma_start(v_scratch[bass.ts(blk * TILES + t, P), :], stage[0][:]).then_inc(stored[0], 16)
            per_block(sp, chunk)
            for b in range(STAGES):
                sp.wait_ge(stored[b], START + 16 * blocks * TILES * (2 if b == 0 else 1))

        @block.gpsimd
        def _(pool):
            nc.gpsimd.memset(neg_half[:], -0.5).then_inc(rstd_step, 1)

            def rstd_of(n, b):
                pool.wait_ge(stat_step, 3 * n + 3)
                pool.wait_ge(rstd_step, 2 * n + 1)
                alone(pool, parted["pool"])
                nc.gpsimd.tensor_scalar(var_eps[:], moments[b][:, 1:2], LN_EPS, None, ALU.add).then_inc(rstd_step, 1)
                pool.wait_ge(rstd_step, 2 * n + 2)
                nc.gpsimd.tensor_tensor(rstd[b][:], var_eps[:], neg_half[:], ALU.pow).then_inc(rstd_step, 1)

            for t in range(TILES):
                rstd_of(t, t % 2)

            def chunk(blk, par, t, more, peeled):
                if more:
                    rstd_of((blk + 1) * TILES + t, t % 2)
            per_block(pool, chunk)

        @block.vector
        def _(dve):
            dve.sem_inc(scaled, START)
            def split_weights(k, q):
                dve.wait_ge(w_hi_done, pieces * k + q + 1)
                nc.vector.tensor_tensor(w_lo[piece(k, q)].rearrange("p a n -> p (a n)"), piece_in[q][:],
                                        w_hi[piece(k, q)].rearrange("p a n -> p (a n)").bitcast(F32),
                                        ALU.subtract).then_inc(w_split, 1)

            def norm(n, b):
                dve.wait_ge(x_in, 16 * n + 16)
                dve.wait_ge(stat_step, 3 * n)
                for c in range(2):
                    nc.vector.bn_stats(stats[:, c, :], xt[:, c * 512:(c + 1) * 512]).then_inc(stat_step, 1)
                dve.wait_ge(stat_step, 3 * n + 2)
                alone(dve, parted["dve"])
                nc.vector.bn_aggr(moments[b][:], stats[:]).then_inc(stat_step, 1)
                dve.wait_ge(rstd_step, 2 * n + 3)
                dve.wait_ge(stat_step, 3 * n + 3)
                nc.vector.tensor_scalar(xt[:], xt[:], moments[b][:, 0:1], rstd[b][:], ALU.subtract,
                                        ALU.mult).then_inc(normed, 1)

            def low(n, par, t):
                dve.wait_ge(hi_done, n + 1)
                for c in range(2):
                    at = (slice(None), slice(c * KT // 2, (c + 1) * KT // 2), slice(t * P, (t + 1) * P))
                    last = nc.vector.tensor_tensor(h_lo[par][at], turn[c][:], h_hi[par][at].bitcast(F32), ALU.subtract)
                last.then_inc(lo_done, 1)

            for t in range(TILES):
                norm(t, t % 2)
                with dve.Fori(t * W_PER_TILE, (t + 1) * W_PER_TILE) as k:
                    for q in range(pieces):
                        split_weights(k, q)
                low(t, 0, t)

            def chunk(blk, par, t, more, peeled):
                n = (blk + 1) * TILES + t
                if more:
                    norm(n, t % 2)
                for jj in range(QK_PER_CHUNK):
                    m = t * QK_PER_CHUNK + jj
                    sq = squares[m % 2]
                    dve.wait_ge(root_done, START + blk * qk_tiles + m + 1)
                    nc.vector.reciprocal(sq[:], sq[:]).then_inc(recip_done, 1)
                    dve.wait_ge(recip_done, blk * qk_tiles + m + 1)
                    nc.vector.scalar_tensor_tensor(out=stage[jj][:], in0=sq[:], scalar=1e6, in1=stage[jj][:],
                                                   op0=ALU.min, op1=ALU.mult).then_inc(scaled, 1)
                    if more and jj == 0:
                        low(n, 1 - par, t)
            per_block(dve, chunk)

        @block.scalar
        def _(act):
            act.sem_inc(evac, START)
            act.sem_inc(root_done, START)
            act.wait_ge(consts_in, 48)

            def high(n, par, t):
                act.wait_ge(turned, n + 1)
                for c in range(2):
                    at = (slice(None), slice(c * KT // 2, (c + 1) * KT // 2), slice(t * P, (t + 1) * P))
                    last = nc.scalar.activation(h_hi[par][at], turn[c][:], ACT.Copy)
                last.then_inc(hi_done, 1)

            for t in range(TILES):
                with act.Fori(t * W_PER_TILE, (t + 1) * W_PER_TILE) as k:
                    for q in range(pieces):
                        act.wait_ge(w_in[q], 16 * k + 16)
                        nc.scalar.activation(w_hi[piece(k, q)].rearrange("p a n -> p (a n)"), piece_in[q][:],
                                             ACT.Copy).then_inc(w_hi_done, 1)
                high(t, 0, t)

            def chunk(blk, par, t, more, peeled):
                for jj in range(CH):
                    out = blk * outs_per_block + t * CH + jj
                    b = jj % STAGES
                    act.wait_ge(mm_done, out + 1)
                    earlier = 2 * (blk * TILES + t) + jj // STAGES if b == 0 else blk * TILES + t
                    act.wait_ge(stored[b], START + 16 * earlier)
                    if jj < QK_PER_CHUNK:
                        m = t * QK_PER_CHUNK + jj
                        nc.scalar.activation(stage[b][:], mm[jj][:], ACT.Identity, bias=bias[:, m:m + 1])
                        act.wait_ge(scaled, START + blk * qk_tiles + m - 1)
                        nc.scalar.activation(squares[m % 2][:], mm[jj][:], ACT.Square, bias=bias[:, m:m + 1]).then_inc(evac, 1)
                        if jj == 1 and more:
                            high((blk + 1) * TILES + t, 1 - par, t)
                        act.wait_ge(norm_done, blk * qk_tiles + m + 1)
                        nc.scalar.activation(squares[m % 2][:], norm_ps[:], ACT.Sqrt).then_inc(root_done, 1)
                    else:
                        nc.scalar.activation(stage[b][:], mm[jj][:], ACT.Copy).then_inc(evac, 1)
            per_block(act, chunk)

        @block.tensor
        def _(pe):
            pe.wait_ge(consts_in, 48)

            def transposes(n):
                pe.wait_ge(normed, n + 1)
                pe.wait_ge(lo_done, n)
                for k in range(KT):
                    last = nc.tensor.transpose(turn[k * 2 // KT][:, k % (KT // 2), :], xt[:, k * P:(k + 1) * P], ident[:])
                last.then_inc(turned, 1)

            for t in range(TILES):
                transposes(t)
            pe.wait_ge(w_split, pieces * KT)

            def norms(blk, out, m):
                pe.wait_ge(evac, START + out + 1)
                pe.wait_ge(root_done, START + blk * qk_tiles + m)
                nc.tensor.matmul(norm_ps[:], ones[:], squares[m % 2][:], start=True, stop=True).then_inc(norm_done, 1)

            def chunk(blk, par, t, more, peeled):
                if t == 0:
                    pe.wait_ge(lo_done, (blk + 1) * TILES)
                for jj in range(CH):
                    out = blk * outs_per_block + t * CH + jj
                    bank = mm[jj]
                    if t or jj == MM_BANKS - 1:
                        pe.wait_ge(evac, START + out - MM_BANKS + 1)
                    hh, hl = h_hi[par], h_lo[par]
                    for k in range(KT):
                        if jj < QK_PER_CHUNK:
                            c = slice((t * QK_PER_CHUNK + jj) * P, (t * QK_PER_CHUNK + jj + 1) * P)
                            terms = split_passes(w_hi[:, k, c], w_lo[:, k, c], hh[:, k, :], hl[:, k, :])
                        else:
                            c = slice(t * P, (t + 1) * P)
                            terms = split_passes(hh[:, k, c], hl[:, k, c], w_hi[:, k, qk_tiles * P:], w_lo[:, k, qk_tiles * P:])
                        for s, (a, b) in enumerate(terms):
                            last = nc.tensor.matmul(bank[:], a, b, start=(k == 0 and s == 0), stop=(k == KT - 1 and s == 2))
                    last.then_inc(mm_done, 1)
                    if jj:
                        norms(blk, out - 1, t * QK_PER_CHUNK + jj - 1)
                    if jj == 1 and more:
                        transposes((blk + 1) * TILES + t)
                if more and t == TILES - 1:
                    pe.wait_ge(evac, START + (blk + 1) * outs_per_block - 1)
            per_block(pe, chunk)


ROUND = 1.5 * 2.0 ** 23
TWO_PI = 6.2831850
GROUP = P // KV_HEADS
ROTARY_SHIFT = HEAD // 2


def mix_phase(nc, x, qk_scratch, v_scratch, cos_t, sin_t, features, phase, v_bias, own_token, w_o_t, o_bias,
              bias_signs, router, router_bias, out, score_out):
    tokens, width = x.shape
    blocks = tokens // TOK_BLOCK
    KT = width // P
    q_tiles = HEADS // 2
    k_tiles = KV_HEADS // 2
    rot_tiles = q_tiles + k_tiles
    UNITS = KV_HEADS + q_tiles
    SUPER = 4 * GROUP
    SUPERS = TOK_BLOCK // SUPER
    SPT = SUPERS // TILES
    QK_RING = 3
    GROUPS = TOK_BLOCK // GROUP
    V_PIECES = 4
    HALVES = width // 512
    feature_scale = 2.0 / HEAD
    HEAD_START = 2 * HALVES
    UNITS_UP_TO = (0, 1, 4, 7, 10, 12, 14, 16, 16)
    assert UNITS_UP_TO[-1] == UNITS and len(UNITS_UP_TO) == HALVES * TILES + 1

    with ExitStack() as ctx:
        sb = lambda n, s, d=F32: ctx.enter_context(nc.sbuf_tensor(n, s, d))
        ps = lambda n, s: ctx.enter_context(nc.psum_tensor(n, s, F32))
        sem = lambda n: ctx.enter_context(nc.semaphore("m_" + n))
        wo_hi = sb("wo_hi", [P, KT, width], F32R)
        wo_lo = sb("wo_lo", [P, KT, width], F32R)
        qf = sb("qf", [P, q_tiles, TOK_BLOCK])
        kf = sb("kf", [P, TOK_BLOCK, KV_HEADS])
        ctx_hi = [sb(f"ctx_hi{t}", [P, P, GROUP // 2], F32R) for t in range(TILES)]
        ctx_lo = [sb(f"ctx_lo{t}", [P, P, GROUP // 2], F32R) for t in range(TILES)]
        att = [sb(f"att{b}", [P, 2, GROUP // 2, 4, HEADS]) for b in range(2)]
        qk_in = [sb(f"qk_in{b}", [P, TOK_BLOCK]) for b in range(QK_RING)]
        qk_swap = [sb(f"qk_swap{b}", [P, TOK_BLOCK]) for b in range(QK_RING)]
        q_cos = [sb(f"q_cos{b}", [P, TOK_BLOCK]) for b in range(2)]
        rotated = [sb(f"rotated{b}", [P, TOK_BLOCK]) for b in range(2)]
        turns = [sb(f"turns{b}", [P, TOK_BLOCK]) for b in range(2)]
        whole = sb("whole", [P, TOK_BLOCK])
        cs = sb("cs", [P, 2, TOK_BLOCK])
        vg = sb("vg", [P, GROUPS, HEAD])
        vb = sb("vb", [P, HEAD])
        xr = [sb(f"xr{b}", [P, width]) for b in range(2)]
        y = [sb(f"y{b}", [P, width]) for b in range(2)]
        wr = sb("wr", [P, width])
        feat_w = sb("feat_w", [P, 3, P])
        phases = sb("phases", [P, 1])
        own = sb("own", [P, GROUP])
        br = sb("br", [P, 1])
        signs = sb("signs", [2, 1 + P])
        ones_r = sb("ones_r", [2, P], F32R)
        bias_hi = sb("bias_hi", [2, width], F32R)
        bias_r = sb("bias_r", [2, width], F32R)
        raw = sb("raw", [P, TILES])
        raws = sb("raws", [P, blocks * TILES])
        variances = sb("variances", [P, blocks * TILES])
        scores = sb("scores", [P, blocks * TILES])
        stats1 = sb("m_stats1", [P, HALVES, 6])
        stats2 = sb("m_stats2", [P, HALVES, 6])
        moments1 = sb("m_moments1", [P, 2])
        moments2 = sb("m_moments2", [P, TILES, 2])
        var_eps = sb("m_var_eps", [P, 1])
        rstd = sb("m_rstd", [P, 1])
        shift = sb("m_shift", [P, 1])
        neg_half = sb("m_neg_half", [P, blocks * TILES])
        pair_ps = [ps(f"pair_ps{b}", [P, 512]) for b in range(2)]
        att_ps = [[ps(f"att_ps{b}{r}", [P, 4 * P]) for r in range(2)] for b in range(2)]
        own_ps = [ps(f"y_ps{h}", [P, 512]) for h in range(HALVES)]
        y_ps = [att_ps[1], own_ps]

        consts_in = sem("consts_in")
        parted = {e: sem(f"parted_{e}") for e in ("pool", "dve", "sp", "act")}
        signs_done = sem("signs_done")
        bias_done = sem("bias_done")
        w_in = [sem(f"w_in{b}") for b in range(2)]
        w_hi_done = sem("w_hi_done")
        w_split = sem("w_split")
        cs_in = sem("cs_in")
        qk_loaded = [sem(f"qk_loaded{b}") for b in range(QK_RING)]
        v_in = sem("v_in")
        v_ready = sem("v_ready")
        cos_done = sem("cos_done")
        sin_done = sem("sin_done")
        rot_done = sem("rot_done")
        p_done = sem("p_done")
        turn_done = sem("turn_done")
        whole_done = sem("whole_done")
        frac_done = sem("frac_done")
        feat_done = sem("feat_done")
        att_done = sem("att_done")
        masked = sem("masked")
        ctx_done = sem("ctx_done")
        ctx_hi_done = sem("ctx_hi_done")
        ctx_lo_done = sem("ctx_lo_done")
        y_done = sem("y_done")
        stat1 = sem("stat1")
        rstd_step = sem("rstd_step")
        y_normed = sem("y_normed")
        x_loaded = [sem(f"x_loaded{b}") for b in range(2)]
        x1_done = sem("x1_done")
        stat2 = sem("stat2")
        scored = sem("scored")
        kept = sem("kept")
        x1_stored = [sem(f"x1_stored{b}") for b in range(2)]
        score_step = sem("score_step")
        score_stored = sem("score_stored")

        v_rows = v_scratch.rearrange("t (g d) -> (t g) d", d=HEAD).rearrange("(b s n p) d -> b s p n d", p=P, s=V_PIECES,
                                                                             n=GROUPS // V_PIECES)
        x_rows = x.rearrange("(h n g) d -> n h g d", h=HEADS, g=GROUP // 2)
        out_rows = out.rearrange("(h n g) d -> n h g d", h=HEADS, g=GROUP // 2)

        block = ctx.enter_context(nc.Block())

        def rotated_of(u):
            return u // 2 if u < KV_HEADS else u - k_tiles

        def first_unit(m):
            return 2 * m if m < k_tiles else m + k_tiles

        def readers_before(m):
            return first_unit(m - 1) if m >= 1 else first_unit(rot_tiles - 1) - UNITS

        def units_of(j):
            return range(UNITS_UP_TO[j], UNITS_UP_TO[j + 1])

        def rotations_for(u):
            if u == 0:
                return (0, 1)
            return (rotated_of(u) + 1,) if rotated_of(u) != rotated_of(u - 1) and rotated_of(u) + 1 < rot_tiles else ()

        @block.sync
        def _(sp):
            def load_cs(blk):
                for j, table in enumerate((cos_t, sin_t)):
                    sp.dma_start(cs[:, j, :], table[:, bass.ts(blk, TOK_BLOCK)]).then_inc(cs_in, 16)

            def load_qk(blk, m):
                b = m % QK_RING
                tile = qk_scratch[blk, m + q_tiles if m < k_tiles else m - k_tiles]
                sp.dma_start(qk_in[b][:], tile).then_inc(qk_loaded[b], 16)
                for head in range(2):
                    halves = tile[head * HEAD:(head + 1) * HEAD].rearrange("(s p) n -> s p n", s=2)
                    for s in range(2):
                        at = head * HEAD + (1 - s) * ROTARY_SHIFT
                        sp.dma_start(qk_swap[b][at:at + ROTARY_SHIFT, :], halves[s]).then_inc(qk_loaded[b], 16)

            def load_v(blk):
                for s in range(V_PIECES):
                    n = GROUPS // V_PIECES
                    sp.dma_start(vg[:, s * n:(s + 1) * n, :], v_rows[blk, s]).then_inc(v_in, 16)

            def load_x(n, b):
                sp.dma_start(xr[b][:], x_rows[n]).then_inc(x_loaded[b], 16)

            def reload_qk(blk, m):
                sp.wait_ge(rot_done, rot_tiles * blk + m - QK_RING + 1)
                alone(sp, parted["sp"])
                load_qk(blk, m)

            def store_x1(blk, t):
                sp.wait_ge(x1_done, blk * TILES + t + 1)
                sp.dma_start(out_rows[blk * TILES + t], xr[t % 2][:]).then_inc(x1_stored[t % 2], 16)

            def next_x(blk, t):
                sp.wait_ge(x1_stored[t % 2], 16 * (blk * 2 + t // 2 + 1))
                alone(sp, parted["sp"])
                sp.wait_ge(scored, START + blk * TILES + t + 1)
                load_x(blk * TILES + t + 2, t % 2)

            def first_tiles(blk):
                sp.wait_ge(rot_done, rot_tiles * blk)
                alone(sp, parted["sp"])
                load_cs(blk)
                for m in range(QK_RING):
                    load_qk(blk, m)

            for dst, src in ((feat_w, features), (phases, phase)):
                sp.dma_start(dst[:], src).then_inc(consts_in, 16)
            load_cs(0)
            load_qk(0, 0)
            load_qk(0, 1)
            for dst, src in ((vb, v_bias), (own, own_token), (signs, bias_signs), (wr, router), (br, router_bias)):
                sp.dma_start(dst[:], src).then_inc(consts_in, 16)
            load_qk(0, 2)
            for m in range(QK_RING, rot_tiles):
                reload_qk(0, m)
                if m == QK_RING + 1:
                    for k in range(2):
                        sp.dma_start(xr[k][:], w_o_t[k * P:(k + 1) * P, :]).then_inc(w_in[k], 16)
                    sp.dma_start(y[0][0:2, :], o_bias).then_inc(consts_in, 16)
                if m == QK_RING + 2:
                    load_v(0)
            first_tiles(1)
            for k in range(2, KT):
                sp.wait_ge(w_split, k - 1)
                sp.dma_start(xr[k % 2][:], w_o_t[k * P:(k + 1) * P, :]).then_inc(w_in[k % 2], 16)
            for b in range(2):
                sp.wait_ge(w_split, KT - 1 + b)
                load_x(b, b)

            def chunk(blk, more, ahead):
                if more:
                    sp.wait_ge(ctx_done, SUPERS * (blk + 1))
                    alone(sp, parted["sp"])
                    load_v(blk + 1)
                for j in range(HALVES * TILES):
                    t = j // HALVES
                    if more:
                        for m in range(QK_RING, rot_tiles):
                            if first_unit(max(m - QK_RING - 1, 0)) in units_of(j):
                                reload_qk(blk + 1, m)
                    if t and j % HALVES == 0:
                        store_x1(blk, t - 1)
                    if t and j % HALVES == HALVES - 1 and (more or t - 1 < TILES - 2):
                        next_x(blk, t - 1)
                if ahead:
                    first_tiles(blk + 2)
                store_x1(blk, TILES - 1)
                if more:
                    next_x(blk, TILES - 1)
            with sp.Fori(0, blocks - 2) as i:
                chunk(i, True, True)
            chunk(blocks - 2, True, False)
            chunk(blocks - 1, False, False)
            sp.wait_ge(score_step, 4)
            sp.dma_start(score_out, scores[:]).then_inc(score_stored, 16)
            for b in range(2):
                sp.wait_ge(x1_stored[b], 16 * blocks * TILES // 2)
            sp.wait_ge(score_stored, 16)

        @block.gpsimd
        def _(pool):
            nc.gpsimd.memset(neg_half[:], -0.5).then_inc(rstd_step, 1)

            def scale_of(n):
                pool.wait_ge(stat1, START + 3 * n + 3)
                pool.wait_ge(rstd_step, 3 * n + 1)
                alone(pool, parted["pool"])
                nc.gpsimd.tensor_scalar(var_eps[:], moments1[:, 1:2], LN_EPS, None, ALU.add).then_inc(rstd_step, 1)
                pool.wait_ge(rstd_step, 3 * n + 2)
                pool.wait_ge(y_normed, HEAD_START + HALVES * n)
                alone(pool, parted["pool"])
                nc.gpsimd.tensor_tensor(rstd[:], var_eps[:], neg_half[:, 0:1], ALU.pow).then_inc(rstd_step, 1)
                pool.wait_ge(rstd_step, 3 * n + 3)
                alone(pool, parted["pool"])
                nc.gpsimd.tensor_scalar(shift[:], moments1[:, 0:1], rstd[:], -1.0, ALU.mult, ALU.mult).then_inc(rstd_step, 1)

            def rotate(blk, m):
                pool.wait_ge(qk_loaded[m % QK_RING], 80 * (blk * (rot_tiles // QK_RING) + m // QK_RING + 1))
                if m == 0:
                    pool.wait_ge(cs_in, 32 * (blk + 1))
                    alone(pool, parted["pool"])
                swap = qk_swap[m % QK_RING]
                nc.gpsimd.tensor_tensor(swap[:], swap[:], cs[:, 1, :], ALU.mult).then_inc(sin_done, 1)
                for s in (sin_done, cos_done):
                    pool.wait_ge(s, rot_tiles * blk + m + 1)
                if m >= 2 or not (isinstance(blk, int) and blk == 0):
                    pool.wait_ge(p_done, UNITS * blk + readers_before(m))
                nc.gpsimd.tensor_tensor(rotated[m % 2][:], q_cos[m % 2][:], swap[:], ALU.add).then_inc(rot_done, 1)

            def add_v_bias(blk):
                pool.wait_ge(v_in, 16 * V_PIECES * (blk + 1))
                nc.gpsimd.tensor_tensor(vg[:], vg[:], vb[:].unsqueeze(1).to_broadcast([P, GROUPS, HEAD]),
                                        ALU.add).then_inc(v_ready, 1)

            def residual(blk, t):
                b = t % 2
                pool.wait_ge(y_normed, HEAD_START + HALVES * (blk * TILES + t + 1))
                pool.wait_ge(x_loaded[b], 16 * (blk * 2 + t // 2 + 1))
                nc.gpsimd.tensor_tensor(xr[b][:], xr[b][:], y[b][:], ALU.add).then_inc(x1_done, 1)

            for u in range(UNITS):
                for m in rotations_for(u):
                    rotate(0, m)
            pool.wait_ge(consts_in, 16 * 8)
            add_v_bias(0)

            def chunk(blk, more):
                for j in range(HALVES * TILES):
                    t = j // HALVES
                    if more:
                        for u in units_of(j):
                            for m in rotations_for(u):
                                rotate(blk + 1, m)
                    if t and j % HALVES == 0:
                        residual(blk, t - 1)
                    if j % HALVES == HALVES - 1:
                        if more and t == TILES - 1:
                            add_v_bias(blk + 1)
                        scale_of(blk * TILES + t)
                residual(blk, TILES - 1)
            with pool.Fori(0, blocks - 1) as i:
                chunk(i, True)
            chunk(blocks - 1, False)
            pool.wait_ge(kept, 2 * blocks)
            nc.gpsimd.tensor_scalar(variances[:], variances[:], LN_EPS, None, ALU.add).then_inc(score_step, 1)
            pool.wait_ge(score_step, 1)
            nc.gpsimd.tensor_tensor(variances[:], variances[:], neg_half[:], ALU.pow).then_inc(score_step, 1)

        @block.vector
        def _(dve):
            dve.sem_inc(ctx_lo_done, START)
            dve.sem_inc(stat1, START)
            dve.sem_inc(stat2, START)
            dve.sem_inc(scored, START)

            def cosine(blk, m):
                dve.wait_ge(qk_loaded[m % QK_RING], 80 * (blk * (rot_tiles // QK_RING) + m // QK_RING + 1))
                if m == 0:
                    dve.wait_ge(cs_in, 32 * (blk + 1))
                if m >= 2 or not (isinstance(blk, int) and blk == 0):
                    dve.wait_ge(rot_done, rot_tiles * blk + m - 1)
                    alone(dve, parted["dve"])
                nc.vector.tensor_tensor(q_cos[m % 2][:], qk_in[m % QK_RING][:], cs[:, 0, :], ALU.mult).then_inc(cos_done, 1)

            def fraction(blk, u):
                e = UNITS * blk + u
                dve.wait_ge(turn_done, e + 1)
                dve.wait_ge(frac_done, e)
                nc.vector.tensor_scalar(whole[:], turns[u % 2][:], ROUND, ROUND, ALU.add, ALU.subtract).then_inc(whole_done, 1)
                dve.wait_ge(whole_done, e + 1)
                nc.vector.tensor_tensor(turns[u % 2][:], turns[u % 2][:], whole[:], ALU.subtract).then_inc(frac_done, 1)

            def units(blk, which):
                for u in which:
                    for m in rotations_for(u):
                        cosine(blk, m)
                    fraction(blk, u)

            def y_stats(n, t, h):
                dve.wait_ge(y_done, HALVES * n + h + 1)
                dve.wait_ge(stat1, START + 3 * n)
                nc.vector.bn_stats(stats1[:, h, :], y_ps[t % 2][h][:]).then_inc(stat1, 1)
                if h == HALVES - 1:
                    dve.wait_ge(stat1, START + 3 * n + 2)
                    dve.wait_ge(rstd_step, 3 * n + 1)
                    alone(dve, parted["dve"])
                    nc.vector.bn_aggr(moments1[:], stats1[:]).then_inc(stat1, 1)

            def router(blk, t):
                n = blk * TILES + t
                dve.wait_ge(x1_done, n + 1)
                dve.wait_ge(stat2, START + 3 * n)
                alone(dve, parted["dve"])
                for c in range(HALVES):
                    nc.vector.bn_stats(stats2[:, c, :], xr[t % 2][:, c * 512:(c + 1) * 512]).then_inc(stat2, 1)
                dve.wait_ge(stat2, START + 3 * n + 2)
                alone(dve, parted["dve"])
                nc.vector.bn_aggr(moments2[:, t, :], stats2[:]).then_inc(stat2, 1)
                dve.wait_ge(stat2, START + 3 * n + 3)
                nc.vector.scalar_tensor_tensor(out=y[t % 2][:], in0=xr[t % 2][:], scalar=moments2[:, t, 0:1], in1=wr[:],
                                               op0=ALU.subtract, op1=ALU.mult, accum_out=raw[:, t:t + 1]).then_inc(scored, 1)

            def keep(blk):
                dve.wait_ge(scored, START + TILES * (blk + 1))
                nc.vector.tensor_copy(raws[:, bass.ds(blk * TILES, TILES)], raw[:]).then_inc(kept, 1)
                nc.vector.tensor_copy(variances[:, bass.ds(blk * TILES, TILES)], moments2[:, :, 1]).then_inc(kept, 1)

            def mask(blk, s):
                e = SUPERS * blk + s
                dve.wait_ge(att_done, e + 1)
                if s >= 2:
                    dve.wait_ge(ctx_done, e - 1)
                for r in range(2):
                    src = att_ps[s % 2][r][:].rearrange("p (gh t a) -> p gh t a", t=GROUP // 2, a=2)
                    dst = att[s % 2][:, :, :, :, r::2].rearrange("p a t g h -> p (g h) t a")
                    mine = own[:].rearrange("p (t a) -> p t a", a=2).unsqueeze(1).to_broadcast([P, 4 * q_tiles, GROUP // 2, 2])
                    last = nc.vector.tensor_tensor(dst, src, mine, ALU.mult)
                last.then_inc(masked, 1)

            def low(blk, s):
                e = SUPERS * blk + s
                dve.wait_ge(ctx_hi_done, e + 1)
                at = (slice(None), slice(None), slice(4 * (s % SPT), 4 * (s % SPT) + 4))
                nc.vector.scalar_tensor_tensor(out=ctx_lo[s // SPT][at], in0=pair_ps[s % 2][:].rearrange("p (g c) -> p c g", g=4),
                                               scalar=feature_scale, in1=ctx_hi[s // SPT][at].bitcast(F32),
                                               op0=ALU.mult, op1=ALU.subtract).then_inc(ctx_lo_done, 1)

            def attention(blk, between):
                mask(blk, 0)
                for s in range(SUPERS):
                    if s + 1 < SUPERS:
                        mask(blk, s + 1)
                    low(blk, s)
                    between(s)

            def split_wo(k):
                dve.wait_ge(w_hi_done, k + 1)
                nc.vector.tensor_tensor(wo_lo[:, k, :], xr[k % 2][:], wo_hi[:, k, :].bitcast(F32), ALU.subtract).then_inc(w_split, 1)

            units(0, range(UNITS))
            dve.wait_ge(signs_done, 2)
            nc.vector.scalar_tensor_tensor(out=bias_r[:], in0=y[0][0:2, :], scalar=signs[:, 0:1], in1=bias_hi[:].bitcast(F32),
                                           op0=ALU.mult, op1=ALU.subtract).then_inc(bias_done, 1)
            assert KT == SUPERS
            attention(0, split_wo)

            def wo_tiles(blk, more):
                for j in range(HALVES * TILES):
                    t = j // HALVES
                    if more:
                        units(blk + 1, units_of(j))
                    if t and j % HALVES == HALVES - 1:
                        router(blk, t - 1)
                    y_stats(blk * TILES + t, t, j % HALVES)

            with dve.Fori(0, blocks - 1) as i:
                def last_router(s):
                    if s == 3:
                        router(i, TILES - 1)
                        keep(i)
                wo_tiles(i, True)
                attention(i + 1, last_router)
            wo_tiles(blocks - 1, False)
            router(blocks - 1, TILES - 1)
            keep(blocks - 1)
            dve.wait_ge(score_step, 2)
            dve.wait_ge(kept, 2 * blocks)
            nc.vector.tensor_tensor(scores[:], raws[:], variances[:], ALU.mult).then_inc(score_step, 1)
            dve.wait_ge(score_step, 3)
            nc.vector.tensor_scalar(scores[:], scores[:], br[:], None, ALU.add).then_inc(score_step, 1)

        @block.scalar
        def _(act):
            act.sem_inc(y_normed, HEAD_START)
            act.wait_ge(consts_in, 16 * 8)

            def sine(blk, u):
                act.wait_ge(frac_done, UNITS * blk + u + 1)
                dst = kf[:, :, u] if u < KV_HEADS else qf[:, u - KV_HEADS, :]
                nc.scalar.activation(dst, turns[u % 2][:], ACT.Sin, scale=TWO_PI).then_inc(feat_done, 1)

            def unit(blk, u):
                act.wait_ge(p_done, UNITS * blk + u + 1)
                if u >= 2:
                    act.wait_ge(feat_done, UNITS * blk + u - 1)
                nc.scalar.activation(turns[u % 2][:], pair_ps[u % 2][:], ACT.Identity, bias=phases[:],
                                     scale=0.15915494309189535).then_inc(turn_done, 1)
                if u:
                    sine(blk, u - 1)
                if u == UNITS - 1:
                    sine(blk, u)

            def normalise(blk, t):
                n = blk * TILES + t
                act.wait_ge(rstd_step, 3 * n + 4)
                act.wait_ge(scored, START + n - 1)
                alone(act, parted["act"])
                for h in range(HALVES):
                    nc.scalar.activation(y[t % 2][:, h * 512:(h + 1) * 512], y_ps[t % 2][h][:], ACT.Identity, bias=shift[:],
                                         scale=rstd[:]).then_inc(y_normed, 1)

            def attention(blk, after):
                for s in range(SUPERS):
                    e = SUPERS * blk + s
                    act.wait_ge(ctx_done, e + 1)
                    nc.scalar.activation(ctx_hi[s // SPT][:, :, 4 * (s % SPT):4 * (s % SPT) + 4],
                                         pair_ps[s % 2][:].rearrange("p (g c) -> p c g", g=4), ACT.Copy,
                                         scale=feature_scale).then_inc(ctx_hi_done, 1)
                    after(s)

            def split_wo(k):
                act.wait_ge(w_in[k % 2], 16 * (k // 2) + 16)
                nc.scalar.activation(wo_hi[:, k, :], xr[k % 2][:], ACT.Copy).then_inc(w_hi_done, 1)

            nc.scalar.activation(ones_r[:], signs[:, 1:1 + P], ACT.Copy).then_inc(signs_done, 1)
            nc.scalar.activation(bias_hi[:], y[0][0:2, :], ACT.Copy).then_inc(signs_done, 1)
            for u in range(UNITS):
                unit(0, u)
            attention(0, split_wo)

            def wo_tiles(blk, more):
                for j in range(HALVES * TILES):
                    t = j // HALVES
                    which = units_of(j) if more else ()
                    for u in which[:1]:
                        unit(blk + 1, u)
                    if t and j % HALVES == 0:
                        normalise(blk, t - 1)
                    for u in which[1:]:
                        unit(blk + 1, u)

            with act.Fori(0, blocks - 1) as i:
                def last_tile(s):
                    if s == 0:
                        normalise(i, TILES - 1)
                wo_tiles(i, True)
                attention(i + 1, last_tile)
            wo_tiles(blocks - 1, False)
            normalise(blocks - 1, TILES - 1)

        @block.tensor
        def _(pe):
            pe.wait_ge(consts_in, 16 * 2)

            def unit(blk, u):
                pe.wait_ge(rot_done, rot_tiles * blk + rotated_of(u) + 1)
                if u >= 2:
                    pe.wait_ge(turn_done, UNITS * blk + u - 1)
                kind = 1 + u % 2 if u < KV_HEADS else 0
                nc.tensor.matmul(pair_ps[u % 2][:], feat_w[:, kind, :], rotated[rotated_of(u) % 2][:], start=True,
                                 stop=True).then_inc(p_done, 1)

            def scores_of(blk, s):
                e = SUPERS * blk + s
                if s >= 2:
                    pe.wait_ge(masked, e - 1)
                for r in range(2):
                    half = slice(r * HEAD, (r + 1) * HEAD)
                    for g in range(4):
                        tok = slice((4 * s + g) * GROUP, (4 * s + g + 1) * GROUP)
                        last = nc.tensor.matmul(att_ps[s % 2][r][:, g * P:(g + 1) * P],
                                                kf[half, tok, :].rearrange("p t g -> p (t g)"), qf[half, :, tok],
                                                start=True, stop=True)
                last.then_inc(att_done, 1)

            def context_of(blk, s):
                e = SUPERS * blk + s
                pe.wait_ge(masked, e + 1)
                pe.wait_ge(ctx_lo_done, START + e - 1)
                for g in range(4):
                    for a in range(2):
                        last = nc.tensor.matmul(pair_ps[s % 2][a * HEAD:(a + 1) * HEAD, g * P:(g + 1) * P], vg[:, 4 * s + g, :],
                                                att[s % 2][:, a, :, g, :], start=True, stop=True)
                last.then_inc(ctx_done, 1)

            def attention(blk):
                pe.wait_ge(feat_done, UNITS * (blk + 1))
                pe.wait_ge(v_ready, blk + 1)
                scores_of(blk, 0)
                if not isinstance(blk, int):
                    pe.wait_ge(y_normed, HEAD_START + HALVES * (TILES * blk - 1))
                for s in range(SUPERS):
                    if s + 1 < SUPERS:
                        scores_of(blk, s + 1)
                    context_of(blk, s)

            def wo_tiles(blk, more):
                for j in range(HALVES * TILES):
                    t, h = j // HALVES, j % HALVES
                    n = blk * TILES + t
                    pe.wait_ge(ctx_lo_done, START + SUPERS * blk + SPT * (t + 1))
                    pe.wait_ge(y_normed, HEAD_START + HALVES * (n - 2) + h + 1)
                    cols = slice(h * 512, (h + 1) * 512)
                    nc.tensor.matmul(y_ps[t % 2][h][:], ones_r[:], bias_r[:, cols], start=True, stop=False)
                    which = units_of(j)
                    for k in range(KT):
                        rows = slice(k * HEADS, (k + 1) * HEADS)
                        a_hi = ctx_hi[t][:, rows, :].rearrange("p h g -> p (h g)")
                        a_lo = ctx_lo[t][:, rows, :].rearrange("p h g -> p (h g)")
                        for s, (a, b) in enumerate(split_passes(a_hi, a_lo, wo_hi[:, k, cols], wo_lo[:, k, cols])):
                            last = nc.tensor.matmul(y_ps[t % 2][h][:], a, b, start=False, stop=(k == KT - 1 and s == 2))
                        if k == KT - 1:
                            last.then_inc(y_done, 1)
                        if more:
                            if j == 0 and k == KT - 1:
                                pe.wait_ge(ctx_lo_done, START + SUPERS * (blk + 1))
                            for i, u in enumerate(which):
                                if k == KT * (i + 1) // len(which) - 1:
                                    unit(blk + 1, u)

            for u in range(UNITS):
                unit(0, u)
            attention(0)
            pe.wait_ge(w_split, KT)
            pe.wait_ge(bias_done, 1)
            with pe.Fori(0, blocks - 1) as i:
                wo_tiles(i, True)
                attention(i + 1)
            wo_tiles(blocks - 1, False)


def route_phase(nc, score_in, order_masks, token_ids, lane_ids, count_up, chosen, keep):
    lanes, per_lane = score_in.shape
    tokens = lanes * per_lane
    slots_a = keep // P
    SIGN, EXPONENT, EXPONENT_LOW = -2 ** 31, 0x7F800000, 0x00800000

    with ExitStack() as ctx:
        sb = lambda n, s, d=F32: ctx.enter_context(nc.sbuf_tensor("r_" + n, s, d))
        ps = lambda n, s: ctx.enter_context(nc.psum_tensor("r_" + n, s, F32))
        sem = lambda n: ctx.enter_context(nc.semaphore("r_" + n))
        every = sb("every", [P, tokens])
        above = sb("above", [P, tokens])
        own = sb("own", [P, per_lane])
        masks = sb("masks", [P, 4, P])
        ids = sb("ids", [P, per_lane])
        lane_f = sb("lane_f", [P, 2])
        up = sb("up", [P, P])
        lane = sb("lane", [P, 2], I32)
        prefix = sb("prefix", [P, 1], I32)
        cand = sb("cand", [P, 1], I32)
        flip = sb("flip", [P, 1], I32)
        bits = sb("bits", [P, 1], I32)
        count = sb("count", [P, 1])
        passing = sb("passing", [P, 1])
        best = sb("best", [P, 1])
        best_i = sb("best_i", [P, 1], I32)
        ones = sb("ones", [P, per_lane])
        over = sb("over", [P, per_lane])
        tie = sb("tie", [P, per_lane])
        incl = sb("incl", [P, per_lane])
        excl = sb("excl", [P, per_lane])
        total = sb("total", [P, per_lane])
        n_over = sb("n_over", [P, 1])
        need = sb("need", [P, 1])
        sel = sb("sel", [P, per_lane])
        slot_i = sb("slot_i", [P, per_lane], I32)
        part_i = sb("part_i", [P, 2, per_lane], I32)
        part = sb("part", [P, 2, per_lane])
        picked = sb("picked", [P, per_lane])
        hot_b = sb("hot_b", [P, per_lane, P])
        hot_a = sb("hot_a", [P, per_lane, slots_a])
        rank_ps = ps("rank_ps", [P, per_lane])
        over_ps = ps("over_ps", [P, 1])
        chosen_ps = ps("chosen_ps", [P, slots_a])

        loaded = sem("loaded")
        step = sem("step")
        passed = sem("passed")
        reduced = sem("reduced")
        rank_ready = sem("rank_ready")
        ranked = sem("ranked")
        over_ready = sem("over_ready")
        over_summed = sem("over_summed")
        hot_ready = sem("hot_ready")
        listed = sem("listed")
        shifts = (25, 18, 11, 4, 0)

        block = ctx.enter_context(nc.Block())

        @block.sync
        def _(sp):
            flat = score_in.rearrange("p n -> (p n)").rearrange("(a n) -> a n", a=1)
            sp.dma_start(every[:], flat.to_broadcast([P, tokens])).then_inc(loaded, 16)
            for dst, src in ((own, score_in), (masks, order_masks), (ids, token_ids), (lane_f, lane_ids), (up, count_up)):
                sp.dma_start(dst[:], src).then_inc(loaded, 16)

        @block.gpsimd
        def _(pool):
            for r in range(len(shifts)):
                pool.wait_ge(passed, r + 1)
                nc.gpsimd.partition_all_reduce(best[:], passing[:], P, bass.bass_isa.ReduceOp.max).then_inc(reduced, 1)

        @block.vector
        def _(dve):
            done = [0]

            def link(instruction):
                done[0] += 1
                instruction.then_inc(step, 1)
                dve.wait_ge(step, done[0])

            def threshold_bits(src):
                link(nc.vector.tensor_scalar(flip[:], src[:], 31, -1, ALU.arith_shift_right, ALU.bitwise_xor))
                link(nc.vector.tensor_scalar(flip[:], flip[:], SIGN, None, ALU.bitwise_or))
                link(nc.vector.tensor_tensor(bits[:], src[:], flip[:], ALU.bitwise_xor))
                link(nc.vector.tensor_scalar(flip[:], bits[:], EXPONENT, None, ALU.bitwise_and))
                link(nc.vector.tensor_scalar(flip[:], flip[:], float(EXPONENT), -1.0, ALU.is_equal, ALU.mult))
                link(nc.vector.tensor_scalar(best_i[:], flip[:], EXPONENT_LOW, -1, ALU.bitwise_and, ALU.bitwise_xor))
                link(nc.vector.tensor_tensor(bits[:], bits[:], best_i[:], ALU.bitwise_and))
                link(nc.vector.tensor_scalar(flip[:], flip[:], EXPONENT_LOW - 1, None, ALU.bitwise_and))
                link(nc.vector.tensor_tensor(bits[:], bits[:], flip[:], ALU.bitwise_or))

            dve.wait_ge(loaded, 16 * 6)
            link(nc.vector.tensor_copy(lane[:], lane_f[:]))
            link(nc.vector.memset(prefix[:], 0))
            link(nc.vector.memset(ones[:], 1.0))
            for r, shift in enumerate(shifts):
                narrow = 1 if shift == 0 else 0
                link(nc.vector.tensor_scalar(cand[:], lane[:, narrow:narrow + 1], shift, None, ALU.logical_shift_left))
                link(nc.vector.tensor_tensor(cand[:], cand[:], prefix[:], ALU.bitwise_or))
                threshold_bits(cand)
                link(nc.vector.tensor_scalar(above[:], every[:], bits[:].bitcast(F32), 0.0, ALU.is_ge, ALU.add,
                                             accum_out=count[:]))
                nc.vector.tensor_scalar(passing[:], count[:], float(keep), lane_f[:, narrow:narrow + 1], ALU.is_ge,
                                        ALU.mult).then_inc(passed, 1)
                dve.wait_ge(reduced, r + 1)
                link(nc.vector.tensor_copy(best_i[:], best[:]))
                link(nc.vector.tensor_scalar(best_i[:], best_i[:], shift, None, ALU.logical_shift_left))
                link(nc.vector.tensor_tensor(prefix[:], prefix[:], best_i[:], ALU.bitwise_or))
            threshold_bits(prefix)
            limit = bits[:].bitcast(F32)
            link(nc.vector.tensor_scalar(over[:], own[:], limit, 0.0, ALU.is_gt, ALU.add, accum_out=n_over[:]))
            nc.vector.tensor_scalar(tie[:], own[:], limit, None, ALU.is_equal).then_inc(over_ready, 1)

            def rank_operands(flags):
                link(nc.vector.tensor_tensor_scan(incl[:], ones[:], flags[:], 0.0, ALU.mult, ALU.add))
                link(nc.vector.tensor_tensor(excl[:], incl[:], flags[:], ALU.subtract))
                nc.vector.tensor_scalar(total[:], flags[:], 0.0, incl[:, per_lane - 1:per_lane], ALU.mult,
                                        ALU.add).then_inc(rank_ready, 1)

            dve.wait_ge(over_ready, 1)
            rank_operands(tie)
            dve.wait_ge(over_summed, 1)
            link(nc.vector.tensor_scalar(need[:], over_ps[:], -1.0, float(keep), ALU.mult, ALU.add))
            dve.wait_ge(ranked, 1)
            link(nc.vector.tensor_scalar(sel[:], rank_ps[:], need[:], None, ALU.is_lt))
            link(nc.vector.tensor_tensor(sel[:], sel[:], tie[:], ALU.mult))
            link(nc.vector.tensor_tensor(sel[:], sel[:], over[:], ALU.add))
            rank_operands(sel)
            dve.wait_ge(ranked, 2)
            link(nc.vector.tensor_copy(slot_i[:], rank_ps[:]))
            link(nc.vector.tensor_scalar(part_i[:, 0, :], slot_i[:], P - 1, None, ALU.bitwise_and))
            link(nc.vector.tensor_scalar(part_i[:, 1, :], slot_i[:], P.bit_length() - 1, None, ALU.arith_shift_right))
            link(nc.vector.tensor_copy(part[:], part_i[:]))
            link(nc.vector.tensor_tensor(picked[:], sel[:], ids[:], ALU.mult))
            link(nc.vector.tensor_tensor(hot_b[:], up[:].unsqueeze(1).to_broadcast([P, per_lane, P]),
                                         part[:, 0, :].unsqueeze(2).to_broadcast([P, per_lane, P]), ALU.is_equal))
            link(nc.vector.tensor_tensor(hot_a[:], up[:, 0:slots_a].unsqueeze(1).to_broadcast([P, per_lane, slots_a]),
                                         part[:, 1, :].unsqueeze(2).to_broadcast([P, per_lane, slots_a]), ALU.is_equal))
            nc.vector.tensor_tensor(hot_a[:], hot_a[:], picked[:].unsqueeze(2).to_broadcast([P, per_lane, slots_a]),
                                    ALU.mult).then_inc(hot_ready, 1)
            dve.wait_ge(listed, 1)
            nc.vector.tensor_copy(chosen[:], chosen_ps[:])

        @block.tensor
        def _(pe):
            pe.wait_ge(over_ready, 1)
            nc.tensor.matmul(over_ps[:], masks[:, 3, :], n_over[:], start=True, stop=True).then_inc(over_summed, 1)
            for n in range(2):
                pe.wait_ge(rank_ready, n + 1)
                nc.tensor.matmul(rank_ps[:], masks[:, 0, :], total[:], start=True, stop=False)
                nc.tensor.matmul(rank_ps[:], masks[:, 1, :], excl[:], start=False, stop=False)
                nc.tensor.matmul(rank_ps[:], masks[:, 2, :], (tie, sel)[n][:], start=False, stop=True).then_inc(ranked, 1)
            pe.wait_ge(hot_ready, 1)
            for n in range(per_lane):
                last = nc.tensor.matmul(chosen_ps[:], hot_b[:, n, :], hot_a[:, n, :], start=(n == 0), stop=(n == per_lane - 1))
            last.then_inc(listed, 1)


def ffn_phase(nc, x1, w1, b1, w2, b2_rows, identity, chosen, out, keep):
    width, hidden = w1.shape
    KT = width // P
    PASSES = 2
    TT = keep // PASSES // P
    CHUNK = 2 * P
    FT = CHUNK // P
    chunks = hidden // CHUNK
    TB = TT * P // TOK_BLOCK
    steps = chunks * TB
    HALVES = width // 512
    OPS = TILES * HALVES
    O_BANKS = 4
    assert TB == 2

    with ExitStack() as ctx:
        sb = lambda n, s, d=F32: ctx.enter_context(nc.sbuf_tensor("f_" + n, s, d))
        ps = lambda n, s: ctx.enter_context(nc.psum_tensor("f_" + n, s, F32))
        sem = lambda n: ctx.enter_context(nc.semaphore("f_" + n))
        xt_hi = sb("xt_hi", [P, KT, TT * P], F32R)
        xt_lo = sb("xt_lo", [P, KT, TT * P], F32R)
        acc = sb("acc", [P, TT, width])
        w1_raw = sb("w1_raw", [P, KT, CHUNK])
        w2_raw = sb("w2_raw", [P, FT, width])
        w1_hi = [sb(f"w1_hi{b}", [P, KT, CHUNK], F32R) for b in range(2)]
        w1_lo = [sb(f"w1_lo{b}", [P, KT, CHUNK], F32R) for b in range(2)]
        w2_hi = [sb(f"w2_hi{b}", [P, FT, width], F32R) for b in range(2)]
        w2_lo = [sb(f"w2_lo{b}", [P, FT, width], F32R) for b in range(2)]
        h_hi = [sb(f"h_hi{b}", [P, FT, TOK_BLOCK], F32R) for b in range(2)]
        h_lo = [sb(f"h_lo{b}", [P, FT, TOK_BLOCK], F32R) for b in range(2)]
        act_out = [sb(f"act_out{f}", [P, TOK_BLOCK]) for f in range(FT)]
        rows = [sb(f"rows{b}", [P, width]) for b in range(2)]
        ident = sb("ident", [P, P])
        bias = sb("bias", [P, hidden // P])
        stats = sb("stats", [P, 2, 6])
        moments = [sb(f"moments{b}", [P, 2]) for b in range(2)]
        var_eps = sb("var_eps", [P, 1])
        rstd = [sb(f"rstd{b}", [P, 1]) for b in range(2)]
        neg_half = sb("neg_half", [P, 1])
        h_ps = [[ps(f"h_ps{b}{f}", [P, TOK_BLOCK]) for f in range(FT)] for b in range(2)]
        o_ps = [ps(f"o_ps{b}", [P, 512]) for b in range(O_BANKS)]
        turn = [t[:].rearrange("p (k n) -> p k n", n=P) for t in h_ps[0]]

        consts_in = sem("consts_in")
        parted = {e: sem(f"parted_{e}") for e in ("pool", "dve", "act")}
        gathered = [sem(f"gathered{u}") for u in range(TT)]
        stat_step = sem("stat_step")
        rstd_step = sem("rstd_step")
        normed = sem("normed")
        turned = sem("turned")
        x_hi = sem("x_hi")
        x_lo = sem("x_lo")
        acc_set = sem("acc_set")
        w1_in, w2_in = sem("w1_in"), sem("w2_in")
        w1_h, w2_h = sem("w1_h"), sem("w2_h")
        w1_l, w2_l = sem("w1_l"), sem("w2_l")
        h_mm = sem("h_mm")
        gelu_done = sem("gelu_done")
        h_h, h_l = sem("h_h"), sem("h_l")
        o_mm = sem("o_mm")
        added = sem("added")
        y_normed = sem("y_normed")
        regathered = [sem(f"regathered{b}") for b in range(2)]
        summed = sem("summed")
        scattered = [sem(f"scattered{b}") for b in range(2)]

        w1_v = w1.rearrange("(k p) (c f) -> c p k f", p=P, f=CHUNK)
        w2_v = w2.rearrange("(c j p) d -> c p j d", p=P, j=FT)

        block = ctx.enter_context(nc.Block())

        def per_pass(eng, prologue, step, epilogue):
            with eng.Fori(0, PASSES) as hf:
                prologue(hf)
                with eng.Fori(0, chunks // 2 - 1) as i:
                    for q in range(2 * TB):
                        step(hf, 2 * i + q // TB, 2 * TB * i + q, q // TB, q, True)
                for q in range(2 * TB):
                    step(hf, chunks - 2 + q // TB, steps - 2 * TB + q, q // TB, q, q < TB)
                epilogue(hf)

        @block.sync
        def _(sp):
            sp.dma_start(ident[:], identity).then_inc(consts_in, 16)
            sp.dma_start(bias[:], b1).then_inc(consts_in, 16)

            def load_w1(hf, c):
                sp.wait_ge(w1_l, START + chunks * hf + c)
                sp.dma_start(w1_raw[:].unsqueeze(1), w1_v[bass.ds(c, 1)].rearrange("c p k f -> p c k f")).then_inc(w1_in, 16)

            def load_w2(hf, c):
                sp.wait_ge(w2_l, START + chunks * hf + c)
                sp.dma_start(w2_raw[:].unsqueeze(1), w2_v[bass.ds(c, 1)].rearrange("c p j d -> p c j d")).then_inc(w2_in, 16)

            def prologue(hf):
                load_w1(hf, 0)
                load_w2(hf, 0)
                for u in range(TT):
                    sp.wait_ge(turned, TT * hf + u + 1)
                    sp.dma_start(acc[:, u, :], b2_rows).then_inc(acc_set, 16)

            def step(hf, c, s, cp, q, more):
                if more:
                    (load_w1 if q % TB == 0 else load_w2)(hf, c + 1)
            per_pass(sp, prologue, step, lambda hf: None)

        @block.gpsimd
        def _(pool):
            nc.gpsimd.memset(neg_half[:], -0.5).then_inc(rstd_step, 1)

            def rstd_of(e):
                pool.wait_ge(stat_step, START + 3 * e + 3)
                pool.wait_ge(rstd_step, 2 * e + 1)
                nc.gpsimd.tensor_scalar(var_eps[:], moments[e % 2][:, 1:2], LN_EPS, None, ALU.add).then_inc(rstd_step, 1)
                pool.wait_ge(rstd_step, 2 * e + 2)
                nc.gpsimd.tensor_tensor(rstd[e % 2][:], var_eps[:], neg_half[:], ALU.pow).then_inc(rstd_step, 1)

            def gather(dst, tile, done):
                pool.indirect_dma_start(out=dst, out_offset=None, in_=x1,
                                        in_offset=bass.IndirectOffsetOnAxis(ap=chosen[:, tile:tile + 1], axis=0)).then_inc(done, 16)

            for hf in range(PASSES):
                for u in range(TT):
                    if hf:
                        pool.wait_ge(summed, hf * TT - TT + u + 1)
                    gather(acc[:, u, :], hf * TT + u, gathered[u])
                for u in range(TT):
                    rstd_of(hf * 2 * TT + u)
                for b in range(2):
                    if hf:
                        pool.wait_ge(scattered[b], 16 * (hf * TT // 2))
                    gather(rows[b][:], hf * TT + b, regathered[b])
                for u in range(TT):
                    b = u % 2
                    rstd_of(hf * 2 * TT + TT + u)
                    pool.wait_ge(y_normed, hf * TT + u + 1)
                    pool.wait_ge(regathered[b], 16 * (hf * TT // 2 + u // 2 + 1))
                    nc.gpsimd.tensor_tensor(rows[b][:], rows[b][:], acc[:, u, :], ALU.add).then_inc(summed, 1)
                    pool.wait_ge(summed, hf * TT + u + 1)
                    pool.indirect_dma_start(out=out, out_offset=bass.IndirectOffsetOnAxis(
                        ap=chosen[:, hf * TT + u:hf * TT + u + 1], axis=0), in_=rows[b][:], in_offset=None).then_inc(scattered[b], 16)
                    if u + 2 < TT:
                        pool.wait_ge(scattered[b], 16 * (hf * TT // 2 + u // 2 + 1))
                        gather(rows[b][:], hf * TT + u + 2, regathered[b])
            for b in range(2):
                pool.wait_ge(scattered[b], 16 * PASSES * TT // 2)

        @block.vector
        def _(dve):
            dve.sem_inc(added, START)
            dve.sem_inc(h_l, START)
            dve.sem_inc(stat_step, START)
            dve.sem_inc(w1_l, START)
            dve.sem_inc(w2_l, START)
            dve.sem_inc(x_lo, START)
            def moments_of(e, b, u):
                dve.wait_ge(stat_step, START + 3 * e)
                for c in range(HALVES):
                    nc.vector.bn_stats(stats[:, c, :], acc[:, u, c * 512:(c + 1) * 512]).then_inc(stat_step, 1)
                dve.wait_ge(stat_step, START + 3 * e + 2)
                alone(dve, parted["dve"])
                nc.vector.bn_aggr(moments[b][:], stats[:]).then_inc(stat_step, 1)

            def normalise(e, b, u, done):
                dve.wait_ge(rstd_step, 2 * e + 3)
                dve.wait_ge(stat_step, START + 3 * e + 3)
                nc.vector.tensor_scalar(acc[:, u, :], acc[:, u, :], moments[b][:, 0:1], rstd[b][:], ALU.subtract,
                                        ALU.mult).then_inc(done, 1)

            def low_w(raw, hi, lo, high, done, n, cp):
                dve.wait_ge(high, n)
                nc.vector.tensor_tensor(lo[cp][:], raw[:], hi[cp][:].bitcast(F32), ALU.subtract).then_inc(done, 1)

            def low_h(hf, s, q):
                for f in range(FT):
                    dve.wait_ge(h_h, FT * (steps * hf + s) + f + 1)
                    nc.vector.tensor_tensor(h_lo[q % 2][:, f, :], act_out[f][:], h_hi[q % 2][:, f, :].bitcast(F32),
                                            ALU.subtract).then_inc(h_l, 1)

            def low_x(hf, u):
                dve.wait_ge(x_hi, TT * hf + u + 1)
                for c in range(2):
                    at = (slice(None), slice(c * KT // 2, (c + 1) * KT // 2), slice(u * P, (u + 1) * P))
                    last = nc.vector.tensor_tensor(xt_lo[at], turn[c], xt_hi[at].bitcast(F32), ALU.subtract)
                last.then_inc(x_lo, 1)

            def prologue(hf):
                low_w(w1_raw, w1_hi, w1_lo, w1_h, w1_l, chunks * hf + 1, 0)
                low_w(w2_raw, w2_hi, w2_lo, w2_h, w2_l, chunks * hf + 1, 0)
                for u in range(TT + 1):
                    if u < TT:
                        e = 2 * TT * hf + u
                        dve.wait_ge(gathered[u], 16 * hf + 16)
                        moments_of(e, u % 2, u)
                        normalise(e, u % 2, u, normed)
                    if u:
                        low_x(hf, u - 1)
                low_h(hf, 0, 0)
                dve.wait_ge(acc_set, 16 * TT * (hf + 1))
                alone(dve, parted["dve"])

            def step(hf, c, s, cp, q, more):
                if more:
                    if q % TB == 0:
                        low_w(w1_raw, w1_hi, w1_lo, w1_h, w1_l, chunks * hf + c + 2, 1 - cp)
                    else:
                        low_w(w2_raw, w2_hi, w2_lo, w2_h, w2_l, chunks * hf + c + 2, 1 - cp)
                if more or q < 2 * TB - 1:
                    low_h(hf, s + 1, q + 1)
                n = OPS * (steps * hf + s)
                dve.wait_ge(added, START + n)
                for j in range(OPS):
                    dve.wait_ge(o_mm, START + n + j + 1)
                    at = (slice(None), q % TB * TILES + j // HALVES, slice(j % HALVES * 512, (j % HALVES + 1) * 512))
                    nc.vector.tensor_tensor(acc[at], o_ps[j % O_BANKS][:], acc[at], ALU.add).then_inc(added, 1)

            def epilogue(hf):
                dve.wait_ge(added, START + OPS * steps * (hf + 1))
                for u in range(TT):
                    e = 2 * TT * hf + TT + u
                    moments_of(e, u % 2, u)
                    normalise(e, u % 2, u, y_normed)
            per_pass(dve, prologue, step, epilogue)

        @block.scalar
        def _(act):
            act.wait_ge(consts_in, 32)

            def high_w(raw, hi, loaded, done, n, cp):
                act.wait_ge(loaded, 16 * n)
                nc.scalar.activation(hi[cp][:], raw[:], ACT.Copy).then_inc(done, 1)

            def gelu(hf, s, c, q, first=False):
                n = steps * hf + s
                for f in range(FT):
                    act.wait_ge(h_mm, FT * n + f + 1)
                    act.wait_ge(h_l, START + (FT * n if first else FT * (n - 1) + f + 1))
                    alone(act, parted["act"])
                    nc.scalar.activation(act_out[f][:], h_ps[q % 2][f][:], ACT.Gelu_apprx_tanh,
                                         bias=bias[:, bass.ds(c * FT + f, 1)]).then_inc(gelu_done, 1)
                    act.wait_ge(gelu_done, FT * n + f + 1)
                    nc.scalar.activation(h_hi[q % 2][:, f, :], act_out[f][:], ACT.Copy).then_inc(h_h, 1)

            def prologue(hf):
                act.wait_ge(o_mm, START + OPS * steps * hf)
                high_w(w1_raw, w1_hi, w1_in, w1_h, chunks * hf + 1, 0)
                high_w(w2_raw, w2_hi, w2_in, w2_h, chunks * hf + 1, 0)
                for u in range(TT):
                    act.wait_ge(turned, TT * hf + u + 1)
                    for k in range(2):
                        at = (slice(None), slice(k * KT // 2, (k + 1) * KT // 2), slice(u * P, (u + 1) * P))
                        last = nc.scalar.activation(xt_hi[at], turn[k], ACT.Copy)
                    last.then_inc(x_hi, 1)
                gelu(hf, 0, 0, 0, True)

            def step(hf, c, s, cp, q, more):
                n = OPS * (steps * hf + s)
                if more:
                    if q % TB == 0:
                        high_w(w1_raw, w1_hi, w1_in, w1_h, chunks * hf + c + 2, 1 - cp)
                    else:
                        act.wait_ge(o_mm, START + n - OPS)
                        high_w(w2_raw, w2_hi, w2_in, w2_h, chunks * hf + c + 2, 1 - cp)
                if more or q < 2 * TB - 1:
                    act.wait_ge(o_mm, START + n)
                    gelu(hf, s + 1, c + (q % TB == TB - 1), q + 1)
            per_pass(act, prologue, step, lambda hf: None)

        @block.tensor
        def _(pe):
            pe.sem_inc(o_mm, START)
            pe.wait_ge(consts_in, 32)

            def first(hf, c, s, cp, q):
                pe.wait_ge(w1_l, START + chunks * hf + c + 1)
                cols = slice(q % TB * TOK_BLOCK, (q % TB + 1) * TOK_BLOCK)
                for f in range(FT):
                    for k in range(KT):
                        fs = slice(f * P, (f + 1) * P)
                        for t, (a, b) in enumerate(split_passes(w1_hi[cp][:, k, fs], w1_lo[cp][:, k, fs],
                                                                xt_hi[:, k, cols], xt_lo[:, k, cols])):
                            last = nc.tensor.matmul(h_ps[q % 2][f][:], a, b, start=(k == 0 and t == 0), stop=(k == KT - 1 and t == 2))
                    last.then_inc(h_mm, 1)

            def second(hf, c, s, cp, q):
                n = steps * hf + s
                pe.wait_ge(h_l, START + FT * (n + 1))
                pe.wait_ge(w2_l, START + chunks * hf + c + 1)
                for j in range(OPS):
                    if q or j >= O_BANKS - 1:
                        pe.wait_ge(added, START + OPS * n + j - O_BANKS + 1)
                    rs, cs = slice(j // HALVES * P, (j // HALVES + 1) * P), slice(j % HALVES * 512, (j % HALVES + 1) * 512)
                    for f in range(FT):
                        for t, (a, b) in enumerate(split_passes(h_hi[q % 2][:, f, rs], h_lo[q % 2][:, f, rs],
                                                                w2_hi[cp][:, f, cs], w2_lo[cp][:, f, cs])):
                            last = nc.tensor.matmul(o_ps[j % O_BANKS][:], a, b, start=(f == 0 and t == 0), stop=(f == FT - 1 and t == 2))
                    last.then_inc(o_mm, 1)
                if q == 2 * TB - 1:
                    pe.wait_ge(added, START + OPS * (n + 1) - 1)

            def prologue(hf):
                for u in range(TT):
                    pe.wait_ge(normed, TT * hf + u + 1)
                    pe.wait_ge(x_lo, START + TT * hf + u)
                    for k in range(KT):
                        last = nc.tensor.transpose(turn[k * 2 // KT][:, k % (KT // 2), :], acc[:, u, k * P:(k + 1) * P], ident[:])
                    last.then_inc(turned, 1)
                pe.wait_ge(x_lo, START + TT * (hf + 1))
                first(hf, 0, 0, 0, 0)

            def step(hf, c, s, cp, q, more):
                if more or q < 2 * TB - 1:
                    nq = (q + 1) % (2 * TB)
                    first(hf, c + (q % TB == TB - 1), s + 1, nq // TB, nq)
                second(hf, c, s, cp, q)
            per_pass(pe, prologue, step, lambda hf: None)


def shape_constants(tokens):
    import numpy as np
    f32 = np.float32
    inv_freq = (f32(1.0) / f32(10000.0) ** (np.arange(0, HEAD, 2, dtype=f32) / f32(HEAD))).astype(f32)
    angles = (np.arange(tokens, dtype=f32)[None, :] * inv_freq[:, None]).astype(f32)
    cos, sin = np.cos(angles), np.sin(angles)
    lane = np.arange(P)
    rows = GROUP // 2
    head, row = lane // rows, lane % rows
    tiles = tokens // P
    earlier = head[:, None] < head[None, :]
    same = head[:, None] == head[None, :]
    return {
        "rope_cos": np.concatenate([cos] * 4),
        "rope_sin": np.concatenate([-sin, sin] * 2),
        "bias_signs": np.stack([np.concatenate([[0], np.full(P, -1)]), np.concatenate([[1], np.ones(P)])]).astype(f32),
        "identity": np.eye(P, dtype=f32),
        "same_head": np.kron(np.eye(P // HEAD), np.ones((HEAD, HEAD))).astype(f32),
        "phase": np.tile(np.repeat(np.array([0.0, 0.25], f32), HEAD // 2), P // HEAD)[:, None],
        "own_token": np.kron(np.eye(GROUP), np.ones((KV_HEADS, 1))).astype(f32),
        "order_masks": np.stack([earlier, same, same & (row[:, None] < row[None, :]), np.ones((P, P), bool)], 1).astype(f32),
        "token_ids": (head[:, None] * (tokens // HEADS) + np.arange(tiles)[None, :] * rows + row[:, None]).astype(f32),
        "lane_ids": np.stack([lane, lane % 16], 1).astype(f32),
        "count_up": np.tile(np.arange(P, dtype=f32), (P, 1)),
    }


def feature_weights(R):
    import numpy as np
    e = R.shape[0]
    w = np.zeros((P, 3, P), R.dtype)
    for j in range(2):
        rows = slice(HEAD * j, HEAD * (j + 1))
        for c in range(2):
            w[rows, 0, HEAD * j + e * c:HEAD * j + e * (c + 1)] = R.T
            for half in range(2):
                at = HEAD * half + e * c
                w[rows, 1 + j, at:at + e] = R.T
    return w


def build(nc, a, out):
    tokens, width = a["x"].shape
    qk_tiles = (HEADS + KV_HEADS) // 2
    keep = tokens // 2
    qk_scratch = nc.dram_tensor("qk_scratch", (tokens // TOK_BLOCK, qk_tiles, P, TOK_BLOCK), F32, kind="Internal").ap()
    v_scratch = nc.dram_tensor("v_scratch", (tokens, KV_HEADS * HEAD), F32, kind="Internal").ap()
    score_scratch = nc.dram_tensor("score_scratch", (P, tokens // P), F32, kind="Internal").ap()
    project_phase(nc, a["x"], a["w_qkv_t"], a["b_qk"], a["identity"], a["same_head"], qk_scratch, v_scratch)
    mix_phase(nc, a["x"], qk_scratch, v_scratch, a["rope_cos"], a["rope_sin"], a["features"], a["phase"], a["v_bias"],
              a["own_token"], a["w_o_t"], a["o_bias"], a["bias_signs"], a["router"], a["router_bias"], out, score_scratch)
    with nc.sbuf_tensor("chosen", [P, keep // P], I32) as chosen:
        route_phase(nc, score_scratch, a["order_masks"], a["token_ids"], a["lane_ids"], a["count_up"], chosen, keep)
        ffn_phase(nc, out, a["w1"], a["b1"], a["w2"], a["b2_rows"], a["identity"], chosen, out, keep)


def kernel(**inputs):
    import numpy as np
    import concourse.bacc as bacc
    from concourse.bass_utils import run_bass_kernel_spmd

    g = {k: np.asarray(v) for k, v in inputs.items()}
    x = g["L0_attn_hidden_states"]
    arrays = {
        "x": x[0],
        "w_qkv_t": np.concatenate([g["L0_attn_Wq"], g["L0_attn_Wk"], g["L0_attn_Wv"]]).T,
        "b_qk": np.concatenate([g["L0_attn_bq"], g["L0_attn_bk"]]).reshape(-1, P).T,
        "v_bias": np.tile(g["L0_attn_bv"].reshape(KV_HEADS, HEAD), (GROUP, 1)),
        "features": feature_weights(g["L0_attn_rand_matrix"]),
        "w_o_t": g["L0_attn_Wo"].T,
        "o_bias": np.tile(g["L0_attn_bo"], (2, 1)),
        "router": np.tile(g["L0_ffn_w_r"], (P, 1)),
        "router_bias": np.tile(g["L0_ffn_b_r"].reshape(1, 1), (P, 1)),
        "w1": g["L0_ffn_w1"],
        "b1": g["L0_ffn_b1"].reshape(-1, P).T,
        "w2": g["L0_ffn_w2"],
        "b2_rows": np.tile(g["L0_ffn_b2"], (P, 1)),
    }
    arrays.update(shape_constants(x.shape[1]))
    arrays = {k: np.ascontiguousarray(v) for k, v in arrays.items()}

    nc = bacc.Bacc("TRN2", target_bir_lowering=False, num_devices=1)
    tensors = {k: nc.dram_tensor(f"in_{k}", v.shape, mybir.dt.from_np(v.dtype), kind="ExternalInput").ap() for k, v in arrays.items()}
    out = nc.dram_tensor("out_x", x.shape[1:], F32, kind="ExternalOutput").ap()
    build(nc, tensors, out)
    r = run_bass_kernel_spmd(nc, [{f"in_{k}": v for k, v in arrays.items()}], core_ids=[0])
    return r.results[0]["out_x"].reshape(x.shape)
```

```python
from contextlib import ExitStack

import concourse.bass as bass
from concourse import mybir

P = 128
F32 = mybir.dt.float32
F32R = mybir.dt.float32r
I32 = mybir.dt.int32
U32 = mybir.dt.uint32
ALU = mybir.AluOpType
ACT = mybir.ActivationFunctionType
AX_X = mybir.AxisListType.X

HEADS, KV_HEADS, HEAD = 16, 8, 64
LN_EPS = 1e-5
TOK_BLOCK = 512
TILES = TOK_BLOCK // P


START = 2


def alone(eng, sem):
    eng.sem_inc(sem, 1)


def split_passes(hi_a, lo_a, hi_b, lo_b):
    return ((hi_a, hi_b), (hi_a, lo_b), (lo_a, hi_b))


def project_phase(nc, x, w_qkv_t, b_qk, identity, same_head, qk_scratch, v_scratch):
    tokens, width = x.shape
    KT = width // P
    cols = w_qkv_t.shape[1]
    blocks = tokens // TOK_BLOCK
    qk_tiles = qk_scratch.shape[1]
    outs_per_block = qk_tiles + TILES
    QK_PER_CHUNK = qk_tiles // TILES
    CH = QK_PER_CHUNK + 1
    MM_BANKS = CH
    STAGES = QK_PER_CHUNK
    pieces = cols // TOK_BLOCK
    W_ORDER = (0, 3, 1, 2)
    assert pieces == STAGES + 1 == TILES and KT % pieces == 0

    with ExitStack() as ctx:
        sb = lambda n, s, d: ctx.enter_context(nc.sbuf_tensor(n, s, d))
        sem = lambda n: ctx.enter_context(nc.semaphore(n))
        w_hi = sb("w_hi", [P, KT, cols], F32R)
        w_lo = sb("w_lo", [P, KT, cols], F32R)
        h_hi = [sb(f"h_hi{b}", [P, KT, TOK_BLOCK], F32R) for b in range(2)]
        h_lo = [sb(f"h_lo{b}", [P, KT, TOK_BLOCK], F32R) for b in range(2)]
        xt = sb("xt", [P, width], F32)
        stage = [sb(f"stage{b}", [P, TOK_BLOCK], F32) for b in range(STAGES)]
        squares = [sb(f"squares{b}", [P, TOK_BLOCK], F32) for b in range(2)]
        piece_in = stage + squares[:1]
        ident = sb("ident", [P, P], F32)
        ones = sb("ones", [P, P], F32)
        bias = sb("bias", [P, qk_tiles], F32)
        stats = sb("stats", [P, 2, 6], F32)
        moments = [sb(f"moments{b}", [P, 2], F32) for b in range(2)]
        var_eps = sb("var_eps", [P, 1], F32)
        rstd = [sb(f"rstd{b}", [P, 1], F32) for b in range(2)]
        neg_half = sb("neg_half", [P, 1], F32)
        mm = [ctx.enter_context(nc.psum_tensor(f"mm{b}", [P, TOK_BLOCK], F32)) for b in range(MM_BANKS)]
        turn = [ctx.enter_context(nc.psum_tensor(f"turn{b}", [P, KT // 2, P], F32)) for b in range(2)]
        norm_ps = ctx.enter_context(nc.psum_tensor("norm_ps", [P, TOK_BLOCK], F32))

        consts_in = sem("p_consts_in")
        parted = {e: sem(f"p_parted_{e}") for e in ("pool", "dve")}
        w_in = [sem(f"p_w_in{b}") for b in range(pieces)]
        w_hi_done = sem("p_w_hi_done")
        w_split = sem("p_w_split")
        x_in = sem("p_x_in")
        stat_step = sem("p_stat_step")
        rstd_step = sem("p_rstd_step")
        normed = sem("p_normed")
        turned = sem("p_turned")
        hi_done = sem("p_hi_done")
        lo_done = sem("p_lo_done")
        mm_done = sem("p_mm_done")
        evac = sem("p_evac")
        norm_done = sem("p_norm_done")
        root_done = sem("p_root_done")
        recip_done = sem("p_recip_done")
        scaled = sem("p_scaled")
        stored = [sem(f"p_stored{b}") for b in range(STAGES)]

        block = ctx.enter_context(nc.Block())

        def per_block(eng, chunk):
            with eng.Fori(0, blocks // 2 - 1) as i:
                for b in range(2):
                    for t in range(TILES):
                        chunk(2 * i + b, b, t, True, False)
            for b in range(2):
                for t in range(TILES):
                    chunk(blocks - 2 + b, b, t, b == 0, True)

        def piece(k, q):
            return (slice(None), bass.ds(k, 1), slice(q * TOK_BLOCK, (q + 1) * TOK_BLOCK))

        @block.sync
        def _(sp):
            for s in stored:
                sp.sem_inc(s, START)
            sp.dma_start(ident[:], identity).then_inc(consts_in, 16)
            sp.dma_start(xt[:], x[0:P, :]).then_inc(x_in, 16)
            sp.dma_start(ones[:], same_head).then_inc(consts_in, 16)
            sp.dma_start(bias[:], b_qk).then_inc(consts_in, 16)

            def load_w(k, q, b):
                sp.dma_start(piece_in[b][:], w_qkv_t[bass.ts(k, P), q * TOK_BLOCK:(q + 1) * TOK_BLOCK]).then_inc(w_in[b], 16)

            def load_x(n):
                sp.wait_ge(turned, n)
                sp.dma_start(xt[:], x[bass.ts(n, P), :]).then_inc(x_in, 16)

            for t in range(TILES):
                with sp.Fori(0, KT // pieces) as i:
                    for b in range(pieces):
                        sp.wait_ge(w_split, KT * t + pieces * i + b + 1)
                        load_w(pieces * i + b, W_ORDER[t], b)
                load_x(t + 1)

            def chunk(blk, par, t, more, peeled):
                for jj in range(CH):
                    out = blk * outs_per_block + t * CH + jj
                    if jj < QK_PER_CHUNK:
                        m = t * QK_PER_CHUNK + jj
                        sp.wait_ge(scaled, START + blk * qk_tiles + m + 1)
                        sp.dma_start(qk_scratch[blk, m], stage[jj][:]).then_inc(stored[jj], 16)
                        if jj == 0 and more and not (peeled and t == TILES - 1):
                            load_x((blk + 1) * TILES + t + 1)
                    else:
                        sp.wait_ge(evac, START + out + 1)
                        sp.dma_start(v_scratch[bass.ts(blk * TILES + t, P), :], stage[0][:]).then_inc(stored[0], 16)
            per_block(sp, chunk)
            for b in range(STAGES):
                sp.wait_ge(stored[b], START + 16 * blocks * TILES * (2 if b == 0 else 1))

        @block.gpsimd
        def _(pool):
            nc.gpsimd.memset(neg_half[:], -0.5).then_inc(rstd_step, 1)

            def rstd_of(n, b):
                pool.wait_ge(stat_step, 3 * n + 3)
                pool.wait_ge(rstd_step, 2 * n + 1)
                alone(pool, parted["pool"])
                nc.gpsimd.tensor_scalar(var_eps[:], moments[b][:, 1:2], LN_EPS, None, ALU.add).then_inc(rstd_step, 1)
                pool.wait_ge(rstd_step, 2 * n + 2)
                nc.gpsimd.tensor_tensor(rstd[b][:], var_eps[:], neg_half[:], ALU.pow).then_inc(rstd_step, 1)

            for t in range(TILES):
                rstd_of(t, t % 2)

            def chunk(blk, par, t, more, peeled):
                if more:
                    rstd_of((blk + 1) * TILES + t, t % 2)
            per_block(pool, chunk)

        @block.vector
        def _(dve):
            dve.sem_inc(scaled, START)
            dve.sem_inc(w_split, pieces)

            def split_weights(t, i, b):
                k, q = pieces * i + b, W_ORDER[t]
                dve.wait_ge(w_hi_done, KT * t + k + 1)
                nc.vector.tensor_tensor(w_lo[piece(k, q)].rearrange("p a n -> p (a n)"), piece_in[b][:],
                                        w_hi[piece(k, q)].rearrange("p a n -> p (a n)").bitcast(F32),
                                        ALU.subtract).then_inc(w_split, 1)

            def norm(n, b):
                dve.wait_ge(x_in, 16 * n + 16)
                dve.wait_ge(stat_step, 3 * n)
                for c in range(2):
                    nc.vector.bn_stats(stats[:, c, :], xt[:, c * 512:(c + 1) * 512]).then_inc(stat_step, 1)
                dve.wait_ge(stat_step, 3 * n + 2)
                alone(dve, parted["dve"])
                nc.vector.bn_aggr(moments[b][:], stats[:]).then_inc(stat_step, 1)
                dve.wait_ge(rstd_step, 2 * n + 3)
                dve.wait_ge(stat_step, 3 * n + 3)
                nc.vector.tensor_scalar(xt[:], xt[:], moments[b][:, 0:1], rstd[b][:], ALU.subtract,
                                        ALU.mult).then_inc(normed, 1)

            def low(n, par, t):
                dve.wait_ge(hi_done, n + 1)
                for c in range(2):
                    at = (slice(None), slice(c * KT // 2, (c + 1) * KT // 2), slice(t * P, (t + 1) * P))
                    last = nc.vector.tensor_tensor(h_lo[par][at], turn[c][:], h_hi[par][at].bitcast(F32), ALU.subtract)
                last.then_inc(lo_done, 1)

            for t in range(TILES):
                norm(t, t % 2)
                if t == TILES - 1:
                    low(t, 0, t)
                with dve.Fori(0, KT // pieces) as i:
                    for b in range(pieces):
                        split_weights(t, i, b)
                if t < TILES - 1:
                    low(t, 0, t)

            def chunk(blk, par, t, more, peeled):
                n = (blk + 1) * TILES + t
                if more:
                    norm(n, t % 2)
                for jj in range(QK_PER_CHUNK):
                    m = t * QK_PER_CHUNK + jj
                    sq = squares[m % 2]
                    dve.wait_ge(root_done, START + blk * qk_tiles + m + 1)
                    nc.vector.reciprocal(sq[:], sq[:]).then_inc(recip_done, 1)
                    dve.wait_ge(recip_done, blk * qk_tiles + m + 1)
                    nc.vector.scalar_tensor_tensor(out=stage[jj][:], in0=sq[:], scalar=1e6, in1=stage[jj][:],
                                                   op0=ALU.min, op1=ALU.mult).then_inc(scaled, 1)
                    if more and jj == 0:
                        low(n, 1 - par, t)
            per_block(dve, chunk)

        @block.scalar
        def _(act):
            act.sem_inc(evac, START)
            act.sem_inc(root_done, START)
            act.wait_ge(consts_in, 48)

            def high(n, par, t):
                act.wait_ge(turned, n + 1)
                for c in range(2):
                    at = (slice(None), slice(c * KT // 2, (c + 1) * KT // 2), slice(t * P, (t + 1) * P))
                    last = nc.scalar.activation(h_hi[par][at], turn[c][:], ACT.Copy)
                last.then_inc(hi_done, 1)

            for t in range(TILES):
                if t == TILES - 1:
                    high(t, 0, t)
                with act.Fori(0, KT // pieces) as i:
                    for b in range(pieces):
                        act.wait_ge(w_in[b], 16 * (KT // pieces * t + i) + 16)
                        nc.scalar.activation(w_hi[piece(pieces * i + b, W_ORDER[t])].rearrange("p a n -> p (a n)"), piece_in[b][:],
                                             ACT.Copy).then_inc(w_hi_done, 1)
                if t < TILES - 1:
                    high(t, 0, t)

            act.wait_ge(w_split, pieces + KT * TILES)

            def chunk(blk, par, t, more, peeled):
                for jj in range(CH):
                    out = blk * outs_per_block + t * CH + jj
                    b = jj % STAGES
                    act.wait_ge(mm_done, out + 1)
                    earlier = 2 * (blk * TILES + t) + jj // STAGES if b == 0 else blk * TILES + t
                    act.wait_ge(stored[b], START + 16 * earlier)
                    if jj < QK_PER_CHUNK:
                        m = t * QK_PER_CHUNK + jj
                        nc.scalar.activation(stage[b][:], mm[jj][:], ACT.Identity, bias=bias[:, m:m + 1])
                        act.wait_ge(scaled, START + blk * qk_tiles + m - 1)
                        nc.scalar.activation(squares[m % 2][:], mm[jj][:], ACT.Square, bias=bias[:, m:m + 1]).then_inc(evac, 1)
                        if jj == 1 and more:
                            high((blk + 1) * TILES + t, 1 - par, t)
                        act.wait_ge(norm_done, blk * qk_tiles + m + 1)
                        nc.scalar.activation(squares[m % 2][:], norm_ps[:], ACT.Sqrt).then_inc(root_done, 1)
                    else:
                        nc.scalar.activation(stage[b][:], mm[jj][:], ACT.Copy).then_inc(evac, 1)
            per_block(act, chunk)

        @block.tensor
        def _(pe):
            pe.wait_ge(consts_in, 48)

            def transposes(n):
                pe.wait_ge(normed, n + 1)
                pe.wait_ge(lo_done, n)
                for k in range(KT):
                    last = nc.tensor.transpose(turn[k * 2 // KT][:, k % (KT // 2), :], xt[:, k * P:(k + 1) * P], ident[:])
                last.then_inc(turned, 1)

            for t in range(TILES):
                transposes(t)

            def norms(blk, out, m):
                pe.wait_ge(evac, START + out + 1)
                pe.wait_ge(root_done, START + blk * qk_tiles + m)
                nc.tensor.matmul(norm_ps[:], ones[:], squares[m % 2][:], start=True, stop=True).then_inc(norm_done, 1)

            def chunk(blk, par, t, more, peeled):
                if t == 0:
                    pe.wait_ge(lo_done, (blk + 1) * TILES)
                for jj in range(CH):
                    out = blk * outs_per_block + t * CH + jj
                    bank = mm[jj]
                    if t or jj == MM_BANKS - 1:
                        pe.wait_ge(evac, START + out - MM_BANKS + 1)
                    column = (t * QK_PER_CHUNK + jj) * P // TOK_BLOCK if jj < QK_PER_CHUNK else pieces - 1
                    pe.wait_ge(w_split, pieces + KT * (W_ORDER.index(column) + 1))
                    hh, hl = h_hi[par], h_lo[par]
                    for k in range(KT):
                        if jj < QK_PER_CHUNK:
                            c = slice((t * QK_PER_CHUNK + jj) * P, (t * QK_PER_CHUNK + jj + 1) * P)
                            terms = split_passes(w_hi[:, k, c], w_lo[:, k, c], hh[:, k, :], hl[:, k, :])
                        else:
                            c = slice(t * P, (t + 1) * P)
                            terms = split_passes(hh[:, k, c], hl[:, k, c], w_hi[:, k, qk_tiles * P:], w_lo[:, k, qk_tiles * P:])
                        for s, (a, b) in enumerate(terms):
                            last = nc.tensor.matmul(bank[:], a, b, start=(k == 0 and s == 0), stop=(k == KT - 1 and s == 2))
                    last.then_inc(mm_done, 1)
                    if jj:
                        norms(blk, out - 1, t * QK_PER_CHUNK + jj - 1)
                    if jj == 1 and more:
                        transposes((blk + 1) * TILES + t)
                if more and t == TILES - 1:
                    pe.wait_ge(evac, START + (blk + 1) * outs_per_block - 1)
            per_block(pe, chunk)


ROUND = 1.5 * 2.0 ** 23
TWO_PI = 6.2831850
GROUP = P // KV_HEADS
ROTARY_SHIFT = HEAD // 2


def mix_phase(nc, x, qk_scratch, v_scratch, cos_t, sin_t, features, phase, v_bias, own_token, w_o_t, o_bias,
              bias_signs, router, router_bias, out, score_out, scale_out):
    tokens, width = x.shape
    blocks = tokens // TOK_BLOCK
    KT = width // P
    q_tiles = HEADS // 2
    k_tiles = KV_HEADS // 2
    rot_tiles = q_tiles + k_tiles
    UNITS = KV_HEADS + q_tiles
    SUPER = 4 * GROUP
    SUPERS = TOK_BLOCK // SUPER
    SPT = SUPERS // TILES
    QK_RING = 4
    ROT_RING = 3
    GROUPS = TOK_BLOCK // GROUP
    V_PIECES = 4
    HALVES = width // 512
    feature_scale = 2.0 / HEAD
    HEAD_START = 2 * HALVES
    UNITS_UP_TO = (0, 3, 6, 9, 12, 14, 16)
    WO_UP_TO = (0, 3, 8, 10, 12, 14, HALVES * KT)
    WO_SUPERS = len(WO_UP_TO) - 2
    LAST_TILE = TILES - 1
    ROTATE_AT = (3, 4, 6)
    assert UNITS_UP_TO[-1] == UNITS and len(UNITS_UP_TO) == HALVES * LAST_TILE + 1

    with ExitStack() as ctx:
        sb = lambda n, s, d=F32: ctx.enter_context(nc.sbuf_tensor(n, s, d))
        ps = lambda n, s: ctx.enter_context(nc.psum_tensor(n, s, F32))
        sem = lambda n: ctx.enter_context(nc.semaphore("m_" + n))
        wo_hi = sb("wo_hi", [P, KT, width], F32R)
        wo_lo = sb("wo_lo", [P, KT, width], F32R)
        qf = sb("qf", [P, q_tiles, TOK_BLOCK])
        kf = sb("kf", [P, TOK_BLOCK, KV_HEADS])
        ctx_hi = [sb(f"ctx_hi{t}", [P, P, GROUP // 2], F32R) for t in range(TILES)]
        ctx_lo = [sb(f"ctx_lo{t}", [P, P, GROUP // 2], F32R) for t in range(TILES)]
        att = [sb(f"att{b}", [P, 2, GROUP // 2, 4, HEADS]) for b in range(2)]
        qk_in = [sb(f"qk_in{b}", [P, TOK_BLOCK]) for b in range(QK_RING)]
        qk_swap = [sb(f"qk_swap{b}", [P, TOK_BLOCK]) for b in range(QK_RING)]
        q_cos = [sb(f"q_cos{b}", [P, TOK_BLOCK]) for b in range(2)]
        rotated = [sb(f"rotated{b}", [P, TOK_BLOCK]) for b in range(ROT_RING)]
        turns = [sb(f"turns{b}", [P, TOK_BLOCK]) for b in range(2)]
        whole = sb("whole", [P, TOK_BLOCK])
        cs = sb("cs", [P, 2, TOK_BLOCK])
        vg = sb("vg", [P, GROUPS, HEAD])
        vb = sb("vb", [P, HEAD])
        xr = [sb(f"xr{b}", [P, width]) for b in range(2)]
        y = [sb(f"y{b}", [P, width]) for b in range(2)]
        wr = sb("wr", [P, width])
        feat_w = sb("feat_w", [P, 3, P])
        phases = sb("phases", [P, 1])
        own = sb("own", [P, GROUP])
        br = sb("br", [P, 1])
        signs = y[1][0:2, 0:1 + P]
        ones_r = sb("ones_r", [2, P], F32R)
        bias_hi = ctx_hi[0][0:2].rearrange("p h g -> p (h g)")
        bias_r = sb("bias_r", [2, width], F32R)
        raw = sb("raw", [P, TILES])
        scores = sb("scores", [P, blocks * TILES])
        scales = sb("scales", [P, blocks * TILES, 2])
        means = sb("means", [P, blocks * TILES])
        variances = sb("variances", [P, blocks * TILES])
        stats1 = sb("m_stats1", [P, HALVES, 6])
        stats2 = sb("m_stats2", [P, HALVES, 6])
        moments1 = sb("m_moments1", [P, 2])
        moments2 = sb("m_moments2", [P, TILES, 2])
        var_eps = sb("m_var_eps", [P, 1])
        rstd = sb("m_rstd", [P, 1])
        shift = sb("m_shift", [P, 1])
        neg_half = sb("m_neg_half", [P, 1])
        pair_ps = [ps(f"pair_ps{b}", [P, 512]) for b in range(2)]
        att_ps = [[ps(f"att_ps{b}{r}", [P, 4 * P]) for r in range(2)] for b in range(2)]
        own_ps = [ps(f"y_ps{h}", [P, 512]) for h in range(HALVES)]
        y_ps = [att_ps[1], own_ps]

        feat_in = sem("feat_in")
        consts_in = sem("consts_in")
        parted = {e: sem(f"parted_{e}") for e in ("pool", "dve", "sp", "act")}
        signs_done = sem("signs_done")
        bias_done = sem("bias_done")
        w_in = [sem(f"w_in{b}") for b in range(2)]
        w_hi_done = sem("w_hi_done")
        w_split = sem("w_split")
        cs_in = sem("cs_in")
        qk_loaded = [sem(f"qk_loaded{b}") for b in range(QK_RING)]
        v_in = sem("v_in")
        v_ready = sem("v_ready")
        cos_done = sem("cos_done")
        sin_done = sem("sin_done")
        rot_done = sem("rot_done")
        p_done = sem("p_done")
        turn_done = sem("turn_done")
        whole_done = sem("whole_done")
        frac_done = sem("frac_done")
        feat_done = sem("feat_done")
        att_done = sem("att_done")
        masked = sem("masked")
        ctx_done = sem("ctx_done")
        ctx_hi_done = sem("ctx_hi_done")
        ctx_lo_done = sem("ctx_lo_done")
        y_done = sem("y_done")
        stat1 = sem("stat1")
        rstd_step = sem("rstd_step")
        y_normed = sem("y_normed")
        x_loaded = [sem(f"x_loaded{b}") for b in range(2)]
        x1_done = sem("x1_done")
        stat2 = sem("stat2")
        scored = sem("scored")
        kept = sem("kept")
        x1_stored = [sem(f"x1_stored{b}") for b in range(2)]
        score_step = sem("score_step")
        score_stored = sem("score_stored")

        v_rows = v_scratch.rearrange("t (g d) -> (t g) d", d=HEAD).rearrange("(b s n p) d -> b s p n d", p=P, s=V_PIECES,
                                                                             n=GROUPS // V_PIECES)
        x_rows = x.rearrange("(h n g) d -> n h g d", h=HEADS, g=GROUP // 2)
        out_rows = out.rearrange("(h n g) d -> n h g d", h=HEADS, g=GROUP // 2)

        block = ctx.enter_context(nc.Block())

        def rotated_of(u):
            return u // 2 if u < KV_HEADS else u - k_tiles

        def first_unit(m):
            return 2 * m if m < k_tiles else m + k_tiles

        def readers_before(m):
            after = m - ROT_RING + 1
            return first_unit(after) if m >= ROT_RING else first_unit(after + rot_tiles) - UNITS

        def units_of(j):
            return range(UNITS_UP_TO[j], UNITS_UP_TO[j + 1])

        def rotations_for(u, earlier=0):
            ahead = rotated_of(u) + ROT_RING - 1 + earlier
            return (ahead,) if u and rotated_of(u) != rotated_of(u - 1) and ahead < rot_tiles else ()

        @block.sync
        def _(sp):
            def load_cs(blk):
                for j, table in enumerate((cos_t, sin_t)):
                    sp.dma_start(cs[:, j, :], table[:, bass.ts(blk, TOK_BLOCK)]).then_inc(cs_in, 16)

            def load_qk(blk, m):
                b = m % QK_RING
                tile = qk_scratch[blk, m + q_tiles if m < k_tiles else m - k_tiles]
                sp.dma_start(qk_in[b][:], tile).then_inc(qk_loaded[b], 16)
                for head in range(2):
                    halves = tile[head * HEAD:(head + 1) * HEAD].rearrange("(s p) n -> s p n", s=2)
                    for s in range(2):
                        at = head * HEAD + (1 - s) * ROTARY_SHIFT
                        sp.dma_start(qk_swap[b][at:at + ROTARY_SHIFT, :], halves[s]).then_inc(qk_loaded[b], 16)

            def load_v(blk):
                for s in range(V_PIECES):
                    n = GROUPS // V_PIECES
                    sp.dma_start(vg[:, s * n:(s + 1) * n, :], v_rows[blk, s]).then_inc(v_in, 16)

            def load_x(n, b):
                sp.dma_start(xr[b][:], x_rows[n]).then_inc(x_loaded[b], 16)

            def reload_qk(blk, m):
                sp.wait_ge(rot_done, rot_tiles * blk + m - QK_RING + 1)
                alone(sp, parted["sp"])
                load_qk(blk, m)

            def store_x1(blk, t):
                sp.wait_ge(x1_done, blk * TILES + t + 1)
                sp.dma_start(out_rows[blk * TILES + t], xr[t % 2][:]).then_inc(x1_stored[t % 2], 16)

            def next_x(blk, t):
                sp.wait_ge(x1_stored[t % 2], 16 * (blk * 2 + t // 2 + 1))
                alone(sp, parted["sp"])
                sp.wait_ge(scored, START + blk * TILES + t + 1)
                load_x(blk * TILES + t + 2, t % 2)

            def first_tiles(blk):
                sp.wait_ge(rot_done, rot_tiles * blk)
                alone(sp, parted["sp"])
                load_cs(blk)
                for m in range(QK_RING):
                    load_qk(blk, m)

            for dst, src in ((feat_w, features), (phases, phase)):
                sp.dma_start(dst[:], src).then_inc(feat_in, 16)
            load_cs(0)
            for m in range(QK_RING):
                load_qk(0, m)
            for dst, src in ((vb, v_bias), (own, own_token), (wr, router), (br, router_bias)):
                sp.dma_start(dst[:], src).then_inc(consts_in, 16)
            sp.dma_start(signs, bias_signs).then_inc(consts_in, 16)
            for m in range(QK_RING, rot_tiles):
                reload_qk(0, m)
                if m == QK_RING + 1:
                    for k in range(2):
                        sp.dma_start(xr[k][:], w_o_t[k * P:(k + 1) * P, :]).then_inc(w_in[k], 16)
                    sp.dma_start(y[0][0:2, :], o_bias).then_inc(consts_in, 16)
                if m == QK_RING + 2:
                    load_v(0)
            first_tiles(1)
            for k in range(2, KT):
                sp.wait_ge(w_split, k - 1)
                sp.dma_start(xr[k % 2][:], w_o_t[k * P:(k + 1) * P, :]).then_inc(w_in[k % 2], 16)
            for b in range(2):
                sp.wait_ge(w_split, KT - 1 + b)
                load_x(b, b)

            def chunk(blk, more, ahead):
                if more:
                    sp.wait_ge(ctx_done, SUPERS * (blk + 1))
                    alone(sp, parted["sp"])
                    load_v(blk + 1)
                for j in range(HALVES * LAST_TILE):
                    t = j // HALVES
                    if more:
                        for m in range(QK_RING, rot_tiles):
                            if first_unit(max(m - QK_RING - ROT_RING + 1, 0)) in units_of(j):
                                reload_qk(blk + 1, m)
                    if t and j % HALVES == 0:
                        store_x1(blk, t - 1)
                    if t and j % HALVES == HALVES - 1 and (more or t - 1 < TILES - 2):
                        next_x(blk, t - 1)
                if ahead:
                    first_tiles(blk + 2)
                for t in (LAST_TILE - 1, LAST_TILE):
                    store_x1(blk, t)
                    if more:
                        next_x(blk, t)
            with sp.Fori(0, blocks - 2) as i:
                chunk(i, True, True)
            chunk(blocks - 2, True, False)
            chunk(blocks - 1, False, False)
            sp.wait_ge(score_step, 4)
            sp.dma_start(score_out, scores[:]).then_inc(score_stored, 16)
            sp.dma_start(scale_out.rearrange("(p n) c -> p n c", p=P), scales[:]).then_inc(score_stored, 16)
            for b in range(2):
                sp.wait_ge(x1_stored[b], 16 * blocks * TILES // 2)
            sp.wait_ge(score_stored, 32)

        @block.gpsimd
        def _(pool):
            nc.gpsimd.memset(neg_half[:], -0.5).then_inc(rstd_step, 1)

            def scale_of(n):
                pool.wait_ge(stat1, START + 3 * n + 3)
                pool.wait_ge(rstd_step, 3 * n + 1)
                alone(pool, parted["pool"])
                nc.gpsimd.tensor_scalar(var_eps[:], moments1[:, 1:2], LN_EPS, None, ALU.add).then_inc(rstd_step, 1)
                pool.wait_ge(rstd_step, 3 * n + 2)
                pool.wait_ge(y_normed, HEAD_START + HALVES * n)
                alone(pool, parted["pool"])
                nc.gpsimd.tensor_tensor(rstd[:], var_eps[:], neg_half[:], ALU.pow).then_inc(rstd_step, 1)
                pool.wait_ge(rstd_step, 3 * n + 3)
                alone(pool, parted["pool"])
                nc.gpsimd.tensor_scalar(shift[:], moments1[:, 0:1], rstd[:], -1.0, ALU.mult, ALU.mult).then_inc(rstd_step, 1)

            def sine_part(blk, m):
                pool.wait_ge(qk_loaded[m % QK_RING], 80 * (blk * (rot_tiles // QK_RING) + m // QK_RING + 1))
                if m == 0:
                    pool.wait_ge(cs_in, 32 * (blk + 1))
                    alone(pool, parted["pool"])
                swap = qk_swap[m % QK_RING]
                nc.gpsimd.tensor_tensor(swap[:], swap[:], cs[:, 1, :], ALU.mult).then_inc(sin_done, 1)

            def add_v_bias(blk, piece):
                pool.wait_ge(v_in, 16 * V_PIECES * (blk + 1))
                n = GROUPS // V_PIECES
                v = vg[:, piece * n:(piece + 1) * n, :]
                nc.gpsimd.tensor_tensor(v, v, vb[:].unsqueeze(1).to_broadcast([P, n, HEAD]), ALU.add).then_inc(v_ready, 1)

            def residual(blk, t):
                b = t % 2
                pool.wait_ge(y_normed, HEAD_START + HALVES * (blk * TILES + t + 1))
                pool.wait_ge(x_loaded[b], 16 * (blk * 2 + t // 2 + 1))
                nc.gpsimd.tensor_tensor(xr[b][:], xr[b][:], y[b][:], ALU.add).then_inc(x1_done, 1)

            for m in range(QK_RING):
                sine_part(0, m)
            for u in range(UNITS):
                for m in rotations_for(u, 1):
                    sine_part(0, m)
            pool.wait_ge(consts_in, 16 * 6)
            for piece in range(V_PIECES):
                add_v_bias(0, piece)

            for m in range(QK_RING):
                sine_part(1, m)

            def chunk(blk, more, ahead):
                for j in range(HALVES * LAST_TILE):
                    t = j // HALVES
                    if more:
                        for u in units_of(j):
                            for m in rotations_for(u, 1):
                                sine_part(blk + 1, m)
                    if t and j % HALVES == 0:
                        residual(blk, t - 1)
                    if more and 1 <= j <= V_PIECES:
                        add_v_bias(blk + 1, j - 1)
                    if j % HALVES == HALVES - 1:
                        scale_of(blk * TILES + t)
                residual(blk, LAST_TILE - 1)
                if ahead:
                    for m in range(QK_RING):
                        sine_part(blk + 2, m)
                scale_of(blk * TILES + LAST_TILE)
                residual(blk, LAST_TILE)
            with pool.Fori(0, blocks - 2) as i:
                chunk(i, True, True)
            chunk(blocks - 2, True, False)
            chunk(blocks - 1, False, False)
            pool.wait_ge(kept, 3 * blocks)
            nc.gpsimd.tensor_scalar(variances[:], variances[:], LN_EPS, None, ALU.add).then_inc(score_step, 1)
            pool.wait_ge(score_step, 1)
            nc.gpsimd.tensor_tensor(scales[:, :, 0], variances[:], neg_half[:].to_broadcast([P, blocks * TILES]), ALU.pow).then_inc(score_step, 1)

        @block.vector
        def _(dve):
            dve.sem_inc(ctx_lo_done, START)
            dve.sem_inc(stat1, START)
            dve.sem_inc(stat2, START)
            dve.sem_inc(scored, START)

            def rotate(blk, m):
                dve.wait_ge(qk_loaded[m % QK_RING], 80 * (blk * (rot_tiles // QK_RING) + m // QK_RING + 1))
                if m == 0:
                    dve.wait_ge(cs_in, 32 * (blk + 1))
                if m >= 2 or not (isinstance(blk, int) and blk == 0):
                    dve.wait_ge(rot_done, rot_tiles * blk + m - 1)
                    alone(dve, parted["dve"])
                nc.vector.tensor_tensor(q_cos[m % 2][:], qk_in[m % QK_RING][:], cs[:, 0, :], ALU.mult).then_inc(cos_done, 1)
                for s in (cos_done, sin_done):
                    dve.wait_ge(s, rot_tiles * blk + m + 1)
                if m >= ROT_RING or not (isinstance(blk, int) and blk == 0):
                    dve.wait_ge(p_done, UNITS * blk + readers_before(m))
                    alone(dve, parted["dve"])
                nc.vector.tensor_tensor(rotated[m % ROT_RING][:], q_cos[m % 2][:], qk_swap[m % QK_RING][:],
                                        ALU.add).then_inc(rot_done, 1)

            def fraction(blk, u):
                e = UNITS * blk + u
                dve.wait_ge(turn_done, e + 1)
                dve.wait_ge(frac_done, e)
                nc.vector.tensor_scalar(whole[:], turns[u % 2][:], ROUND, ROUND, ALU.add, ALU.subtract).then_inc(whole_done, 1)
                dve.wait_ge(whole_done, e + 1)
                nc.vector.tensor_tensor(turns[u % 2][:], turns[u % 2][:], whole[:], ALU.subtract).then_inc(frac_done, 1)

            def units(blk, which):
                for u in which:
                    for m in rotations_for(u):
                        rotate(blk, m)
                    fraction(blk, u)

            def y_stats(n, t, h):
                dve.wait_ge(y_done, HALVES * n + h + 1)
                dve.wait_ge(stat1, START + 3 * n)
                nc.vector.bn_stats(stats1[:, h, :], y_ps[t % 2][h][:]).then_inc(stat1, 1)
                if h == HALVES - 1:
                    dve.wait_ge(stat1, START + 3 * n + 2)
                    dve.wait_ge(rstd_step, 3 * n + 1)
                    alone(dve, parted["dve"])
                    nc.vector.bn_aggr(moments1[:], stats1[:]).then_inc(stat1, 1)

            def x1_stats(blk, t):
                n = blk * TILES + t
                dve.wait_ge(x1_done, n + 1)
                dve.wait_ge(stat2, START + 3 * n)
                alone(dve, parted["dve"])
                for c in range(HALVES):
                    nc.vector.bn_stats(stats2[:, c, :], xr[t % 2][:, c * 512:(c + 1) * 512]).then_inc(stat2, 1)
                dve.wait_ge(stat2, START + 3 * n + 2)
                alone(dve, parted["dve"])
                nc.vector.bn_aggr(moments2[:, t, :], stats2[:]).then_inc(stat2, 1)

            def router(blk, t):
                n = blk * TILES + t
                dve.wait_ge(stat2, START + 3 * n + 3)
                nc.vector.scalar_tensor_tensor(out=y[t % 2][:], in0=xr[t % 2][:], scalar=moments2[:, t, 0:1], in1=wr[:],
                                               op0=ALU.subtract, op1=ALU.mult, accum_out=raw[:, t:t + 1]).then_inc(scored, 1)

            def keep(blk):
                dve.wait_ge(scored, START + TILES * (blk + 1))
                nc.vector.tensor_copy(scores[:, bass.ds(blk * TILES, TILES)], raw[:]).then_inc(kept, 1)
                nc.vector.tensor_copy(variances[:, bass.ds(blk * TILES, TILES)], moments2[:, :, 1]).then_inc(kept, 1)
                nc.vector.tensor_copy(means[:, bass.ds(blk * TILES, TILES)], moments2[:, :, 0]).then_inc(kept, 1)

            def mask(blk, s):
                e = SUPERS * blk + s
                dve.wait_ge(att_done, e + 1)
                if s >= 2:
                    dve.wait_ge(ctx_done, e - 1)
                for r in range(2):
                    src = att_ps[s % 2][r][:].rearrange("p (gh t a) -> p gh t a", t=GROUP // 2, a=2)
                    dst = att[s % 2][:, :, :, :, r::2].rearrange("p a t g h -> p (g h) t a")
                    mine = own[:].rearrange("p (t a) -> p t a", a=2).unsqueeze(1).to_broadcast([P, 4 * q_tiles, GROUP // 2, 2])
                    last = nc.vector.tensor_tensor(dst, src, mine, ALU.mult)
                last.then_inc(masked, 1)

            def low(blk, s):
                e = SUPERS * blk + s
                dve.wait_ge(ctx_hi_done, e + 1)
                at = (slice(None), slice(None), slice(4 * (s % SPT), 4 * (s % SPT) + 4))
                nc.vector.scalar_tensor_tensor(out=ctx_lo[s // SPT][at], in0=pair_ps[s % 2][:].rearrange("p (g c) -> p c g", g=4),
                                               scalar=feature_scale, in1=ctx_hi[s // SPT][at].bitcast(F32),
                                               op0=ALU.mult, op1=ALU.subtract).then_inc(ctx_lo_done, 1)

            def attention(blk, between):
                mask(blk, 0)
                for s in range(SUPERS):
                    if s + 1 < SUPERS:
                        mask(blk, s + 1)
                    low(blk, s)
                    between(s)

            def split_wo(k):
                dve.wait_ge(w_hi_done, k + 1)
                nc.vector.tensor_tensor(wo_lo[:, k, :], xr[k % 2][:], wo_hi[:, k, :].bitcast(F32), ALU.subtract).then_inc(w_split, 1)

            for m in range(ROT_RING):
                rotate(0, m)
            units(0, range(UNITS))
            dve.wait_ge(signs_done, 2)
            nc.vector.scalar_tensor_tensor(out=bias_r[:], in0=y[0][0:2, :], scalar=signs[:, 0:1], in1=bias_hi.bitcast(F32),
                                           op0=ALU.mult, op1=ALU.subtract).then_inc(bias_done, 1)
            assert KT == SUPERS
            def first_between(s):
                split_wo(s)
                if s < ROT_RING:
                    rotate(1, s)
            attention(0, first_between)

            def wo_tiles(blk, more):
                for j in range(HALVES * LAST_TILE):
                    t = j // HALVES
                    if more:
                        units(blk + 1, units_of(j))
                    if t and j % HALVES == HALVES - 1:
                        x1_stats(blk, t - 1)
                        router(blk, t - 1)
                    y_stats(blk * TILES + t, t, j % HALVES)

            def last_tile(blk):
                for t in (LAST_TILE - 1, LAST_TILE):
                    if t == LAST_TILE:
                        for h in range(HALVES):
                            y_stats(blk * TILES + t, t, h)
                    x1_stats(blk, t)
                    router(blk, t)
                keep(blk)

            def chunk(blk, ahead):
                def between(s):
                    if s == 1:
                        x1_stats(blk, LAST_TILE - 1)
                    if s == 2:
                        router(blk, LAST_TILE - 1)
                    if s == (WO_SUPERS + 1) // 2:
                        y_stats(blk * TILES + LAST_TILE, LAST_TILE, 0)
                    if s == WO_SUPERS:
                        y_stats(blk * TILES + LAST_TILE, LAST_TILE, 1)
                    if ahead and s in ROTATE_AT:
                        rotate(blk + 2, ROTATE_AT.index(s))
                wo_tiles(blk, True)
                attention(blk + 1, between)
                x1_stats(blk, LAST_TILE)
                router(blk, LAST_TILE)
                keep(blk)
            with dve.Fori(0, blocks - 2) as i:
                chunk(i, True)
            chunk(blocks - 2, False)
            wo_tiles(blocks - 1, False)
            last_tile(blocks - 1)
            dve.wait_ge(score_step, 2)
            dve.wait_ge(kept, 3 * blocks)
            nc.vector.scalar_tensor_tensor(out=scales[:, :, 1], in0=means[:], scalar=-1.0, in1=scales[:, :, 0],
                                           op0=ALU.mult, op1=ALU.mult)
            nc.vector.tensor_tensor(scores[:], scores[:], scales[:, :, 0], ALU.mult).then_inc(score_step, 1)
            dve.wait_ge(score_step, 3)
            nc.vector.tensor_scalar(scores[:], scores[:], br[:], None, ALU.add).then_inc(score_step, 1)

        @block.scalar
        def _(act):
            act.sem_inc(y_normed, HEAD_START)
            act.wait_ge(feat_in, 32)

            def sine(blk, u):
                act.wait_ge(frac_done, UNITS * blk + u + 1)
                dst = kf[:, :, u] if u < KV_HEADS else qf[:, u - KV_HEADS, :]
                nc.scalar.activation(dst, turns[u % 2][:], ACT.Sin, scale=TWO_PI).then_inc(feat_done, 1)

            def unit(blk, u):
                act.wait_ge(p_done, UNITS * blk + u + 1)
                if u >= 2:
                    act.wait_ge(feat_done, UNITS * blk + u - 1)
                nc.scalar.activation(turns[u % 2][:], pair_ps[u % 2][:], ACT.Identity, bias=phases[:],
                                     scale=0.15915494309189535).then_inc(turn_done, 1)
                if u:
                    sine(blk, u - 1)
                if u == UNITS - 1:
                    sine(blk, u)

            def normalise(blk, t):
                n = blk * TILES + t
                act.wait_ge(rstd_step, 3 * n + 4)
                act.wait_ge(scored, START + n - 1)
                alone(act, parted["act"])
                for h in range(HALVES):
                    nc.scalar.activation(y[t % 2][:, h * 512:(h + 1) * 512], y_ps[t % 2][h][:], ACT.Identity, bias=shift[:],
                                         scale=rstd[:]).then_inc(y_normed, 1)

            def attention(blk, after):
                for s in range(SUPERS):
                    e = SUPERS * blk + s
                    act.wait_ge(ctx_done, e + 1)
                    nc.scalar.activation(ctx_hi[s // SPT][:, :, 4 * (s % SPT):4 * (s % SPT) + 4],
                                         pair_ps[s % 2][:].rearrange("p (g c) -> p c g", g=4), ACT.Copy,
                                         scale=feature_scale).then_inc(ctx_hi_done, 1)
                    after(s)

            def split_wo(k):
                act.wait_ge(w_in[k % 2], 16 * (k // 2) + 16)
                nc.scalar.activation(wo_hi[:, k, :], xr[k % 2][:], ACT.Copy).then_inc(w_hi_done, 1)

            for u in range(UNITS):
                unit(0, u)
            act.wait_ge(consts_in, 16 * 6)
            nc.scalar.activation(ones_r[:], signs[:, 1:1 + P], ACT.Copy).then_inc(signs_done, 1)
            nc.scalar.activation(bias_hi, y[0][0:2, :], ACT.Copy).then_inc(signs_done, 1)
            attention(0, split_wo)

            def wo_tiles(blk, more):
                for j in range(HALVES * LAST_TILE):
                    t = j // HALVES
                    which = units_of(j) if more else ()
                    for u in which[:2]:
                        unit(blk + 1, u)
                    if t and j % HALVES == 0:
                        normalise(blk, t - 1)
                    for u in which[2:]:
                        unit(blk + 1, u)

            with act.Fori(0, blocks - 1) as i:
                def after(s):
                    if s == WO_SUPERS:
                        act.wait_ge(y_done, HALVES * TILES * (i + 1))
                    if s == SUPERS - 1:
                        normalise(i, LAST_TILE)
                wo_tiles(i, True)
                normalise(i, LAST_TILE - 1)
                attention(i + 1, after)
            wo_tiles(blocks - 1, False)
            normalise(blocks - 1, LAST_TILE - 1)
            normalise(blocks - 1, LAST_TILE)

        @block.tensor
        def _(pe):
            pe.wait_ge(feat_in, 32)

            def unit(blk, u):
                pe.wait_ge(rot_done, rot_tiles * blk + rotated_of(u) + 1)
                if u >= 2:
                    pe.wait_ge(turn_done, UNITS * blk + u - 1)
                kind = 1 + u % 2 if u < KV_HEADS else 0
                nc.tensor.matmul(pair_ps[u % 2][:], feat_w[:, kind, :], rotated[rotated_of(u) % ROT_RING][:], start=True,
                                 stop=True).then_inc(p_done, 1)

            def scores_of(blk, s):
                e = SUPERS * blk + s
                if s >= 2:
                    pe.wait_ge(masked, e - 1)
                for r in range(2):
                    half = slice(r * HEAD, (r + 1) * HEAD)
                    for g in range(4):
                        tok = slice((4 * s + g) * GROUP, (4 * s + g + 1) * GROUP)
                        last = nc.tensor.matmul(att_ps[s % 2][r][:, g * P:(g + 1) * P],
                                                kf[half, tok, :].rearrange("p t g -> p (t g)"), qf[half, :, tok],
                                                start=True, stop=True)
                last.then_inc(att_done, 1)

            def context_of(blk, s):
                e = SUPERS * blk + s
                pe.wait_ge(masked, e + 1)
                pe.wait_ge(ctx_lo_done, START + e - 1)
                for g in range(4):
                    for a in range(2):
                        last = nc.tensor.matmul(pair_ps[s % 2][a * HEAD:(a + 1) * HEAD, g * P:(g + 1) * P], vg[:, 4 * s + g, :],
                                                att[s % 2][:, a, :, g, :], start=True, stop=True)
                last.then_inc(ctx_done, 1)

            def attention(blk, among):
                among(0)
                pe.wait_ge(feat_done, UNITS * (blk + 1))
                pe.wait_ge(v_ready, V_PIECES * (blk + 1))
                scores_of(blk, 0)
                among(1)
                if not isinstance(blk, int) or blk:
                    pe.wait_ge(y_normed, HEAD_START + HALVES * (TILES * blk - 1))
                for s in range(SUPERS):
                    if s + 1 < SUPERS:
                        scores_of(blk, s + 1)
                    if s:
                        among(s + 1)
                    context_of(blk, s)

            def wo_products(blk, t, h, ks):
                cols = slice(h * 512, (h + 1) * 512)
                if ks[0] == 0:
                    pe.wait_ge(ctx_lo_done, START + SUPERS * blk + SPT * (t + 1))
                    pe.wait_ge(y_normed, HEAD_START + HALVES * (blk * TILES + t - 2) + h + 1)
                    nc.tensor.matmul(y_ps[t % 2][h][:], ones_r[:], bias_r[:, cols], start=True, stop=False)
                for k in ks:
                    rows = slice(k * HEADS, (k + 1) * HEADS)
                    a_hi = ctx_hi[t][:, rows, :].rearrange("p h g -> p (h g)")
                    a_lo = ctx_lo[t][:, rows, :].rearrange("p h g -> p (h g)")
                    for s, (a, b) in enumerate(split_passes(a_hi, a_lo, wo_hi[:, k, cols], wo_lo[:, k, cols])):
                        last = nc.tensor.matmul(y_ps[t % 2][h][:], a, b, start=False, stop=(k == KT - 1 and s == 2))
                    if k == KT - 1:
                        last.then_inc(y_done, 1)

            def wo_tiles(blk, more):
                for j in range(HALVES * LAST_TILE):
                    which = units_of(j)
                    for k in range(KT):
                        wo_products(blk, j // HALVES, j % HALVES, (k,))
                        if more:
                            if j == 0 and k == KT - 1 - 2 * (len(which) - 1):
                                pe.wait_ge(ctx_lo_done, START + SUPERS * (blk + 1))
                            for i, u in enumerate(which):
                                if k == (KT * (i + 1) // len(which) - 1 if j else KT - 1 - 2 * (len(which) - 1 - i)):
                                    unit(blk + 1, u)

            def last_tile(blk, which):
                for n in which:
                    wo_products(blk, LAST_TILE, n // KT, (n % KT,))

            for u in range(UNITS):
                unit(0, u)
            attention(0, lambda s: None)
            pe.wait_ge(w_split, KT)
            pe.wait_ge(bias_done, 1)
            with pe.Fori(0, blocks - 1) as i:
                def among(s):
                    if s <= WO_SUPERS:
                        last_tile(i, range(WO_UP_TO[s], WO_UP_TO[s + 1]))
                wo_tiles(i, True)
                attention(i + 1, among)
            wo_tiles(blocks - 1, False)
            last_tile(blocks - 1, range(HALVES * KT))


def route_phase(nc, score_in, order_masks, token_ids, count_up, chosen, chosen_at, keep):
    lanes, per_lane = score_in.shape
    tokens = lanes * per_lane
    slots_a = keep // P
    SIGN = -2 ** 31
    DIGIT = 4
    VALUES = 2 ** DIGIT
    ROUNDS = 32 // DIGIT
    ABOVE = 2.0 * VALUES
    HOT_PIECES = 4
    PIECE = per_lane // HOT_PIECES

    with ExitStack() as ctx:
        sb = lambda n, s, d=F32: ctx.enter_context(nc.sbuf_tensor("r_" + n, s, d))
        ps = lambda n, s: ctx.enter_context(nc.psum_tensor("r_" + n, s, F32))
        sem = lambda n: ctx.enter_context(nc.semaphore("r_" + n))
        own = sb("own", [P, per_lane])
        masks = sb("masks", [P, 4, P])
        ids = sb("ids", [P, per_lane])
        up = sb("up", [P, P])
        flip = sb("flip", [P, per_lane], I32)
        key = sb("key", [P, per_lane], I32)
        digit_i = sb("digit_i", [P, ROUNDS, per_lane], I32)
        digit = sb("digit", [P, ROUNDS, per_lane])
        alive = sb("alive", [P, per_lane])
        higher = sb("higher", [P, per_lane])
        rank = sb("rank", [P, per_lane])
        at_least = sb("at_least", [P, VALUES, per_lane])
        lane_count = sb("lane_count", [P, VALUES])
        enough = sb("enough", [P, VALUES])
        best = sb("best", [P, 1])
        ones = sb("ones", [P, per_lane])
        over = sb("over", [P, per_lane])
        tie = sb("tie", [P, per_lane])
        incl = sb("incl", [P, per_lane])
        excl = sb("excl", [P, per_lane])
        total = sb("total", [P, per_lane])
        n_over = sb("n_over", [P, 1])
        need = sb("need", [P, 1])
        sel = sb("sel", [P, per_lane])
        slot_i = sb("slot_i", [P, per_lane], I32)
        part_i = sb("part_i", [P, 2, per_lane], I32)
        part = sb("part", [P, 2, per_lane])
        picked = sb("picked", [P, per_lane])
        place = sb("place", [P, 2, slots_a], I32)
        hot_b = sb("hot_b", [P, per_lane, P], F32R)
        in_a = sb("in_a", [P, per_lane, slots_a])
        hot_a = sb("hot_a", [P, per_lane, slots_a], F32R)
        rank_ps = ps("rank_ps", [P, per_lane])
        over_ps = ps("over_ps", [P, 1])
        count_ps = ps("count_ps", [P, VALUES])
        chosen_ps = ps("chosen_ps", [P, slots_a])

        loaded = sem("loaded")
        step = sem("step")
        counted = sem("counted")
        totalled = sem("totalled")
        rank_ready = sem("rank_ready")
        ranked = sem("ranked")
        over_ready = sem("over_ready")
        over_summed = sem("over_summed")
        hot_ready = sem("hot_ready")
        listed = sem("listed")
        block = ctx.enter_context(nc.Block())

        @block.sync
        def _(sp):
            for dst, src in ((own, score_in), (masks, order_masks), (ids, token_ids), (up, count_up)):
                sp.dma_start(dst[:], src).then_inc(loaded, 16)

        @block.vector
        def _(dve):
            done = [0]

            def link(instruction):
                done[0] += 1
                instruction.then_inc(step, 1)
                dve.wait_ge(step, done[0])

            dve.wait_ge(loaded, 16 * 4)
            nc.vector.memset(ones[:], 1.0)
            nc.vector.memset(alive[:], 1.0)
            link(nc.vector.memset(higher[:], 0.0))
            link(nc.vector.tensor_scalar(flip[:], own[:].bitcast(I32), 31, SIGN, ALU.arith_shift_right, ALU.bitwise_or))
            link(nc.vector.tensor_tensor(key[:], own[:].bitcast(I32), flip[:], ALU.bitwise_xor))
            for r in range(ROUNDS):
                last = nc.vector.tensor_scalar(digit_i[:, r, :], key[:], 32 - DIGIT * (r + 1), VALUES - 1,
                                               ALU.logical_shift_right, ALU.bitwise_and)
            link(last)
            link(nc.vector.tensor_copy(digit[:], digit_i[:]))
            for r in range(ROUNDS):
                link(nc.vector.scalar_tensor_tensor(out=rank[:], in0=digit[:, r, :], scalar=1.0, in1=alive[:], op0=ALU.add, op1=ALU.mult))
                link(nc.vector.tensor_tensor(rank[:], rank[:], higher[:], ALU.add))
                link(nc.vector.tensor_tensor(at_least[:], rank[:].unsqueeze(1).to_broadcast([P, VALUES, per_lane]),
                                             up[:, 1:1 + VALUES].unsqueeze(2).to_broadcast([P, VALUES, per_lane]), ALU.is_ge))
                nc.vector.tensor_reduce(lane_count[:], at_least[:], AX_X, ALU.add).then_inc(counted, 1)
                dve.wait_ge(totalled, r + 1)
                link(nc.vector.tensor_scalar(enough[:], count_ps[:], float(keep), 0.0, ALU.is_ge, ALU.add, accum_out=best[:]))
                if r + 1 < ROUNDS:
                    nc.vector.tensor_scalar(higher[:], rank[:], best[:], ABOVE, ALU.is_gt, ALU.mult)
                    link(nc.vector.tensor_scalar(alive[:], rank[:], best[:], None, ALU.is_equal))
            link(nc.vector.tensor_scalar(over[:], rank[:], best[:], 0.0, ALU.is_gt, ALU.add, accum_out=n_over[:]))
            nc.vector.tensor_scalar(tie[:], rank[:], best[:], None, ALU.is_equal).then_inc(over_ready, 1)

            def rank_operands(flags):
                link(nc.vector.tensor_tensor_scan(incl[:], ones[:], flags[:], 0.0, ALU.mult, ALU.add))
                link(nc.vector.tensor_tensor(excl[:], incl[:], flags[:], ALU.subtract))
                nc.vector.tensor_scalar(total[:], flags[:], 0.0, incl[:, per_lane - 1:per_lane], ALU.mult,
                                        ALU.add).then_inc(rank_ready, 1)

            dve.wait_ge(over_ready, 1)
            rank_operands(tie)
            dve.wait_ge(over_summed, 1)
            link(nc.vector.tensor_scalar(need[:], over_ps[:], -1.0, float(keep), ALU.mult, ALU.add))
            dve.wait_ge(ranked, 1)
            link(nc.vector.tensor_scalar(sel[:], rank_ps[:], need[:], None, ALU.is_lt))
            link(nc.vector.tensor_tensor(sel[:], sel[:], tie[:], ALU.mult))
            link(nc.vector.tensor_tensor(sel[:], sel[:], over[:], ALU.add))
            rank_operands(sel)
            dve.wait_ge(ranked, 2)
            link(nc.vector.tensor_copy(slot_i[:], rank_ps[:]))
            link(nc.vector.tensor_scalar(part_i[:, 0, :], slot_i[:], P - 1, None, ALU.bitwise_and))
            link(nc.vector.tensor_scalar(part_i[:, 1, :], slot_i[:], P.bit_length() - 1, None, ALU.arith_shift_right))
            link(nc.vector.tensor_copy(part[:], part_i[:]))
            link(nc.vector.tensor_tensor(picked[:], sel[:], ids[:], ALU.mult))
            link(nc.vector.tensor_tensor(in_a[:], up[:, 0:slots_a].unsqueeze(1).to_broadcast([P, per_lane, slots_a]),
                                         part[:, 1, :].unsqueeze(2).to_broadcast([P, per_lane, slots_a]), ALU.is_equal))
            nc.vector.tensor_tensor(hot_a[:], in_a[:], picked[:].unsqueeze(2).to_broadcast([P, per_lane, slots_a]), ALU.mult)
            for piece in range(HOT_PIECES):
                n = slice(piece * PIECE, (piece + 1) * PIECE)
                nc.vector.tensor_tensor(hot_b[:, n, :], up[:].unsqueeze(1).to_broadcast([P, PIECE, P]),
                                        part[:, 0, n].unsqueeze(2).to_broadcast([P, PIECE, P]), ALU.is_equal).then_inc(hot_ready, 1)
            dve.wait_ge(listed, 1)
            link(nc.vector.tensor_copy(chosen[:], chosen_ps[:]))
            row_bits, tile_bits = (GROUP // 2).bit_length() - 1, per_lane.bit_length() - 1
            nc.vector.tensor_scalar(place[:, 0, :], chosen[:], 2 ** row_bits - 1, tile_bits, ALU.bitwise_and, ALU.logical_shift_left)
            nc.vector.tensor_scalar(place[:, 1, :], chosen[:], row_bits, per_lane - 1, ALU.logical_shift_right, ALU.bitwise_and)
            link(nc.vector.tensor_scalar(chosen_at[:], chosen[:], -2 ** (row_bits + tile_bits), None, ALU.bitwise_and))
            for j in range(2):
                link(nc.vector.tensor_tensor(chosen_at[:], chosen_at[:], place[:, j, :], ALU.bitwise_or))

        @block.tensor
        def _(pe):
            for r in range(ROUNDS):
                pe.wait_ge(counted, r + 1)
                nc.tensor.matmul(count_ps[:], masks[:, 3, :], lane_count[:], start=True, stop=True).then_inc(totalled, 1)
            pe.wait_ge(over_ready, 1)
            nc.tensor.matmul(over_ps[:], masks[:, 3, :], n_over[:], start=True, stop=True).then_inc(over_summed, 1)
            for n in range(2):
                pe.wait_ge(rank_ready, n + 1)
                nc.tensor.matmul(rank_ps[:], masks[:, 0, :], total[:], start=True, stop=False)
                nc.tensor.matmul(rank_ps[:], masks[:, 1, :], excl[:], start=False, stop=False)
                nc.tensor.matmul(rank_ps[:], masks[:, 2, :], (tie, sel)[n][:], start=False, stop=True).then_inc(ranked, 1)
            for n in range(per_lane):
                if n % PIECE == 0:
                    pe.wait_ge(hot_ready, n // PIECE + 1)
                last = nc.tensor.matmul(chosen_ps[:], hot_b[:, n, :], hot_a[:, n, :], start=(n == 0), stop=(n == per_lane - 1))
            last.then_inc(listed, 1)


def ffn_phase(nc, x1, x1_scale, w1, b1, w2, b2_rows, identity, chosen, chosen_at, out, keep):
    width, hidden = w1.shape
    KT = width // P
    PASSES = 2
    TT = keep // PASSES // P
    CHUNK = 2 * P
    FT = CHUNK // P
    chunks = hidden // CHUNK
    TB = TT * P // TOK_BLOCK
    steps = chunks * TB
    HALVES = width // 512
    OPS = TILES * HALVES
    O_BANKS = 4
    RING = 3
    RES_RING = 2
    PIECES = 4
    HALF_K = KT // 2
    LAG = 2
    assert TB == 2 and OPS == 2 * TILES and TT == 2 * TILES

    with ExitStack() as ctx:
        sb = lambda n, s, d=F32: ctx.enter_context(nc.sbuf_tensor("f_" + n, s, d))
        ps = lambda n, s: ctx.enter_context(nc.psum_tensor("f_" + n, s, F32))
        sem = lambda n: ctx.enter_context(nc.semaphore("f_" + n))
        xt_hi = sb("xt_hi", [P, KT, TT * P], F32R)
        xt_lo = sb("xt_lo", [P, KT, TT * P], F32R)
        acc = sb("acc", [P, TT, width])
        w1_hi = [sb(f"w1_hi{b}", [P, KT, CHUNK], F32R) for b in range(2)]
        w1_lo = [sb(f"w1_lo{b}", [P, KT, CHUNK], F32R) for b in range(2)]
        w2_hi = [sb(f"w2_hi{b}", [P, FT, width], F32R) for b in range(2)]
        w2_lo = [sb(f"w2_lo{b}", [P, FT, width], F32R) for b in range(2)]
        h_hi = [sb(f"h_hi{b}", [P, FT, TOK_BLOCK], F32R) for b in range(2)]
        h_lo = [sb(f"h_lo{b}", [P, FT, TOK_BLOCK], F32R) for b in range(2)]
        act_out = [sb(f"act_out{f}", [P, TOK_BLOCK]) for f in range(FT)]
        raw = sb("raw", [P, width])
        rows = [sb(f"rows{b}", [P, width]) for b in range(RING)]
        res = [sb(f"res{b}", [P, width]) for b in range(RES_RING)] + rows
        ident = sb("ident", [P, P])
        bias = sb("bias", [P, hidden // P])
        neg_half = sb("neg_half", [P, 1])
        h_ps = [[ps(f"h_ps{b}{f}", [P, TOK_BLOCK]) for f in range(FT)] for b in range(2)]
        o_ps = [ps(f"o_ps{b}", [P, 512]) for b in range(O_BANKS)]
        x_scale = sb("x_scale", [P, PASSES * TT, 2])
        stats = sb("stats", [P, HALVES, 6])
        moments = [sb(f"moments{b}", [P, 2]) for b in range(2)]
        var_eps = sb("var_eps", [P, 1])
        rstd = [sb(f"rstd{b}", [P, 1]) for b in range(2)]
        shift = [sb(f"shift{b}", [P, 1]) for b in range(2)]

        consts_in = sem("consts_in")
        parted = {e: sem(f"parted_{e}") for e in ("pool", "dve", "act", "sp")}
        half_set = sem("half_set")
        first_gathered = [sem(f"first_gathered{u}") for u in range(TT)]
        scales_in = sem("scales_in")
        x_normed = sem("x_normed")
        measured = sem("measured")
        scaled = sem("scaled")
        y_normed = sem("y_normed")
        gathered = [sem(f"gathered{b}") for b in range(RING)]
        turned = sem("turned")
        x_hi = sem("x_hi")
        x_lo = sem("x_lo")
        acc_set = [sem(f"acc_set{b}") for b in range(TB)]
        piece_in = sem("piece_in")
        piece_h = sem("piece_h")
        piece_l = sem("piece_l")
        h_mm = sem("h_mm")
        gelu_done = sem("gelu_done")
        h_h, h_l = sem("h_h"), sem("h_l")
        o_mm = sem("o_mm")
        added = sem("added")
        res_in = [sem(f"res_in{b}") for b in range(RES_RING + RING)]
        summed = sem("summed")
        last_summed = sem("last_summed")
        scattered = [sem(f"scattered{b}") for b in range(RES_RING + RING)]

        w1_v = w1.rearrange("(h k p) (c f) -> c h p k f", h=2, p=P, f=CHUNK)
        w2_v = w2.rearrange("(c j p) d -> c j p d", p=P, j=FT)

        block = ctx.enter_context(nc.Block())

        def per_pass(eng, opening, step, closing):
            for hf in range(PASSES):
                opening(hf)
                with eng.Fori(0, chunks // 2 - 1) as i:
                    for q in range(2 * TB):
                        step(hf, i, q)
                for q in range(TB):
                    step(hf, LAST, q)
                closing(hf)

        def slots(slot, new, which):
            for i in which:
                slot(i, new if new < PASSES else None, new - 1 if new else None)

        LAST = chunks // 2 - 1

        def piece_of(k, cp):
            if k < 2:
                at = (slice(None), slice(k * HALF_K, (k + 1) * HALF_K), slice(None))
                return w1_hi[cp][at], w1_lo[cp][at], raw[:].rearrange("p (k f) -> p k f", k=HALF_K)
            return w2_hi[cp][:, k - 2, :], w2_lo[cp][:, k - 2, :], raw[:]

        def pieces_at(hf, i, q):
            g, cp = chunks * hf + chunk_of(i, q), q // TB
            return ((g + 1, 2 * (q % TB) + 1, 1 - cp), (g + 1, 2, 1 - cp) if q % TB == 0 else (g + 2, 0, cp))

        def exists(g):
            return not isinstance(g, int) or g < chunks * PASSES

        res_ring = [RES_RING] * (PASSES - 1) + [RES_RING + RING]

        def res_use(y, i):
            b = i % res_ring[y]
            return b, sum(t % res_ring[z] == b for z in range(y + 1) for t in range(TT if z < y else i))

        turn_banks = [[t[:].rearrange("p (k n) -> p k n", n=P) for t in pair] for pair in (h_ps[1], o_ps[:2])]

        def turn_of(x, u):
            return u % 2 if x == 0 or u >= TILES else 0

        def last_turn_in(x, u):
            order = [turn_of(e // TT, e % TT) for e in range(TT * x + u)]
            return max([n + 1 for n, b in enumerate(order) if b == turn_of(x, u)], default=0)

        def x_tile(e):
            return acc[:, e, :] if e < TT else rows[(e - TT) % RING][:]

        def chunk_of(i, q):
            return 2 * i + q // TB

        def step_of(i, q):
            return 2 * TB * i + q

        FIRST, SECOND = range(TILES), range(TILES, TT)

        @block.sync
        def _(sp):
            def load(g, c, k):
                w_v, h = (w1_v, k) if k < 2 else (w2_v, k - 2)
                src = w_v[bass.ds(c, 1), h]
                if k < 2:
                    src, dst = src.rearrange("c p k f -> p c k f"), raw[:].rearrange("p (c k f) -> p c k f", c=1, k=HALF_K)
                else:
                    src, dst = src.rearrange("c p d -> p c d"), raw[:].unsqueeze(1)
                sp.dma_start(dst, src).then_inc(piece_in, 16)

            sp.dma_start(ident[:], identity).then_inc(consts_in, 16)
            sp.dma_start(bias[:], b1).then_inc(consts_in, 16)
            for hf in range(PASSES):
                with sp.Fori(0, chunks) as c:
                    for k in range(PIECES):
                        sp.wait_ge(piece_l, START + PIECES * (chunks * hf + c) + k)
                        alone(sp, parted["sp"])
                        load(chunks * hf + c, c, k)

        @block.gpsimd
        def _(pool):
            nc.gpsimd.memset(neg_half[:], -0.5).then_inc(half_set, 1)
            pool.wait_ge(half_set, 1)

            def scale_y(e):
                b = e % 2
                pool.wait_ge(measured, 3 * e + 3)
                if e:
                    pool.wait_ge(scaled, 3 * e)
                nc.gpsimd.tensor_scalar(var_eps[:], moments[b][:, 1:2], LN_EPS, None, ALU.add).then_inc(scaled, 1)
                pool.wait_ge(scaled, 3 * e + 1)
                if e >= 2:
                    pool.wait_ge(y_normed, e - 1)
                nc.gpsimd.tensor_tensor(rstd[b][:], var_eps[:], neg_half[:], ALU.pow).then_inc(scaled, 1)
                pool.wait_ge(scaled, 3 * e + 2)
                nc.gpsimd.tensor_scalar(shift[b][:], moments[b][:, 0:1], rstd[b][:], -1.0, ALU.mult, ALU.mult).then_inc(scaled, 1)

            def gather(dst, tile, done, table=x1, at=chosen):
                pool.indirect_dma_start(out=dst, out_offset=None, in_=table,
                                        in_offset=bass.IndirectOffsetOnAxis(ap=at[:, tile:tile + 1], axis=0)).then_inc(done, 16)

            def gather_x(e):
                if e >= TT + RING:
                    pool.wait_ge(turned, e - RING + 1)
                gather(x_tile(e), e, gathered[(e - TT) % RING] if e >= TT else first_gathered[e])
                if e < TT:
                    gather(x_scale[:, e, :], e, first_gathered[e], x1_scale, chosen_at)

            def gather_res(y, i):
                b, used = res_use(y, i)
                if used:
                    pool.wait_ge(scattered[b], 16 * used)
                gather(res[b][:], TT * y + i, res_in[b])

            def set_acc(tb):
                pool.dma_start(acc[:, tb * TILES:(tb + 1) * TILES, :],
                               b2_rows.unsqueeze(1).to_broadcast([P, TILES, width])).then_inc(acc_set[tb], 16)

            def slot(i, x, y):
                if x and i + RING < TT:
                    gather_x(TT * x + i + RING)
                if y is not None:
                    scale_y(TT * y + i)
                if y is not None and i >= lag(y):
                    finish(y, i - lag(y))

            def lag(y):
                return LAG if y + 1 < PASSES else 1

            def finish(y, i):
                e = TT * y + i
                b, used = res_use(y, i)
                if y + 1 < PASSES:
                    pool.wait_ge(y_normed, e + 1)
                    pool.wait_ge(res_in[b], 16 * (used + 1))
                    nc.gpsimd.tensor_tensor(res[b][:], res[b][:], acc[:, i, :], ALU.add).then_inc(summed, 1)
                    pool.wait_ge(summed, e + 1)
                else:
                    pool.wait_ge(last_summed, i + 1)
                pool.indirect_dma_start(out=out, out_offset=bass.IndirectOffsetOnAxis(ap=chosen[:, e:e + 1], axis=0),
                                        in_=res[b][:], in_offset=None).then_inc(scattered[b], 16)
                if i and i + res_ring[y] - 1 < TT:
                    gather_res(y, i + res_ring[y] - 1)
                if y + 1 < PASSES and i % TILES == TILES - 1:
                    set_acc(i // TILES)

            for new in range(PASSES + 1):
                if new < PASSES:
                    for u in range(RING if new else TT):
                        gather_x(TT * new + u)
                if new:
                    for u in range(res_ring[new - 1]):
                        gather_res(new - 1, u)
                slots(slot, new, range(TT))
                if new == 0:
                    for e in range(TT, PASSES * TT):
                        gather(x_scale[:, e, :], e, scales_in, x1_scale, chosen_at)
                    for tb in range(TB):
                        pool.wait_ge(turned, TILES * (tb + 1))
                        set_acc(tb)
                if new:
                    for i in range(TT - lag(new - 1), TT):
                        finish(new - 1, i)
            for b in range(RES_RING + RING):
                used = sum(res_use(y, i)[0] == b for y in range(PASSES) for i in range(TT))
                pool.wait_ge(scattered[b], 16 * used)

        @block.vector
        def _(dve):
            dve.sem_inc(added, O_BANKS)
            dve.sem_inc(h_l, START)
            dve.sem_inc(piece_l, START)

            def measure_y(y, i):
                e = TT * y + i
                dve.wait_ge(added, O_BANKS + OPS * (steps * (y + 1) - (TB - 1 - i // TILES)))
                if e:
                    dve.wait_ge(measured, 3 * e)
                for c in range(HALVES):
                    nc.vector.bn_stats(stats[:, c, :], acc[:, i, c * 512:(c + 1) * 512]).then_inc(measured, 1)
                dve.wait_ge(measured, 3 * e + 2)
                if e >= 2:
                    dve.wait_ge(scaled, 3 * (e - 1))
                nc.vector.bn_aggr(moments[e % 2][:], stats[:]).then_inc(measured, 1)

            def low_piece(g, k, cp):
                hi, lo, src = piece_of(k, cp)
                dve.wait_ge(piece_h, PIECES * g + k + 1)
                nc.vector.tensor_tensor(lo, src, hi.bitcast(F32), ALU.subtract).then_inc(piece_l, 1)

            def low_h(hf, s, q):
                for f in range(FT):
                    dve.wait_ge(h_h, FT * (steps * hf + s) + f + 1)
                    nc.vector.tensor_tensor(h_lo[q % 2][:, f, :], act_out[f][:], h_hi[q % 2][:, f, :].bitcast(F32),
                                            ALU.subtract).then_inc(h_l, 1)

            def add(hf, s, q, j):
                n = OPS * (steps * hf + s)
                dve.wait_ge(o_mm, START + n + j + 1)
                at = (slice(None), q % TB * TILES + j // HALVES, slice(j % HALVES * 512, (j % HALVES + 1) * 512))
                nc.vector.tensor_tensor(acc[at], o_ps[j % O_BANKS][:], acc[at], ALU.add).then_inc(added, 1)

            def slot(i, x, y):
                if x is not None:
                    dve.wait_ge(x_hi, TT * x + i + 1)
                    for c in range(2):
                        at = (slice(None), slice(c * KT // 2, (c + 1) * KT // 2), slice(i * P, (i + 1) * P))
                        last = nc.vector.tensor_tensor(xt_lo[at], turn_banks[turn_of(x, i)][c], xt_hi[at].bitcast(F32), ALU.subtract)
                    last.then_inc(x_lo, 1)
                if y is not None:
                    measure_y(y, i)
                    if i < TILES:
                        for j in range(2 * i, 2 * i + 2):
                            add(y, steps - 1, TB - 1, j)
                if x is None and i:
                    last_residual(y, i - 1)

            def last_residual(y, i):
                b, used = res_use(y, i)
                dve.wait_ge(y_normed, TT * y + i + 1)
                dve.wait_ge(res_in[b], 16 * (used + 1))
                nc.vector.tensor_tensor(res[b][:], res[b][:], acc[:, i, :], ALU.add).then_inc(last_summed, 1)

            def opening(hf):
                if hf == 0:
                    low_piece(0, 0, 0)
                    slots(slot, 0, FIRST[:2])
                    low_piece(0, 1, 0)
                    slots(slot, 0, FIRST[2:])
                    low_piece(0, 2, 0)
                slots(slot, hf, SECOND[:2])
                if hf == 0:
                    low_piece(0, 3, 0)
                slots(slot, hf, SECOND[2:])
                if hf == 0:
                    low_piece(1, 0, 1)
                low_h(hf, 0, 0)

            def step(hf, i, q):
                s = step_of(i, q)
                one, other = pieces_at(hf, i, q)
                if exists(one[0]):
                    low_piece(*one)
                if exists(other[0]):
                    low_piece(*other)
                low_h(hf, s + 1, q + 1)
                dve.wait_ge(acc_set[q % TB], 16 * (hf + 1))
                dve.wait_ge(added, O_BANKS + OPS * (steps * hf + s))
                alone(dve, parted["dve"])
                for j in range(OPS):
                    add(hf, s, q, j)

            def closing(hf):
                more = hf + 1 < PASSES
                step(hf, LAST, TB)
                one, other = pieces_at(hf, LAST, TB + 1)
                if more:
                    low_piece(*one)
                slots(slot, hf + 1, FIRST)
                if more:
                    low_piece(*other)
                else:
                    slots(slot, hf + 1, SECOND)
                    last_residual(hf, TT - 1)
            per_pass(dve, opening, step, closing)

        @block.scalar
        def _(act):
            act.wait_ge(consts_in, 32)

            def normalise_x(e):
                if e < TT:
                    act.wait_ge(first_gathered[e], 32)
                else:
                    act.wait_ge(gathered[(e - TT) % RING], 16 * (1 + (e - TT) // RING))
                    act.wait_ge(scales_in, 16 * TT * (PASSES - 1))
                nc.scalar.activation(x_tile(e), x_tile(e), ACT.Identity, bias=x_scale[:, e, 1:2],
                                     scale=x_scale[:, e, 0:1]).then_inc(x_normed, 1)

            def normalise_y(e, i):
                act.wait_ge(scaled, 3 * e + 3)
                nc.scalar.activation(acc[:, i, :], acc[:, i, :], ACT.Identity, bias=shift[e % 2][:],
                                     scale=rstd[e % 2][:]).then_inc(y_normed, 1)

            def high_piece(g, k, cp):
                hi, lo, src = piece_of(k, cp)
                act.wait_ge(piece_in, 16 * (PIECES * g + k + 1))
                if not isinstance(g, int) or g:
                    if k < 2:
                        act.wait_ge(h_mm, START + FT * TB * (g - 1))
                    else:
                        act.wait_ge(o_mm, START + OPS * TB * (g - 1))
                    alone(act, parted["act"])
                nc.scalar.activation(hi, src, ACT.Copy).then_inc(piece_h, 1)

            def gelu(hf, s, c, q):
                n = steps * hf + s
                for f in range(FT):
                    act.wait_ge(h_mm, START + FT * n + f + 1)
                    act.wait_ge(h_l, START + FT * (n - 1) + f + 1)
                    alone(act, parted["act"])
                    nc.scalar.activation(act_out[f][:], h_ps[q % 2][f][:], ACT.Gelu_apprx_tanh,
                                         bias=bias[:, bass.ds(c * FT + f, 1)]).then_inc(gelu_done, 1)
                    act.wait_ge(gelu_done, FT * n + f + 1)
                    nc.scalar.activation(h_hi[q % 2][:, f, :], act_out[f][:], ACT.Copy).then_inc(h_h, 1)

            def slot(i, x, y):
                if x is not None:
                    act.wait_ge(turned, TT * x + i + 1)
                    for k in range(2):
                        at = (slice(None), slice(k * KT // 2, (k + 1) * KT // 2), slice(i * P, (i + 1) * P))
                        last = nc.scalar.activation(xt_hi[at], turn_banks[turn_of(x, i)][k], ACT.Copy)
                    last.then_inc(x_hi, 1)
                if y is not None:
                    normalise_y(TT * y + i, i)
                if x is not None and i + RING - 1 < TT:
                    normalise_x(TT * x + i + RING - 1)

            def opening(hf):
                if hf == 0:
                    high_piece(0, 0, 0)
                    for u in range(RING - 1):
                        normalise_x(u)
                    slots(slot, 0, FIRST[:2])
                    high_piece(0, 1, 0)
                    slots(slot, 0, FIRST[2:])
                    high_piece(0, 2, 0)
                slots(slot, hf, SECOND[:2])
                if hf == 0:
                    high_piece(0, 3, 0)
                slots(slot, hf, SECOND[2:])
                if hf == 0:
                    high_piece(1, 0, 1)
                gelu(hf, 0, 0, 0)

            def next_gelu(hf, i, q):
                s = step_of(i, q)
                act.wait_ge(o_mm, START + OPS * (steps * hf + s))
                gelu(hf, s + 1, chunk_of(i, q + 1), q + 1)

            def step(hf, i, q, extra=lambda: None):
                one, other = pieces_at(hf, i, q)
                if exists(one[0]):
                    high_piece(*one)
                extra()
                if exists(other[0]):
                    high_piece(*other)
                next_gelu(hf, i, q)

            def closing(hf):
                more = hf + 1 < PASSES

                def first_rows():
                    for u in range(RING - 1):
                        normalise_x(TT * (hf + 1) + u)
                step(hf, LAST, TB, first_rows if more else lambda: None)
                one, other = pieces_at(hf, LAST, TB + 1)
                if more:
                    high_piece(*one)
                slots(slot, hf + 1, FIRST)
                if more:
                    high_piece(*other)
                else:
                    slots(slot, hf + 1, SECOND)
            per_pass(act, opening, step, closing)

        @block.tensor
        def _(pe):
            pe.sem_inc(o_mm, START)
            pe.sem_inc(h_mm, START)
            pe.wait_ge(consts_in, 32)

            def transpose(x, u):
                e = TT * x + u
                pe.wait_ge(x_normed, e + 1)
                before = last_turn_in(x, u)
                if before:
                    pe.wait_ge(x_lo, before)
                if x:
                    pe.wait_ge(gelu_done, FT * steps * x)
                    if turn_of(x, u):
                        pe.wait_ge(added, O_BANKS + OPS * steps * x)
                for k in range(KT):
                    last = nc.tensor.transpose(turn_banks[turn_of(x, u)][k * 2 // KT][:, k % (KT // 2), :], x_tile(e)[:, k * P:(k + 1) * P], ident[:])
                last.then_inc(turned, 1)

            def first(hf, c, q, beside=()):
                pe.wait_ge(piece_l, START + PIECES * (chunks * hf + c) + 2)
                cols = slice(q % TB * TOK_BLOCK, (q % TB + 1) * TOK_BLOCK)
                b, cp = q % 2, q // TB
                for f in range(FT):
                    for k in range(KT):
                        fs = slice(f * P, (f + 1) * P)
                        for place, u in beside:
                            if place == f * KT + k:
                                transpose(hf, u)
                        for t, (a, w) in enumerate(split_passes(w1_hi[cp][:, k, fs], w1_lo[cp][:, k, fs],
                                                                xt_hi[:, k, cols], xt_lo[:, k, cols])):
                            last = nc.tensor.matmul(h_ps[b][f][:], a, w, start=(k == 0 and t == 0), stop=(k == KT - 1 and t == 2))
                    last.then_inc(h_mm, 1)

            def second(hf, i, q, beside=None):
                n = steps * hf + step_of(i, q)
                c = chunk_of(i, q)
                cp = q // TB
                pe.wait_ge(h_l, START + FT * (n + 1))
                pe.wait_ge(piece_l, START + PIECES * (chunks * hf + c + 1))
                for j in range(OPS):
                    if beside is not None and j % 2 == 0:
                        transpose(beside, j // 2)
                    pe.wait_ge(added, OPS * n + j + 1)
                    rs, cs = slice(j // HALVES * P, (j // HALVES + 1) * P), slice(j % HALVES * 512, (j % HALVES + 1) * 512)
                    for f in range(FT):
                        for t, (a, b) in enumerate(split_passes(h_hi[q % 2][:, f, rs], h_lo[q % 2][:, f, rs],
                                                                w2_hi[cp][:, f, cs], w2_lo[cp][:, f, cs])):
                            last = nc.tensor.matmul(o_ps[j % O_BANKS][:], a, b, start=(f == 0 and t == 0), stop=(f == FT - 1 and t == 2))
                    last.then_inc(o_mm, 1)

            def opening(hf):
                if hf == 0:
                    for u in FIRST:
                        transpose(0, u)
                pe.wait_ge(x_lo, TT * hf + TILES)
                first(hf, 0, 0, tuple((1 + 4 * i, TILES + i) for i in range(TILES)))
                pe.wait_ge(x_lo, TT * (hf + 1))

            def step(hf, i, q):
                first(hf, chunk_of(i, q + 1), (q + 1) % (2 * TB))
                second(hf, i, q)

            def closing(hf):
                step(hf, LAST, TB)
                second(hf, LAST, TB + 1, hf + 1 if hf + 1 < PASSES else None)
            per_pass(pe, opening, step, closing)


def shape_constants(tokens):
    import numpy as np
    f32 = np.float32
    inv_freq = (f32(1.0) / f32(10000.0) ** (np.arange(0, HEAD, 2, dtype=f32) / f32(HEAD))).astype(f32)
    angles = (np.arange(tokens, dtype=f32)[None, :] * inv_freq[:, None]).astype(f32)
    cos, sin = np.cos(angles), np.sin(angles)
    lane = np.arange(P)
    rows = GROUP // 2
    head, row = lane // rows, lane % rows
    tiles = tokens // P
    earlier = head[:, None] < head[None, :]
    same = head[:, None] == head[None, :]
    return {
        "rope_cos": np.concatenate([cos] * 4),
        "rope_sin": np.concatenate([-sin, sin] * 2),
        "bias_signs": np.stack([np.concatenate([[0], np.full(P, -1)]), np.concatenate([[1], np.ones(P)])]).astype(f32),
        "identity": np.eye(P, dtype=f32),
        "same_head": np.kron(np.eye(P // HEAD), np.ones((HEAD, HEAD))).astype(f32),
        "phase": np.tile(np.repeat(np.array([0.0, 0.25], f32), HEAD // 2), P // HEAD)[:, None],
        "own_token": np.kron(np.eye(GROUP), np.ones((KV_HEADS, 1))).astype(f32),
        "order_masks": np.stack([earlier, same, same & (row[:, None] < row[None, :]), np.ones((P, P), bool)], 1).astype(f32),
        "token_ids": (head[:, None] * (tokens // HEADS) + np.arange(tiles)[None, :] * rows + row[:, None]).astype(f32),
        "count_up": np.tile(np.arange(P, dtype=f32), (P, 1)),
    }


def feature_weights(R):
    import numpy as np
    e = R.shape[0]
    w = np.zeros((P, 3, P), R.dtype)
    for j in range(2):
        rows = slice(HEAD * j, HEAD * (j + 1))
        for c in range(2):
            w[rows, 0, HEAD * j + e * c:HEAD * j + e * (c + 1)] = R.T
            for half in range(2):
                at = HEAD * half + e * c
                w[rows, 1 + j, at:at + e] = R.T
    return w


def build(nc, a, out):
    tokens, width = a["x"].shape
    qk_tiles = (HEADS + KV_HEADS) // 2
    keep = tokens // 2
    qk_scratch = nc.dram_tensor("qk_scratch", (tokens // TOK_BLOCK, qk_tiles, P, TOK_BLOCK), F32, kind="Internal").ap()
    v_scratch = nc.dram_tensor("v_scratch", (tokens, KV_HEADS * HEAD), F32, kind="Internal").ap()
    score_scratch = nc.dram_tensor("score_scratch", (P, tokens // P), F32, kind="Internal").ap()
    scale_scratch = nc.dram_tensor("scale_scratch", (tokens, 2), F32, kind="Internal").ap()
    project_phase(nc, a["x"], a["w_qkv_t"], a["b_qk"], a["identity"], a["same_head"], qk_scratch, v_scratch)
    mix_phase(nc, a["x"], qk_scratch, v_scratch, a["rope_cos"], a["rope_sin"], a["features"], a["phase"], a["v_bias"],
              a["own_token"], a["w_o_t"], a["o_bias"], a["bias_signs"], a["router"], a["router_bias"], out, score_scratch,
              scale_scratch)
    with nc.sbuf_tensor("chosen", [P, keep // P], I32) as chosen, nc.sbuf_tensor("chosen_at", [P, keep // P], I32) as chosen_at:
        route_phase(nc, score_scratch, a["order_masks"], a["token_ids"], a["count_up"], chosen, chosen_at, keep)
        ffn_phase(nc, out, scale_scratch, a["w1"], a["b1"], a["w2"], a["b2_rows"], a["identity"], chosen, chosen_at, out, keep)


def kernel(**inputs):
    import numpy as np
    import concourse.bacc as bacc
    from concourse.bass_utils import run_bass_kernel_spmd

    g = {k: np.asarray(v) for k, v in inputs.items()}
    x = g["L0_attn_hidden_states"]
    arrays = {
        "x": x[0],
        "w_qkv_t": np.concatenate([g["L0_attn_Wq"], g["L0_attn_Wk"], g["L0_attn_Wv"]]).T,
        "b_qk": np.concatenate([g["L0_attn_bq"], g["L0_attn_bk"]]).reshape(-1, P).T,
        "v_bias": np.tile(g["L0_attn_bv"].reshape(KV_HEADS, HEAD), (GROUP, 1)),
        "features": feature_weights(g["L0_attn_rand_matrix"]),
        "w_o_t": g["L0_attn_Wo"].T,
        "o_bias": np.tile(g["L0_attn_bo"], (2, 1)),
        "router": np.tile(g["L0_ffn_w_r"], (P, 1)),
        "router_bias": np.tile(g["L0_ffn_b_r"].reshape(1, 1), (P, 1)),
        "w1": g["L0_ffn_w1"],
        "b1": g["L0_ffn_b1"].reshape(-1, P).T,
        "w2": g["L0_ffn_w2"],
        "b2_rows": np.tile(g["L0_ffn_b2"], (P, 1)),
    }
    arrays.update(shape_constants(x.shape[1]))
    arrays = {k: np.ascontiguousarray(v) for k, v in arrays.items()}

    nc = bacc.Bacc("TRN2", target_bir_lowering=False, num_devices=1)
    tensors = {k: nc.dram_tensor(f"in_{k}", v.shape, mybir.dt.from_np(v.dtype), kind="ExternalInput").ap() for k, v in arrays.items()}
    out = nc.dram_tensor("out_x", x.shape[1:], F32, kind="ExternalOutput").ap()
    build(nc, tensors, out)
    r = run_bass_kernel_spmd(nc, [{f"in_{k}": v for k, v in arrays.items()}], core_ids=[0])
    return r.results[0]["out_x"].reshape(x.shape)
```
